# Optimizing a Trainium2 kernel written in Bass

```python
import numpy as np
import jax
import jax.numpy as jnp

def _softmax(x, axis=-1):
    return jax.nn.softmax(x, axis=axis)

def _gelu(x):
    return jax.nn.gelu(x, approximate=True)

def _silu(x):
    return jax.nn.silu(x)

def _sigmoid(x):
    return jax.nn.sigmoid(x)

def _layernorm(x, axis=-1, eps=1e-05):
    m = jnp.mean(x, axis=axis, keepdims=True)
    v = jnp.var(x, axis=axis, keepdims=True)
    return (x - m) / jnp.sqrt(v + eps)

def _scatter_add(tgt, idx, src, axis=0):
    return tgt.at[idx].add(src)

def _segment_sum(src, seg, n):
    return jax.ops.segment_sum(src, seg, n)
kernel_name = 'mk_seq_postln_d2_jaxref_r8_462d90'

def setup_inputs(seed: int=0):
    np.random.seed(seed)
    _w = jnp.asarray

    def _L0_attn_setup():
        import math
        import jax, jax.numpy as jnp
        import numpy as np
        HEADS = 16
        DIM_HEAD = 64
        NUM_NULL_KV = 2
        ATTN_SCALE = 8.0
        LN_EPS = 1e-05

        def _alibi_slopes(heads):
            start = 2.0 ** (-2.0 ** (-(math.log2(heads) - 3.0)))
            return np.array([start * start ** i for i in range(heads)], dtype=np.float32)

        def _l2norm(t):
            return t / jnp.maximum(jnp.linalg.norm(t, axis=-1, keepdims=True), 1e-12)
        key = jax.random.key(seed)
        ks = jax.random.split(key, 5)
        b, n, dim = (4, 256, 128)
        return {'x': jax.random.normal(ks[0], (b, n, dim), dtype=jnp.float32), 'gamma': jnp.ones((dim,), dtype=jnp.float32), 'w_q': jax.random.normal(ks[1], (dim, HEADS * DIM_HEAD), dtype=jnp.float32) * 0.02, 'w_kv': jax.random.normal(ks[2], (dim, 2 * HEADS * DIM_HEAD), dtype=jnp.float32) * 0.02, 'null_kv': jax.random.normal(ks[3], (HEADS, 2 * NUM_NULL_KV, DIM_HEAD), dtype=jnp.float32), 'q_scale': jnp.ones((DIM_HEAD,), dtype=jnp.float32), 'k_scale': jnp.ones((DIM_HEAD,), dtype=jnp.float32), 'w_out': jax.random.normal(ks[4], (HEADS * DIM_HEAD, dim), dtype=jnp.float32) * 0.02}
    _L0_attn_in = _L0_attn_setup()

    def _L0_ffn_setup():
        import jax, jax.numpy as jnp
        import numpy as np
        S, B, H, I, E = (64, 2, 128, 352, 8)
        key = jax.random.key(seed)
        ks = jax.random.split(key, 5)
        return {'hidden_states': jax.random.normal(ks[0], (S, B, H), dtype=jnp.float32), 'router_w': jax.random.normal(ks[1], (E, H), dtype=jnp.float32) * 0.02, 'gate_w': jax.random.normal(ks[2], (E, I, H), dtype=jnp.float32) * 0.02, 'up_w': jax.random.normal(ks[3], (E, I, H), dtype=jnp.float32) * 0.02, 'down_w': jax.random.normal(ks[4], (E, H, I), dtype=jnp.float32) * 0.02}
    _L0_ffn_in = _L0_ffn_setup()

    def _L1_attn_setup():
        import jax, jax.numpy as jnp
        import numpy as np
        import math
        EMBED_DIM = 128
        NUM_HEADS = 16
        HEAD_DIM = EMBED_DIM // NUM_HEADS
        T, N = (128, 8)
        key = jax.random.key(seed)
        k1, k2, k3, k4 = jax.random.split(key, 4)
        scale = 0.02
        x = jax.random.normal(k1, (T, N, EMBED_DIM), dtype=jnp.float32)
        q_weight = jax.random.normal(k2, (EMBED_DIM, NUM_HEADS, HEAD_DIM), dtype=jnp.float32) * scale
        v_weight = jax.random.normal(k3, (EMBED_DIM, NUM_HEADS, HEAD_DIM), dtype=jnp.float32) * scale
        out_w = jax.random.normal(k4, (EMBED_DIM, EMBED_DIM), dtype=jnp.float32) * scale
        out_b = jnp.zeros((EMBED_DIM,), dtype=jnp.float32)
        return {'x': x, 'q_weight': q_weight, 'v_weight': v_weight, 'out_w': out_w, 'out_b': out_b}
    _L1_attn_in = _L1_attn_setup()

    def _L1_ffn_setup():
        import jax, jax.numpy as jnp
        import numpy as np
        B, S, D = (2, 256, 128)
        I = 64
        E = 16
        TOP_K = 2

        def _mlp(x, wg, wu, wd):
            return jnp.einsum('bsi,id->bsd', jax.nn.silu(x @ wg) * (x @ wu), wd)
        key = jax.random.key(seed)
        ks = jax.random.split(key, 10)
        sc_d = 1.0 / np.sqrt(D)
        sc_i = 1.0 / np.sqrt(I)
        return {'x': jax.random.normal(ks[0], (B, S, D), dtype=jnp.float32), 'gate_w': jax.random.normal(ks[1], (D, E), dtype=jnp.float32) * sc_d, 'gate_b': jnp.zeros((E,), dtype=jnp.float32), 'shared_wg': jax.random.normal(ks[2], (D, I), dtype=jnp.float32) * sc_d, 'shared_wu': jax.random.normal(ks[3], (D, I), dtype=jnp.float32) * sc_d, 'shared_wd': jax.random.normal(ks[4], (I, D), dtype=jnp.float32) * sc_i, 'experts_wg': jax.random.normal(ks[5], (E, D, I), dtype=jnp.float32) * sc_d, 'experts_wu': jax.random.normal(ks[6], (E, D, I), dtype=jnp.float32) * sc_d, 'experts_wd': jax.random.normal(ks[7], (E, I, D), dtype=jnp.float32) * sc_i}
    _L1_ffn_in = _L1_ffn_setup()
    _d = {'L0_attn_x': _L0_attn_in['x'], 'L0_attn_gamma': _L0_attn_in['gamma'], 'L0_attn_w_q': _L0_attn_in['w_q'], 'L0_attn_w_kv': _L0_attn_in['w_kv'], 'L0_attn_null_kv': _L0_attn_in['null_kv'], 'L0_attn_q_scale': _L0_attn_in['q_scale'], 'L0_attn_k_scale': _L0_attn_in['k_scale'], 'L0_attn_w_out': _L0_attn_in['w_out'], 'L0_ffn_router_w': _L0_ffn_in['router_w'], 'L0_ffn_gate_w': _L0_ffn_in['gate_w'], 'L0_ffn_up_w': _L0_ffn_in['up_w'], 'L0_ffn_down_w': _L0_ffn_in['down_w'], 'L1_attn_q_weight': _L1_attn_in['q_weight'], 'L1_attn_v_weight': _L1_attn_in['v_weight'], 'L1_attn_out_w': _L1_attn_in['out_w'], 'L1_attn_out_b': _L1_attn_in['out_b'], 'L1_ffn_gate_w': _L1_ffn_in['gate_w'], 'L1_ffn_gate_b': _L1_ffn_in['gate_b'], 'L1_ffn_shared_wg': _L1_ffn_in['shared_wg'], 'L1_ffn_shared_wu': _L1_ffn_in['shared_wu'], 'L1_ffn_shared_wd': _L1_ffn_in['shared_wd'], 'L1_ffn_experts_wg': _L1_ffn_in['experts_wg'], 'L1_ffn_experts_wu': _L1_ffn_in['experts_wu'], 'L1_ffn_experts_wd': _L1_ffn_in['experts_wd']}
    _x0 = _d['L0_attn_x']
    _d['L0_attn_x'] = jax.random.normal(jax.random.fold_in(jax.random.key(seed), 1), (4, 1024, 128), dtype=_x0.dtype)
    del _x0
    return _d

def reference(L0_attn_x, L0_attn_gamma, L0_attn_w_q, L0_attn_w_kv, L0_attn_null_kv, L0_attn_q_scale, L0_attn_k_scale, L0_attn_w_out, L0_ffn_router_w, L0_ffn_gate_w, L0_ffn_up_w, L0_ffn_down_w, L1_attn_q_weight, L1_attn_v_weight, L1_attn_out_w, L1_attn_out_b, L1_ffn_gate_w, L1_ffn_gate_b, L1_ffn_shared_wg, L1_ffn_shared_wu, L1_ffn_shared_wd, L1_ffn_experts_wg, L1_ffn_experts_wu, L1_ffn_experts_wd):

    def _L0_attn_ref(x, gamma, w_q, w_kv, null_kv, q_scale, k_scale, w_out):
        import math
        import jax, jax.numpy as jnp
        import numpy as np
        HEADS = 16
        DIM_HEAD = 64
        NUM_NULL_KV = 2
        ATTN_SCALE = 8.0
        LN_EPS = 1e-05

        def _alibi_slopes(heads):
            start = 2.0 ** (-2.0 ** (-(math.log2(heads) - 3.0)))
            return np.array([start * start ** i for i in range(heads)], dtype=np.float32)

        def _l2norm(t):
            return t / jnp.maximum(jnp.linalg.norm(t, axis=-1, keepdims=True), 1e-12)
        b, n, dim = x.shape
        mu = jnp.mean(x, axis=-1, keepdims=True)
        var = jnp.mean(jnp.square(x - mu), axis=-1, keepdims=True)
        xn = (x - mu) * jax.lax.rsqrt(var + LN_EPS) * gamma
        q = (xn @ w_q).reshape(b, n, HEADS, DIM_HEAD).transpose(0, 2, 1, 3)
        kv = xn @ w_kv
        k, v = jnp.split(kv, 2, axis=-1)
        k = k.reshape(b, n, HEADS, DIM_HEAD).transpose(0, 2, 1, 3)
        v = v.reshape(b, n, HEADS, DIM_HEAD).transpose(0, 2, 1, 3)
        nkv = null_kv.reshape(HEADS, NUM_NULL_KV, 2, DIM_HEAD)
        nk = jnp.broadcast_to(nkv[:, :, 0][None], (b, HEADS, NUM_NULL_KV, DIM_HEAD))
        nv = jnp.broadcast_to(nkv[:, :, 1][None], (b, HEADS, NUM_NULL_KV, DIM_HEAD))
        k = jnp.concatenate([nk, k], axis=2)
        v = jnp.concatenate([nv, v], axis=2)
        q = _l2norm(q) * q_scale
        k = _l2norm(k) * k_scale
        sim = jnp.einsum('bhid,bhjd->bhij', q, k) * ATTN_SCALE
        j = n + NUM_NULL_KV
        rows = jnp.arange(n)
        cols = jnp.arange(j)
        dist = -jnp.abs(cols[None, :] - (rows[:, None] + NUM_NULL_KV)).astype(sim.dtype)
        slopes = jnp.asarray(_alibi_slopes(HEADS))
        sim = sim + dist[None, None] * slopes[None, :, None, None]
        causal_mask = cols[None, :] > rows[:, None] + NUM_NULL_KV
        neg = -jnp.finfo(sim.dtype).max
        sim = jnp.where(causal_mask[None, None], neg, sim)
        attn = jax.nn.softmax(sim, axis=-1)
        out = jnp.einsum('bhij,bhjd->bhid', attn, v)
        out = out.transpose(0, 2, 1, 3).reshape(b, n, HEADS * DIM_HEAD)
        return out @ w_out

    def _L0_ffn_ref(hidden_states, router_w, gate_w, up_w, down_w):
        import jax, jax.numpy as jnp
        import numpy as np
        S, B, H, I, E = (64, 2, 128, 352, 8)
        router_logits = jnp.einsum('sbh,eh->sbe', hidden_states, router_w)
        routing_indices = jnp.argmax(router_logits, axis=-1)
        out = jnp.zeros_like(hidden_states)
        for e in range(E):
            mask = (routing_indices == e)[..., None]
            xe = jnp.where(mask, hidden_states, 0.0)
            g = jnp.einsum('sbh,ih->sbi', xe, gate_w[e])
            u = jnp.einsum('sbh,ih->sbi', xe, up_w[e])
            ye = jnp.einsum('sbi,hi->sbh', jax.nn.silu(g) * u, down_w[e])
            out = out + jnp.where(mask, ye, 0.0)
        return out

    def _L1_attn_ref(x, q_weight, v_weight, out_w, out_b):
        import jax, jax.numpy as jnp
        import numpy as np
        import math
        EMBED_DIM = 128
        NUM_HEADS = 16
        HEAD_DIM = EMBED_DIM // NUM_HEADS
        T, N = (128, 8)
        head_dim = q_weight.shape[-1]
        inv_sqrt_d = 1.0 / math.sqrt(head_dim)
        q = jnp.einsum('tbm,mhd->tbhd', x, q_weight)
        k = q
        q_sq = jnp.einsum('tbhd,tbhd->tbh', q, q)
        k_sq = jnp.einsum('sbhd,sbhd->sbh', k, k)
        qk = jnp.einsum('tbhd,sbhd->tsbh', q, k)
        squared_dist = q_sq[:, None] + k_sq[None, :] - 2.0 * qk
        attn_logits = -squared_dist * inv_sqrt_d
        attn_weights = jax.nn.softmax(attn_logits, axis=1)
        A = jnp.einsum('mhd,nhd->hmn', q_weight, q_weight) * inv_sqrt_d
        XA = jnp.einsum('tbm,hmn->tbhn', x, A)
        PXA = jnp.einsum('tsbh,sbhm->tbhm', attn_weights, XA)
        Tn, Bn = (x.shape[0], x.shape[1])
        PXAV = jnp.einsum('tbhm,mhd->tbhd', PXA, v_weight).reshape(Tn, Bn, -1)
        return PXAV @ out_w.T + out_b

    def _L1_ffn_ref(x, gate_w, gate_b, shared_wg, shared_wu, shared_wd, experts_wg, experts_wu, experts_wd):
        import jax, jax.numpy as jnp
        import numpy as np
        B, S, D = (2, 256, 128)
        I = 64
        E = 16
        TOP_K = 2

        def _mlp(x, wg, wu, wd):
            return jnp.einsum('bsi,id->bsd', jax.nn.silu(x @ wg) * (x @ wu), wd)
        router_logits = jax.nn.sigmoid(x @ gate_w + gate_b)
        expert_values, expert_indices = jax.lax.top_k(router_logits, k=TOP_K)
        expert_values = expert_values / jnp.sum(expert_values, axis=-1, keepdims=True)
        hg = jnp.einsum('bsd,edi->bsei', x, experts_wg)
        hu = jnp.einsum('bsd,edi->bsei', x, experts_wu)
        all_outputs = jnp.einsum('bsei,eid->bsed', jax.nn.silu(hg) * hu, experts_wd)
        selected = jnp.take_along_axis(all_outputs, expert_indices[..., None], axis=2)
        expert_weighted = jnp.sum(expert_values[..., None] * selected, axis=2)
        return x + _mlp(x, shared_wg, shared_wu, shared_wd) + expert_weighted
    x = L0_attn_x
    x = _layernorm(x + _L0_attn_ref(x, L0_attn_gamma, L0_attn_w_q, L0_attn_w_kv, L0_attn_null_kv, L0_attn_q_scale, L0_attn_k_scale, L0_attn_w_out), axis=-1)
    x = _layernorm(x + _L0_ffn_ref(x, L0_ffn_router_w, L0_ffn_gate_w, L0_ffn_up_w, L0_ffn_down_w), axis=-1)
    x = _layernorm(x + _L1_attn_ref(x, L1_attn_q_weight, L1_attn_v_weight, L1_attn_out_w, L1_attn_out_b), axis=-1)
    x = _layernorm(x + _L1_ffn_ref(x, L1_ffn_gate_w, L1_ffn_gate_b, L1_ffn_shared_wg, L1_ffn_shared_wu, L1_ffn_shared_wd, L1_ffn_experts_wg, L1_ffn_experts_wu, L1_ffn_experts_wd), axis=-1)
    return x

_drawn_inputs = setup_inputs


def setup_inputs(seed=0):
    import zlib

    import numpy as np

    out = dict(_drawn_inputs(seed))
    spreads = {'L0_attn_gamma': (1.0, 0.2),
     'L0_attn_q_scale': (1.0, 0.6),
     'L0_attn_k_scale': (1.0, 0.6),
     'L1_attn_out_b': (0.0, 0.1),
     'L1_ffn_gate_b': (0.0, 0.1)}
    factors = {'L1_attn_q_weight': 8.0, 'L1_attn_v_weight': 8.0, 'L1_attn_out_w': 8.0}
    for name, (base, spread) in spreads.items():
        noise = np.random.default_rng([zlib.crc32(name.encode()), seed]).standard_normal(out[name].shape)
        drawn = base * np.exp(spread * noise) if base else spread * noise
        out[name] = jnp.asarray(drawn.astype(out[name].dtype))
    for name, factor in factors.items():
        out[name] = (out[name] * factor).astype(out[name].dtype)
    return out
```

```python
from contextlib import ExitStack

import numpy as np

import concourse.bass as bass
from concourse import mybir

F32 = mybir.dt.float32
BF16 = mybir.dt.bfloat16
ALU = mybir.AluOpType
ACT = mybir.ActivationFunctionType
AX = mybir.AxisListType

P = 128
NB, SEQ, D = 4, 1024, 128
TT = SEQ // P
H, DH = 16, 64
NNULL = 2
HG = 4
NG = H // HG
TURNS = NB * NG
VW = DH + 1
QW = DH + 1
KW = HG * DH
CEN = SEQ // 2
LIFT = 40.0
EPS = 1e-5
CREDIT = 1
E0, I0 = 8, 352
E1, I1 = 16, 64
H1, DH1 = 16, 8
CH = NB * P
KB0 = [(k, min(P, I0 - k)) for k in range(0, I0, P)]
NK0 = len(KB0)
NJ1 = E1 // 2 + 1
NE1 = E1 + 1
PAIRS = [(t, s) for t in range(NB) for s in range(t + 1, NB)]
OFF = [sum(SEQ - P * i for i in range(j)) for j in range(TT + 1)]
TAB = HG * TT + TT * HG + HG * NNULL


def slopes():
    start = 2.0 ** (-2.0 ** (-(np.log2(H) - 3.0)))
    return np.array([start * start ** i for i in range(H)], dtype=np.float32).astype(np.float64)


def constants():
    sl = slopes()
    p = np.arange(P)[:, None, None]
    jt = np.arange(TT)
    key = sl[None, :, None] * (P * jt[None, None, :] + p - CEN)
    qry = LIFT - sl[None, None, :] * (P * jt[None, :, None] + p - CEN)
    nul = np.broadcast_to(sl[:, None] * (np.arange(NNULL)[None] - NNULL - CEN), (P, H, NNULL))
    tab = np.zeros((P, NG, TAB), np.float32)
    for g in range(NG):
        h = slice(g * HG, g * HG + HG)
        tab[:, g] = np.concatenate([key[:, h].reshape(P, -1), qry[:, :, h].reshape(P, -1),
                                    nul[:, h].reshape(P, -1)], axis=1)
    bits = lambda v: (np.asarray(v, np.float32).view(np.uint32) >> 16).astype(np.uint16)
    sel0 = np.zeros((E0, E0, P), np.float32)
    for e in range(E0):
        sel0[e, e] = 1
    sel1 = np.zeros((3, NE1, NJ1, P), np.float32)
    for e in range(NE1):
        sel1[:, e, e // 2, (e % 2) * I1:(e % 2) * I1 + I1] = 1
    nvone = np.zeros((HG, NNULL, NG, HG, VW), np.float32)
    for h in range(HG):
        nvone[h, :, :, h, DH] = 1
    blk = np.zeros((P, P), np.float32)
    for h in range(H1):
        blk[h * DH1:(h + 1) * DH1, h * DH1:(h + 1) * DH1] = DH1 ** -0.5
    rank = np.concatenate([np.tile(E0 - np.arange(E0), NB), np.tile(E1 - np.arange(E1), NB)])
    return {
        "c_tab": tab, "c_sel0": bits(sel0), "c_sel1": bits(sel1.reshape(3 * NE1, NJ1, P)),
        "c_nvone": nvone.reshape(HG * NNULL, NG * HG * VW), "c_blk": blk,
        "c_idf": np.eye(P, dtype=np.float32), "c_idb": bits(np.eye(P)),
        "c_future": bits(np.where(np.arange(P)[:, None] > np.arange(P)[None], -1e30, 0.0)),
        "c_rank": np.broadcast_to(rank.astype(np.float32), (P, rank.size)).copy(),
    }


def build(nc, a, out):
    ctx = ExitStack()
    with ctx:
        def sb(name, shape, dt=F32, scope=ctx):
            return scope.enter_context(nc.sbuf_tensor(name, shape, dt))

        def ps(name, shape, dt=F32, scope=ctx):
            return scope.enter_context(nc.psum_tensor(name, shape, dt))

        X = sb("X", [P, TT, NB, D])
        XT = sb("XT", [P, NB * SEQ])
        idf = sb("idf", [P, P])
        idb = sb("idb", [P, P], BF16)
        future = sb("future", [P, P], BF16)
        rank = sb("rank", [P, NB * (E0 + E1)])
        half = sb("half", [P, 2, 64])
        gw0 = sb("gw0", [P, E0 * I0])
        uw0 = sb("uw0", [P, E0 * I0])
        rw0 = sb("rw0", [P, E0])
        w1q = sb("w1q", [P, 2, D])
        ow1 = sb("ow1", [P, D])
        stat = sb("stat", [P, NB, 6])
        mv = sb("mv", [P, NB, 2])
        vareps = sb("vareps", [P, NB])
        rstd = sb("rstd", [P, NB])
        xn = sb("xn", [P, NB, D])

        def chunk(t, c):
            return t[:, bass.ds(c, 1), :, :].rearrange("p a b d -> p (a b) d")

        class Norm:

            def __init__(self, name):
                s = lambda n: ctx.enter_context(nc.semaphore(f"{name}_{n}"))
                self.stats, self.mean, self.var, self.root, self.done = (
                    s("stats"), s("mean"), s("var"), s("root"), s("done"))

            def vector(self, dve, src, dst, n):
                for b in range(NB):
                    last = nc.vector.bn_stats(stat[:, b, :], src[:, b, :])
                last.then_inc(self.stats, 1)
                dve.wait_ge(self.stats, n + 1)
                hold(dve)
                for b in range(NB):
                    last = nc.vector.bn_aggr(mv[:, b, :], stat[:, b, :])
                last.then_inc(self.mean, 1)
                dve.wait_ge(self.mean, n + 1)
                nc.vector.tensor_scalar(vareps[:], mv[:, :, 1], EPS, None, ALU.add).then_inc(self.var, 1)
                dve.wait_ge(self.root, n + 1)
                for b in range(NB):
                    last = nc.vector.tensor_scalar(dst[:, b, :], src[:, b, :], mv[:, b, 0:1],
                                                   rstd[:, b:b + 1], ALU.subtract, ALU.mult)
                last.then_inc(self.done, 1)

            def pool(self, pool, n):
                pool.wait_ge(self.var, n + 1)
                nc.gpsimd.tensor_tensor(rstd[:], vareps[:], half[:, 0, 0:NB], ALU.pow).then_inc(self.root, 1)

        norm = Norm("norm")
        n0, n1, n2, n3, n4 = (lambda c: c), (lambda c: TT + c), (lambda c: 2 * TT + 2 * c), (
            lambda c: 2 * TT + 2 * c + 1), (lambda c: 4 * TT + c)

        with ExitStack() as sc:
            def s1(name):
                return ctx.enter_context(nc.semaphore(name))

            wqkv = sb("wqkv", [P, NG, 3 * KW], F32, sc)
            wout = sb("wout", [P, H * DH // P, D], F32, sc)
            wnull = sb("wnull", [P, NG, HG * NNULL], F32, sc)
            tabs = sb("tabs", [P, NG, TAB], F32, sc)
            nvb = sb("nvb", [HG * NNULL, NG, HG * VW], F32, sc)
            scl = sb("scl", [P, DH], F32, sc)
            ksc = sb("ksc", [P, DH], F32, sc)
            w1qt = sb("w1qt", [P, D], F32, sc)
            w1v = sb("w1v", [P, D], F32, sc)
            w1m = sb("w1m", [P, D], F32, sc)
            blk = sb("blk", [P, D], F32, sc)
            nks = sb("nks", [H * NNULL, 3, DH], F32, sc)
            nkt = sb("nkt", [DH, H * NNULL], F32, sc)
            nkss = sb("nkss", [H * NNULL, 2], F32, sc)
            gam = sb("gam", [P, 1], F32, sc)
            xns = sb("xns", [P, SEQ], F32, sc)
            keyb = sb("keyb", [P, HG * TT], F32, sc)
            qterm = sb("qterm", [P, TT * HG + HG * NNULL], F32, sc)
            nvs = sb("nvs", [HG * NNULL, HG * VW], F32, sc)
            Pw = sb("Pw", [P, 2, OFF[TT]], F32, sc)
            QT = sb("QT", [QW, HG, SEQ], F32, sc)
            KT = sb("KT", [QW, HG, SEQ], F32, sc)
            V = sb("V", [P, 2, TT, HG, VW], F32, sc)
            QS = sb("QS", [P, TT, HG, QW], F32, sc)
            KS = sb("KS", [P, TT, HG, QW], F32, sc)
            sq = sb("sq", [P, 2 * KW], F32, sc)
            qn = sb("qn", [P, HG, DH], F32, sc)
            ss = sb("ss", [P, 2, 2 * HG], F32, sc)
            rn = sb("rn", [P, 2 * HG], F32, sc)
            bs = sb("bs", [P, HG], F32, sc)
            bn = sb("bn", [P, HG], F32, sc)
            nl = sb("nl", [P, TT, HG * NNULL], F32, sc)
            pn = sb("pn", [P, TT, HG * NNULL], F32, sc)
            pnt = sb("pnt", [HG * NNULL, SEQ], F32, sc)
            rl = sb("rl", [P, 2, 4], F32, sc)
            OS = sb("OS", [P, TT, KW], F32, sc)
            ots = sb("ots", [P, 2, KW], F32, sc)

            S = [ps(f"S{i}", [P, SEQ], F32, sc) for i in range(2)]
            O = [ps(f"O{i}", [P, 4, P], F32, sc) for i in range(2)]
            A = [ps(f"A{i}", [P, 512], F32, sc) for i in range(2)]

            ld_x, ld_w, ld_c, ld_nv, ld_ffn = s1("ld_x"), s1("ld_w"), s1("ld_c"), s1("ld_nv"), s1("ld_ffn")
            consts = s1("consts")
            scale2, scale_ok, null_sq, null_ss, null_cl, null_rn, null_n, null_k = (
                s1("scale2"), s1("scale_ok"), s1("null_sq"), s1("null_ss"), s1("null_cl"), s1("null_rn"),
                s1("null_n"), s1("null_k"))
            null_t, null_te, wnull_mm, wnull_ok = s1("null_t"), s1("null_te"), s1("wnull_mm"), s1("wnull_ok")
            g_mm, g_ok, m_mm, m_ok = s1("g_mm"), s1("g_ok"), s1("m_mm"), s1("m_ok")
            xnt_mm, xnt_ok = s1("xnt_mm"), s1("xnt_ok")
            xns_ok = s1("xns_ok")
            proj = s1("proj")
            sq_ok, v_ok, ss_red, ss_ok, rn_ok = s1("sq_ok"), s1("v_ok"), s1("ss_red"), s1("ss_ok"), s1("rn_ok")
            kq_ok, qp_ok, sq2_ok, bs_ok, bn_ok = s1("kq_ok"), s1("qp_ok"), s1("sq2_ok"), s1("bs_ok"), s1("bn_ok")
            e_ok, nl_add, nl_ok = s1("e_ok"), s1("nl_add"), s1("nl_ok")
            pn_ok = s1("pn_ok")
            tr, tq_ok, tk_ok = s1("tr"), s1("tq_ok"), s1("tk_ok")
            ptr, pnt_ok = s1("ptr"), s1("pnt_ok")
            tab_ok = s1("tab_ok")
            qk, exp_ok, pv = s1("qk"), s1("exp_ok"), s1("pv")
            rl_ok, on = s1("rl_ok"), s1("on")
            ctr, cot, cmm, cy = s1("ctr"), s1("cot"), s1("cmm"), s1("cy")

            block = sc.enter_context(nc.Block())

            @block.sync
            def _(sp):
                for c in range(TT):
                    sp.dma_start(X[:, c], a["x"][:, c]).then_inc(ld_x, 16)
                for dst, src in ((idf, "c_idf"), (idb, "c_idb"), (future, "c_future"), (rank, "c_rank"), (tabs, "c_tab")):
                    sp.dma_start(dst[:], a[src].bitcast(dst.dtype)).then_inc(ld_c, 16)
                sp.dma_start(gam[:], a["gamma"]).then_inc(ld_c, 16)
                sp.dma_start(nvb[:].rearrange("p g n -> p (g n)"), a["c_nvone"]).then_inc(ld_nv, 16)
                sp.dma_start(scl[:], a["q_scale"].partition_broadcast(P)).then_inc(ld_c, 16)
                sp.dma_start(ksc[:], a["k_scale"].partition_broadcast(P)).then_inc(ld_c, 16)
                sp.dma_start(nks[:, 0, :], a["null_k"]).then_inc(ld_c, 16)
                sp.dma_start(KT[0:DH, 0:2, :], a["w_q_t"]).then_inc(ld_c, 16)
                sp.dma_start(wqkv[:], a["w_qkv"]).then_inc(ld_w, 16)
                sp.wait_ge(ld_nv, 16)
                for h in range(HG):
                    sp.dma_start(nvb[h * NNULL:(h + 1) * NNULL, :, h * VW:h * VW + DH],
                                 a["null_v"][h]).then_inc(ld_nv, 16)
                sp.dma_start(wout[:], a["w_out"]).then_inc(ld_w, 16)
                for dst, src in ((w1q[:, 0, :], "w1_q"), (ow1[:], "w1_o"), (rw0[:], "rw0"),
                                 (w1qt[:], "w1_q_t"), (w1v[:], "w1_v"), (blk[:], "c_blk")):
                    sp.dma_start(dst, a[src]).then_inc(ld_w, 16)
                sp.dma_start(gw0[:], a["gw0"]).then_inc(ld_ffn, 16)
                sp.dma_start(uw0[:], a["uw0"]).then_inc(ld_ffn, 16)
                sp.wait_ge(ld_ffn, 32)

            LDC, LDW, LDNV = 16 * 10, 16 * 8, 16 * (1 + HG)

            def bcast(ap, shape):
                return ap.broadcast_to(shape)

            @block.tensor
            def _(pe):
                credit(pe, cmm, ctr, pv, xnt_mm)
                def project(n, u):
                    g = n % NG
                    pe.wait_ge(xns_ok, n + 1)
                    pe.wait_ge(sq_ok, 8 * n + u)
                    pe.wait_ge(v_ok, 8 * n + u)
                    pe.wait_ge(kq_ok, 8 * n + u)
                    x = xns[:, u * P:(u + 1) * P]
                    w = wqkv[:, bass.ds(g, 1), :].rearrange("p a n -> p (a n)")
                    wn = wnull[:, bass.ds(g, 1), :].rearrange("p a n -> p (a n)")
                    nc.tensor.matmul(A[0][:], x, w[:, 0:2 * KW], start=True, stop=True)
                    nc.tensor.matmul(A[1][:, 0:KW], x, w[:, 2 * KW:3 * KW], start=True, stop=True)
                    nc.tensor.matmul(A[1][:, KW:KW + HG * NNULL], x, wn, start=True, stop=True).then_inc(proj, 1)

                def transposes(t):
                    pe.wait_ge(e_ok, 8 * t + 8)
                    pe.wait_ge(nl_ok, 8 * t + 8)
                    pe.wait_ge(kq_ok, 8 * t + 8)
                    pe.wait_ge(v_ok, 8 * t + 8)
                    pe.wait_ge(exp_ok, CREDIT + 32 * t)
                    for u in range(TT):
                        if u >= 2:
                            pe.wait_ge(tq_ok, 8 * t + u - 1)
                            pe.wait_ge(tk_ok, 8 * t + u - 1)
                        for h in range(HG):
                            nc.tensor.transpose(S[u % 2][0:QW, h * P:(h + 1) * P], QS[:, u, h, :], idf[:])
                        for h in range(HG):
                            last = nc.tensor.transpose(S[u % 2][0:QW, 512 + h * P:512 + (h + 1) * P],
                                                       KS[:, u, h, :], idf[:])
                        last.then_inc(tr, 1)
                    pe.wait_ge(pn_ok, t + 1)
                    pe.wait_ge(cot, CREDIT + 8 * t)
                    for u in range(TT):
                        last = nc.tensor.transpose(A[u // 4][0:HG * NNULL, (u % 4) * P:(u % 4 + 1) * P],
                                                   pn[:, u, :], idf[:])
                    last.then_inc(ptr, 1)

                def scores(t, h, jt):
                    k = h * TT + jt
                    if k == 0:
                        pe.wait_ge(tq_ok, 8 * t + 8)
                        pe.wait_ge(tk_ok, 8 * t + 8)
                    if k >= 2:
                        pe.wait_ge(exp_ok, CREDIT + 32 * t + k - 1)
                    n = SEQ - P * jt
                    for c in range(0, n, 512):
                        w = min(512, n - c)
                        last = nc.tensor.matmul(S[jt % 2][:, c:c + w], KT[:, h, jt * P:(jt + 1) * P],
                                                QT[:, h, jt * P + c:jt * P + c + w], start=True, stop=c > 0)
                        if c == 0:
                            last = nc.tensor.matmul(S[jt % 2][:, 0:P], idb[:], future[:], start=False, stop=True)
                    last.then_inc(qk, 1)

                def values(t, r, h, it):
                    if h == 0 and it == 0:
                        pe.wait_ge(pnt_ok, 2 * t + 2)
                        pe.wait_ge(tab_ok, t + 1)
                        pe.wait_ge(v_ok, 8 * t + 8)
                    if it % 4 == 0:
                        if h:
                            pe.wait_ge(on, 8 * t + 2 * (h - 1) + it // 4 + 1)
                        else:
                            pe.wait_ge(cy, CREDIT + 2 * t)
                    pe.wait_ge(exp_ok, CREDIT + 32 * t + h * TT + it + 1)
                    o = O[it // 4][:, it % 4, 0:VW]
                    nc.tensor.matmul(o, pnt[:, it * P:(it + 1) * P], nvs[:, h * VW:(h + 1) * VW],
                                     start=True, stop=False)
                    for jt in range(it + 1):
                        at = OFF[jt] + (it - jt) * P
                        last = nc.tensor.matmul(o, Pw[:, h % 2, at:at + P], V[:, r, jt, h, :],
                                                start=False, stop=jt == it)
                    last.then_inc(pv, 1)

                def project_out(t):
                    g = t % NG
                    pe.wait_ge(sq_ok, 8 * t + 16)
                    pe.wait_ge(v_ok, 8 * t + 16)
                    pe.wait_ge(kq_ok, 8 * t + 16)
                    w = wout[:, bass.ds(g * 2, 2), :]
                    for it in range(TT + 1):
                        if it < TT:
                            pe.wait_ge(on, 8 * t + 7 + it // 4)
                            if it >= 2:
                                pe.wait_ge(cot, CREDIT + 8 * t + it - 1)
                            for k in range(2):
                                last = nc.tensor.transpose(A[it % 2][:, k * P:(k + 1) * P],
                                                           OS[:, it, k * P:(k + 1) * P], idf[:])
                            last.then_inc(ctr, 1)
                        if it:
                            j = it - 1
                            if j % 4 == 0:
                                pe.wait_ge(on, 8 * t + 7 + j // 4)
                            pe.wait_ge(cot, CREDIT + 8 * t + j + 1)
                            for k in range(2):
                                last = nc.tensor.matmul(O[j // 4][:, j % 4, :], ots[:, j % 2, k * P:(k + 1) * P],
                                                        w[:, k, :], start=k == 0, stop=k == 1)
                            last.then_inc(cmm, 1)

                pe.wait_ge(ld_c, LDC)
                pe.wait_ge(ld_w, LDW)
                pe.wait_ge(null_k, 1)
                nc.tensor.transpose(A[0][0:DH, 0:H * NNULL], nks[:, 2, :], idf[0:H * NNULL, 0:H * NNULL]).then_inc(null_t, 1)
                pe.wait_ge(null_te, 1)
                for h in range(H):
                    wt = KT[0:DH, h // TT, (h % TT) * P:(h % TT + 1) * P]
                    last = nc.tensor.matmul(A[1][:, h * NNULL:(h + 1) * NNULL], wt,
                                            nkt[:, h * NNULL:(h + 1) * NNULL], start=True, stop=True)
                last.then_inc(wnull_mm, 1)
                nc.tensor.matmul(O[0][:, 0, :], w1q[:, 0, :], w1v[:], start=True, stop=True).then_inc(g_mm, 1)
                pe.wait_ge(g_ok, 1)
                nc.tensor.matmul(O[1][:, 0, :], w1qt[:], w1m[:], start=True, stop=True).then_inc(m_mm, 1)

                with pe.Fori(0, TT) as c:
                    pe.wait_ge(norm.done, n0(c) + 1)
                    pe.wait_ge(xnt_ok, CREDIT + c)
                    for b in range(NB):
                        last = nc.tensor.transpose(S[0][:, b * P:(b + 1) * P], xn[:, b, :], idf[:])
                    last.then_inc(xnt_mm, 1)

                pe.wait_ge(wnull_ok, 1)
                pe.wait_ge(xnt_ok, CREDIT + TT)
                for u in range(TT):
                    project(0, u)
                with pe.Fori(0, TURNS // 2) as i:
                    for r in range(2):
                        t = 2 * i + r
                        transposes(t)
                        for slot in range((HG + 1) * TT):
                            h, s = slot // TT, slot % TT
                            if h < HG:
                                scores(t, h, s)
                            if h:
                                values(t, r, h - 1, s)
                            if slot % 4 == 3 and slot < 4 * TT:
                                if slot == 3:
                                    pe.wait_ge(pnt_ok, 2 * t + 2)
                                project(t + 1, slot // 4)
                        project_out(t)

            @block.scalar
            def _(act):
                credit(act, cot, exp_ok, xnt_ok)
                def squares(n, r, u):
                    act.wait_ge(proj, 8 * n + u + 1)
                    act.wait_ge(bs_ok, 8 * n + u)
                    nc.scalar.activation(sq[:], A[0][:], ACT.Square).then_inc(sq_ok, 1)
                    if u == 0 and not isinstance(n, int):
                        act.wait_ge(pv, CREDIT + 32 * (n - 1))
                    nc.scalar.copy(V[:, r, u, :, 0:DH],
                                   A[1][:, 0:KW].rearrange("p (h d) -> p h d", h=HG)).then_inc(v_ok, 1)

                def squares2(n, u):
                    act.wait_ge(qp_ok, 8 * n + u + 1)
                    act.wait_ge(ss_red, 8 * n + u + 1)
                    nc.scalar.activation(sq[:, 0:KW].rearrange("p (h d) -> p h d", h=HG), QS[:, u, :, 0:DH],
                                         ACT.Square).then_inc(sq2_ok, 1)

                def null_exp(n):
                    act.wait_ge(nl_ok, 8 * n + 8)
                    act.wait_ge(ptr, n)
                    nc.scalar.activation(pn[:], nl[:], ACT.Exp).then_inc(pn_ok, 1)

                act.wait_ge(ld_c, LDC)
                act.wait_ge(null_t, 1)
                nc.scalar.copy(nkt[:], A[0][0:DH, 0:H * NNULL]).then_inc(null_te, 1)
                act.wait_ge(wnull_mm, 1)
                nc.scalar.copy(wnull[:].rearrange("p g n -> p (g n)"), A[1][:, 0:H * NNULL]).then_inc(wnull_ok, 1)
                with act.Fori(0, TT) as c:
                    act.wait_ge(xnt_mm, CREDIT + c + 1)
                    dst = XT[:].rearrange("p (b c n) -> p b c n", b=NB, c=TT)[:, :, bass.ds(c, 1), :]
                    nc.scalar.activation(dst.rearrange("p b a n -> p (b a) n"),
                                         S[0][:, 0:CH].rearrange("p (b n) -> p b n", b=NB), ACT.Copy,
                                         scale=gam[:, 0:1]).then_inc(xnt_ok, 1)
                for u in range(TT):
                    squares(0, 0, u)
                    squares2(0, u)
                null_exp(0)
                with act.Fori(0, TURNS // 2) as i:
                    for r in range(2):
                        t = 2 * i + r
                        for u in range(TT):
                            act.wait_ge(tr, 8 * t + u + 1)
                            nc.scalar.copy(QT[:, :, u * P:(u + 1) * P],
                                           S[u % 2][0:QW, 0:512].rearrange("p (h n) -> p h n", h=HG)).then_inc(tq_ok, 1)
                        for slot in range((HG + 1) * TT):
                            h, jt = slot // TT, slot % TT
                            if h < HG:
                                if h == 0 and jt == 0:
                                    act.wait_ge(tab_ok, t + 1)
                                    act.wait_ge(pv, CREDIT + 32 * t)
                                if h >= 2 and jt == 0:
                                    act.wait_ge(pv, CREDIT + 32 * t + (h - 1) * TT)
                                act.wait_ge(qk, 32 * t + h * TT + jt + 1)
                                n = SEQ - P * jt
                                nc.scalar.activation(Pw[:, h % 2, OFF[jt]:OFF[jt] + n], S[jt % 2][:, 0:n], ACT.Exp,
                                                     bias=keyb[:, h * TT + jt:h * TT + jt + 1]).then_inc(exp_ok, 1)
                            u = slot // 4 - 1
                            if slot % 4 == 0 and 0 <= u < TT:
                                squares(t + 1, 1 - r, u)
                            if slot % 4 == 3 and 0 <= u < TT:
                                squares2(t + 1, u)
                        null_exp(t + 1)
                        for it in range(TT):
                            act.wait_ge(ctr, CREDIT + 8 * t + it + 1)
                            act.wait_ge(cmm, CREDIT + 8 * t + max(it - 1, 0))
                            nc.scalar.copy(ots[:, it % 2, :], A[it % 2][:, 0:KW]).then_inc(cot, 1)

            @block.vector
            def _(dve):
                credit(dve, cy)
                def sums(n, u):
                    dve.wait_ge(sq_ok, 8 * n + u + 1)
                    nc.vector.tensor_reduce(ss[:, 0, :], sq[:].rearrange("p (h d) -> p h d", d=DH), AX.X,
                                            ALU.add).then_inc(ss_red, 1)
                    dve.wait_ge(ss_red, 8 * n + u + 1)
                    nc.vector.tensor_scalar(ss[:, 1, :], ss[:, 0, :], 1e-24, None, ALU.max).then_inc(ss_ok, 1)

                def directions(n, u):
                    dve.wait_ge(rn_ok, 8 * n + u + 1)
                    dve.wait_ge(qp_ok, 8 * n + u)
                    dve.wait_ge(proj, 8 * n + u + 1)
                    dve.wait_ge(v_ok, 8 * n + u + 1)
                    dve.wait_ge(tr, 8 * n)
                    dve.wait_ge(pn_ok, n)
                    nc.vector.tensor_tensor(KS[:, u, :, 0:DH], A[0][:, KW:2 * KW].rearrange("p (h d) -> p h d", h=HG),
                                            bcast(rn[:, HG:2 * HG].unsqueeze(2), [P, HG, DH]), ALU.mult)
                    nc.vector.tensor_tensor(nl[:, u, :].rearrange("p (h k) -> p h k", k=NNULL),
                                            A[1][:, KW:KW + HG * NNULL].rearrange("p (h k) -> p h k", k=NNULL),
                                            bcast(rn[:, 0:HG].unsqueeze(2), [P, HG, NNULL]), ALU.mult)
                    nc.vector.tensor_tensor(qn[:], A[0][:, 0:KW].rearrange("p (h d) -> p h d", h=HG),
                                            bcast(rn[:, 0:HG].unsqueeze(2), [P, HG, DH]), ALU.mult).then_inc(kq_ok, 1)

                def bound(n, u):
                    dve.wait_ge(sq2_ok, 8 * n + u + 1)
                    dve.wait_ge(bn_ok, 8 * n + u)
                    nc.vector.tensor_reduce(bs[:], sq[:, 0:KW].rearrange("p (h d) -> p h d", d=DH), AX.X,
                                            ALU.add).then_inc(bs_ok, 1)

                def guard(n, u):
                    dve.wait_ge(bn_ok, 8 * n + u + 1)
                    dve.wait_ge(kq_ok, 8 * n + u + 1)
                    e = QS[:, u, :, DH]
                    nc.vector.tensor_tensor(e, qterm[:, u * HG:(u + 1) * HG], bn[:], ALU.subtract).then_inc(e_ok, 1)
                    dve.wait_ge(e_ok, 8 * n + u + 1)
                    x = nl[:, u, :].rearrange("p (h k) -> p h k", k=NNULL)
                    nc.vector.tensor_tensor(x, x, bcast(QS[:, u, :, DH:DH + 1], [P, HG, NNULL]), ALU.add).then_inc(nl_add, 1)
                    dve.wait_ge(nl_add, 8 * n + u + 1)
                    nc.vector.tensor_tensor(nl[:, u, :], nl[:, u, :], qterm[:, TT * HG:], ALU.add).then_inc(nl_ok, 1)

                def head_out(t, h, half_):
                    dve.wait_ge(pv, CREDIT + 32 * t + h * TT + half_ * 4 + 4)
                    if h == 0:
                        dve.wait_ge(ctr, CREDIT + 8 * t)
                    o = O[half_]
                    nc.vector.reciprocal(rl[:, half_, :], o[:, :, DH]).then_inc(rl_ok, 1)
                    dve.wait_ge(rl_ok, 8 * t + h * 2 + half_ + 1)
                    nc.vector.tensor_tensor(OS[:, half_ * 4:half_ * 4 + 4, h * DH:(h + 1) * DH], o[:, :, 0:DH],
                                            bcast(rl[:, half_, :].unsqueeze(2), [P, 4, DH]), ALU.mult).then_inc(on, 1)

                nc.vector.memset(half[:, 0, :], -0.5)
                nc.vector.memset(half[:, 1, :], 0.5).then_inc(consts, 1)
                for r in range(2):
                    last = nc.vector.memset(V[:, r, :, :, DH:VW], 1.0)
                last.then_inc(consts, 1)
                dve.wait_ge(ld_c, LDC)
                dve.wait_ge(ld_w, LDW)
                nc.vector.scalar_tensor_tensor(scl[:], scl[:], 8.0, ksc[:], ALU.mult, ALU.mult).then_inc(scale_ok, 1)
                nc.vector.tensor_tensor(nks[:, 1, :], nks[:, 0, :], nks[:, 0, :], ALU.mult).then_inc(null_sq, 1)
                dve.wait_ge(null_sq, 1)
                nc.vector.tensor_reduce(nkss[:, 0:1], nks[:, 1, :], AX.X, ALU.add).then_inc(null_ss, 1)
                dve.wait_ge(null_ss, 1)
                nc.vector.tensor_scalar(nkss[:, 0:1], nkss[:, 0:1], 1e-24, None, ALU.max).then_inc(null_cl, 1)
                dve.wait_ge(null_rn, 1)
                dve.wait_ge(scale_ok, 1)
                nc.vector.scalar_tensor_tensor(nks[:, 2, :], nks[:, 0, :], nkss[:, 1:2], scl[0:H * NNULL, :],
                                               ALU.mult, ALU.mult).then_inc(null_k, 1)
                dve.wait_ge(g_mm, 1)
                nc.vector.tensor_tensor(w1m[:], O[0][:, 0, :], blk[:], ALU.mult).then_inc(g_ok, 1)
                dve.wait_ge(m_mm, 1)
                nc.vector.tensor_copy(w1q[:, 1, :], O[1][:, 0, :]).then_inc(m_ok, 1)
                nc.vector.memset(KS[:, :, :, DH:QW], 1.0).then_inc(consts, 1)

                dve.wait_ge(ld_x, 16 * TT)
                dve.wait_ge(consts, 3)
                with dve.Fori(0, TT) as c:
                    dve.wait_ge(xnt_mm, CREDIT + c)
                    norm.vector(dve, chunk(X, c), xn, n0(c))
                for u in range(TT):
                    sums(0, u)
                    directions(0, u)
                    bound(0, u)
                    guard(0, u)
                with dve.Fori(0, TURNS // 2) as i:
                    for r in range(2):
                        t = 2 * i + r
                        for u in range(TT):
                            dve.wait_ge(tr, 8 * t + u + 1)
                            nc.vector.tensor_copy(KT[:, :, u * P:(u + 1) * P],
                                                  S[u % 2][0:QW, 512:].rearrange("p (h n) -> p h n", h=HG)).then_inc(tk_ok, 1)
                        dve.wait_ge(ptr, t + 1)
                        for k in range(2):
                            nc.vector.tensor_copy(pnt[:, k * 512:(k + 1) * 512],
                                                  A[k][0:HG * NNULL, :]).then_inc(pnt_ok, 1)
                        for slot in range((HG + 1) * TT):
                            h, s = slot // TT, slot % TT
                            if h and s % 4 == 3:
                                head_out(t, h - 1, s // 4)
                            u = slot // 4 - 1
                            if 0 <= u < TT:
                                [sums, directions, None, bound][slot % 4](t + 1, u) if slot % 4 != 2 else None
                                if slot % 4 == 3:
                                    guard(t + 1, u)
                        b = t // NG
                        for k in range(2):
                            dve.wait_ge(cmm, CREDIT + 8 * t + 4 * k + 4)
                            dve.wait_ge(cy, CREDIT + 2 * t)
                            x = X[:, 4 * k:4 * k + 4, bass.ds(b, 1), :].rearrange("p c a d -> p (c a) d")
                            nc.vector.tensor_tensor(x, x, O[k][:], ALU.add).then_inc(cy, 1)

            @block.gpsimd
            def _(pool):
                def load_turn(n):
                    pool.wait_ge(proj, 8 * n)
                    pool.wait_ge(nl_ok, 8 * n)
                    b, g = (n // NG) % NB, n % NG
                    nc.gpsimd.tensor_copy(qterm[:], tabs[:, bass.ds(g, 1), HG * TT:].rearrange("p a n -> p (a n)"))
                    nc.gpsimd.tensor_copy(xns[:], XT[:, bass.ds(b * SEQ, SEQ)]).then_inc(xns_ok, 1)

                def roots(n, u):
                    pool.wait_ge(ss_ok, 8 * n + u + 1)
                    pool.wait_ge(kq_ok, 8 * n + u)
                    nc.gpsimd.tensor_tensor(rn[:], ss[:, 1, :], half[:, 0, 0:2 * HG], ALU.pow).then_inc(rn_ok, 1)

                def scale_q(n, u):
                    pool.wait_ge(kq_ok, 8 * n + u + 1)
                    nc.gpsimd.tensor_tensor(QS[:, u, :, 0:DH], qn[:], bcast(scl[:].unsqueeze(1), [P, HG, DH]),
                                            ALU.mult).then_inc(qp_ok, 1)

                def bound_root(n, u):
                    pool.wait_ge(bs_ok, 8 * n + u + 1)
                    pool.wait_ge(e_ok, 8 * n + u)
                    nc.gpsimd.tensor_tensor(bn[:], bs[:], half[:, 1, 0:HG], ALU.pow).then_inc(bn_ok, 1)

                pool.wait_ge(consts, 1)
                pool.wait_ge(ld_c, LDC)
                pool.wait_ge(null_cl, 1)
                nc.gpsimd.tensor_tensor(nkss[:, 1:2], nkss[:, 0:1], half[0:H * NNULL, 0, 0:1], ALU.pow).then_inc(null_rn, 1)
                with pool.Fori(0, TT) as c:
                    norm.pool(pool, n0(c))
                pool.wait_ge(xnt_ok, CREDIT + TT)
                pool.wait_ge(wnull_mm, 1)
                pool.wait_ge(ld_nv, LDNV)
                pool.wait_ge(scale_ok, 1)
                load_turn(0)
                for u in range(TT):
                    roots(0, u)
                    scale_q(0, u)
                    bound_root(0, u)
                with pool.Fori(0, TURNS // 2) as i:
                    for r in range(2):
                        t = 2 * i + r
                        g = t % NG
                        pool.wait_ge(exp_ok, CREDIT + 32 * t)
                        pool.wait_ge(pv, CREDIT + 32 * t)
                        nc.gpsimd.tensor_copy(keyb[:], tabs[:, bass.ds(g, 1), 0:HG * TT].rearrange("p a n -> p (a n)"))
                        nc.gpsimd.tensor_copy(nvs[:], nvb[:, bass.ds(g, 1), :].rearrange("p a n -> p (a n)")).then_inc(tab_ok, 1)
                        load_turn(t + 1)
                        for slot in range((HG + 1) * TT):
                            u = slot // 4 - 1
                            if 0 <= u < TT:
                                if slot % 4 == 0:
                                    roots(t + 1, u)
                                if slot % 4 == 1:
                                    scale_q(t + 1, u)
                                if slot % 4 == 3:
                                    bound_root(t + 1, u)


        dw0 = sb("dw0", [P, E0 * NK0, D])
        gw1 = sb("gw1", [P, NE1 * I1])
        uw1 = sb("uw1", [P, NE1 * I1])
        dw1 = sb("dw1", [P, NJ1, D])
        rw1 = sb("rw1", [P, E1])
        gb1 = sb("gb1", [P, E1])
        ob1 = sb("ob1", [P, D])
        sel0 = sb("sel0", [E0, E0, P], BF16)
        sel1 = sb("sel1", [3 * NE1, NJ1, P], BF16)
        mask0 = sb("mask0", [E0, TT, CH], BF16)
        comb1 = sb("comb1", [3 * NE1, TT, CH], BF16)
        xts = sb("xts", [P, CH])
        xm = sb("xm", [P, 2, CH])
        sg = sb("sg", [P, 2, CH])
        hid = sb("hid", [P, 2, CH])
        ys = sb("ys", [P, CH])
        ld2, ld3 = (ctx.enter_context(nc.semaphore(n)) for n in ("ld2", "ld3"))
        TOK = "p (b n) -> p b n"
        chunks = XT[:].rearrange("p (c n) -> p c n", c=TT)

        def xt(c):
            return chunks[:, bass.ds(c, 1), :].rearrange("p a n -> p (a n)")

        def first_of(dve, vals, top, eq, key, mkey, hot, s, n, rk, w):
            shape = [P, NB, w]
            nc.vector.tensor_reduce(top, vals, AX.X, ALU.max).then_inc(s[0], 1)
            dve.wait_ge(s[0], n + 1)
            nc.vector.tensor_tensor(eq, vals, top.unsqueeze(2).broadcast_to(shape), ALU.is_equal).then_inc(s[1], 1)
            dve.wait_ge(s[1], n + 1)
            nc.vector.tensor_tensor(key, eq, rk, ALU.mult).then_inc(s[2], 1)
            dve.wait_ge(s[2], n + 1)
            nc.vector.tensor_reduce(mkey, key, AX.X, ALU.max).then_inc(s[3], 1)
            dve.wait_ge(s[3], n + 1)
            nc.vector.tensor_tensor(hot, key, mkey.unsqueeze(2).broadcast_to(shape), ALU.is_equal).then_inc(s[4], 1)

        with ExitStack() as sc:
            def s2(name):
                return ctx.enter_context(nc.semaphore(name))

            lg = sb("lg", [P, NB, E0], F32, sc)
            eq = sb("eq0", [P, NB, E0], F32, sc)
            key = sb("key0", [P, NB, E0], F32, sc)
            top = sb("top0", [P, 2, NB], F32, sc)
            hot = sb("hot0", [P, NB, E0], BF16, sc)
            T = ps("T2", [P, NB, P], F32, sc)
            R = ps("R2", [P, NB, E0], F32, sc)
            MT = ps("MT2", [E0, CH], BF16, sc)
            pick = [s2(f"pick{i}") for i in range(5)]
            xt_mm, xt_ok, xts_ok, r_mm, r_ok, h_mm, h_ok, xk = (
                s2("xt_mm"), s2("xt_ok"), s2("xts_ok"), s2("r_mm"), s2("r_ok"), s2("h_mm"), s2("h_ok"), s2("xk"))
            block = sc.enter_context(nc.Block())

            @block.sync
            def _(sp):
                for dst, src in ((dw0, "dw0"), (sel0, "c_sel0")):
                    sp.dma_start(dst[:], a[src].bitcast(dst.dtype)).then_inc(ld2, 16)
                for dst, src in ((gw1, "gw1"), (uw1, "uw1"), (dw1, "dw1"), (rw1, "rw1"), (sel1, "c_sel1")):
                    sp.dma_start(dst[:], a[src].bitcast(dst.dtype)).then_inc(ld3, 16)
                sp.dma_start(gb1[:], a["gb1"].partition_broadcast(P)).then_inc(ld3, 16)
                sp.dma_start(ob1[:], a["ob1"].partition_broadcast(P)).then_inc(ld3, 16)
                sp.wait_ge(ld2, 32)
                sp.wait_ge(ld3, 112)

            @block.tensor
            def _(pe):
                credit(pe, h_mm, r_mm, xt_mm)
                with pe.Fori(0, TT) as c:
                    pe.wait_ge(norm.done, n1(c) + 1)
                    pe.wait_ge(xts_ok, CREDIT + c)
                    pe.wait_ge(xt_ok, CREDIT + c)
                    for b in range(NB):
                        last = nc.tensor.transpose(T[:, b, :], xn[:, b, :], idf[:])
                    last.then_inc(xt_mm, 1)
                    pe.wait_ge(xts_ok, CREDIT + c + 1)
                    pe.wait_ge(r_ok, CREDIT + c)
                    for b in range(NB):
                        last = nc.tensor.matmul(R[:, b, :], xts[:, b * P:(b + 1) * P], rw0[:], start=True, stop=True)
                    last.then_inc(r_mm, 1)
                    pe.wait_ge(pick[4], c + 1)
                    pe.wait_ge(h_ok, CREDIT + c)
                    for b in range(NB):
                        last = nc.tensor.transpose(MT[:, b * P:(b + 1) * P], hot[:, b, :], idb[:])
                    last.then_inc(h_mm, 1)

            @block.scalar
            def _(act):
                credit(act, h_ok, xt_ok, xts_ok)
                with act.Fori(0, TT) as c:
                    act.wait_ge(xt_mm, CREDIT + c + 1)
                    act.wait_ge(r_mm, CREDIT + c)
                    nc.scalar.copy(xts[:].rearrange(TOK, b=NB), T[:]).then_inc(xts_ok, 1)
                    nc.scalar.copy(xt(c).rearrange(TOK, b=NB), T[:]).then_inc(xt_ok, 1)
                    act.wait_ge(h_mm, CREDIT + c + 1)
                    nc.scalar.copy(mask0[:, bass.ds(c, 1), :].rearrange("p a n -> p (a n)"), MT[:]).then_inc(h_ok, 1)

            @block.vector
            def _(dve):
                credit(dve, r_ok, xk)
                with dve.Fori(0, TT) as c:
                    dve.wait_ge(xt_mm, CREDIT + c)
                    dve.wait_ge(xk, CREDIT + c)
                    norm.vector(dve, chunk(X, c), xn, n1(c))
                    dve.wait_ge(norm.done, n1(c) + 1)
                    hold(dve)
                    nc.vector.tensor_copy(chunk(X, c), xn[:]).then_inc(xk, 1)
                    dve.wait_ge(r_mm, CREDIT + c + 1)
                    nc.vector.tensor_copy(lg[:], R[:]).then_inc(r_ok, 1)
                    dve.wait_ge(r_ok, CREDIT + c + 1)
                    dve.wait_ge(h_mm, CREDIT + c)
                    first_of(dve, lg[:], top[:, 0, :], eq[:], key[:], top[:, 1, :], hot[:], pick, c,
                             rank[:, 0:NB * E0].rearrange("p (b e) -> p b e", b=NB), E0)

            @block.gpsimd
            def _(pool):
                with pool.Fori(0, TT) as c:
                    norm.pool(pool, n1(c))

        with ExitStack() as sc:
            def s3(name):
                return ctx.enter_context(nc.semaphore(name))

            G = [ps(f"G3{i}", [P, CH], F32, sc) for i in range(2)]
            U = [ps(f"U3{i}", [P, CH], F32, sc) for i in range(2)]
            M = [ps(f"M3{i}", [P, CH], F32, sc) for i in range(2)]
            Y = ps("Y3", [P, CH], F32, sc)
            T = ps("T3", [P, NB, P], F32, sc)
            m_mm, xm_ok, gu, silu, hid_ok, dn, ys_ok, y_t, x_ok = (
                s3("m_mm3"), s3("xm_ok"), s3("gu3"), s3("silu3"), s3("hid_ok3"), s3("dn3"), s3("ys_ok3"),
                s3("y_t3"), s3("x_ok3"))
            NQ = E0 * NK0
            block = sc.enter_context(nc.Block())

            @block.tensor
            def _(pe):
                credit(pe, dn, gu, y_t)
                def spread(c, e):
                    if e >= 2:
                        pe.wait_ge(xm_ok, CREDIT + E0 * c + e - 1)
                    else:
                        pe.wait_ge(xm_ok, CREDIT + E0 * c)
                    hold(pe)
                    nc.tensor.matmul(M[e % 2][:], sel0[:, e, :],
                                     mask0[:, bass.ds(c, 1), :].rearrange("p a n -> p (a n)"),
                                     start=True, stop=True).then_inc(m_mm, 1)

                def gate_up(c, q):
                    e, (at, rows) = q // NK0, KB0[q % NK0]
                    if q % NK0 == 0:
                        pe.wait_ge(xm_ok, CREDIT + E0 * c + e + 1)
                    pe.wait_ge(hid_ok, CREDIT + NQ * c + max(q - 1, 0))
                    for w, o in ((gw0, G), (uw0, U)):
                        last = nc.tensor.matmul(o[q % 2][0:rows, :], w[:, e * I0 + at:e * I0 + at + rows],
                                                xm[:, e % 2, :], start=True, stop=True)
                    last.then_inc(gu, 1)

                def down(c, q):
                    if q == 0:
                        pe.wait_ge(ys_ok, CREDIT + c)
                    pe.wait_ge(hid_ok, CREDIT + NQ * c + q + 1)
                    rows = KB0[q % NK0][1]
                    nc.tensor.matmul(Y[:], dw0[0:rows, q, :], hid[0:rows, q % 2, :], start=q == 0,
                                     stop=q == NQ - 1).then_inc(dn, 1)

                with pe.Fori(0, TT) as c:
                    spread(c, 0)
                    for q in range(NQ):
                        if q % NK0 == 0 and q // NK0 + 1 < E0:
                            spread(c, q // NK0 + 1)
                        gate_up(c, q)
                        if q:
                            down(c, q - 1)
                    down(c, NQ - 1)
                    pe.wait_ge(ys_ok, CREDIT + c + 1)
                    pe.wait_ge(x_ok, CREDIT + c)
                    for b in range(NB):
                        last = nc.tensor.transpose(T[:, b, :], ys[:, b * P:(b + 1) * P], idf[:])
                    last.then_inc(y_t, 1)

            @block.scalar
            def _(act):
                credit(act, ys_ok)
                with act.Fori(0, TT) as c:
                    for q in range(NQ):
                        rows = KB0[q % NK0][1]
                        act.wait_ge(gu, CREDIT + NQ * c + q + 1)
                        nc.scalar.activation(sg[0:rows, q % 2, :], G[q % 2][0:rows, :], ACT.Silu).then_inc(silu, 1)
                    act.wait_ge(dn, CREDIT + NQ * c + NQ)
                    act.wait_ge(y_t, CREDIT + c)
                    nc.scalar.copy(ys[:], Y[:]).then_inc(ys_ok, 1)

            @block.vector
            def _(dve):
                credit(dve, hid_ok, x_ok, xm_ok)
                def masked(c, e):
                    dve.wait_ge(m_mm, E0 * c + e + 1)
                    dve.wait_ge(gu, CREDIT + NQ * c + NK0 * max(e - 1, 0))
                    nc.vector.tensor_tensor(xm[:, e % 2, :], xt(c), M[e % 2][:], ALU.mult).then_inc(xm_ok, 1)

                with dve.Fori(0, TT) as c:
                    masked(c, 0)
                    for q in range(NQ):
                        if q % NK0 == 0 and q // NK0 + 1 < E0:
                            masked(c, q // NK0 + 1)
                        rows = KB0[q % NK0][1]
                        dve.wait_ge(silu, NQ * c + q + 1)
                        dve.wait_ge(dn, CREDIT + NQ * c + max(q - 1, 0))
                        nc.vector.tensor_tensor(hid[0:rows, q % 2, :], sg[0:rows, q % 2, :], U[q % 2][0:rows, :],
                                                ALU.mult).then_inc(hid_ok, 1)
                    dve.wait_ge(y_t, CREDIT + c + 1)
                    nc.vector.tensor_tensor(chunk(X, c), chunk(X, c), T[:], ALU.add).then_inc(x_ok, 1)

        with ExitStack() as sc:
            def s4(name):
                return ctx.enter_context(nc.semaphore(name))

            NP = len(PAIRS)
            dif = sb("dif", [P, NP, D], F32, sc)
            sqd = sb("sqd", [P, NP, D], F32, sc)
            qv = sb("qv", [P, 2, NB, D], F32, sc)
            dist = sb("dist", [P, NP, H1], F32, sc)
            wp = sb("wp", [P, NP, H1], F32, sc)
            wf = sb("wf", [P, NB, NB, H1], F32, sc)
            prod = sb("prod", [P, 2, NB, D], F32, sc)
            den = sb("den", [P, 2, NB * H1], F32, sc)
            o1 = sb("o1", [P, NB, D], F32, sc)
            o1n = sb("o1n", [P, NB, D], F32, sc)
            ots1 = sb("ots1", [P, CH], F32, sc)
            x2 = sb("x2", [P, NB, D], F32, sc)
            y1 = sb("y1", [P, NB, D], F32, sc)
            y2 = sb("y2", [P, NB, D], F32, sc)
            sc1 = sb("sc1", [P, 4, NB, E1], F32, sc)
            eq = sb("eq1", [P, NB, E1], F32, sc)
            key = sb("key1", [P, NB, E1], F32, sc)
            top = sb("top1", [P, 6, NB], F32, sc)
            hot = sb("hot1", [P, 2, NB, E1], F32, sc)
            rest = sb("rest", [P, NB, E1], F32, sc)
            wt = sb("wt", [P, 3, NB, NE1], F32, sc)
            w3 = sb("w3", [P, NB, 3, NE1], BF16, sc)
            T = ps("T4", [P, NB, P], F32, sc)
            QV = ps("QV", [P, NB, 2 * D], F32, sc)
            Y = ps("Y4", [P, NB, P], F32, sc)
            R = ps("R4", [P, NB, E1], F32, sc)
            C = ps("C4", [3 * NE1, CH], BF16, sc)
            pick1 = [s4(f"pick1{i}") for i in range(5)]
            pick2 = [s4(f"pick2{i}") for i in range(5)]
            init = s4("init4")
            (x2_mm, x2_ok, qv_mm, qv_ok, dif_ok, sqd_ok, dist_ok, wp_ok, wf_ok, pr_ok, o1_ok, den_ok, rden_ok,
             on_ok, o_mm, ots_ok, y_mm, yb_ok, y_ok, x3_mm, x3s_ok, x3_ok, r_mm, lg_ok, ex_ok, ex1_ok, sig_ok,
             rest_ok, num_ok, dn_ok, rd_ok, w_ok, part_ok, w3_ok, c_mm, c_ok, xk2, yb_pre) = (
                s4(n + "4") for n in ("x2_mm x2_ok qv_mm qv_ok dif_ok sqd_ok dist_ok wp_ok wf_ok pr_ok o1_ok "
                "den_ok rden_ok on_ok o_mm ots_ok y_mm yb_ok y_ok x3_mm x3s_ok x3_ok r_mm lg_ok ex_ok ex1_ok "
                "sig_ok rest_ok num_ok dn_ok rd_ok w_ok part_ok w3_ok c_mm c_ok xk2 yb_pre").split())
            block = sc.enter_context(nc.Block())

            @block.tensor
            def _(pe):
                credit(pe, c_mm, r_mm, x2_mm, y_mm)
                with pe.Fori(0, TT) as c:
                    pe.wait_ge(norm.done, n2(c) + 1)
                    pe.wait_ge(x3_ok, CREDIT + c)
                    for b in range(NB):
                        last = nc.tensor.transpose(T[:, b, :], x2[:, b, :], idf[:])
                    last.then_inc(x2_mm, 1)
                    pe.wait_ge(x2_ok, c + 1)
                    pe.wait_ge(qv_ok, CREDIT + c)
                    for b in range(NB):
                        last = nc.tensor.matmul(QV[:, b, :], xts[:, b * P:(b + 1) * P],
                                                w1q[:].rearrange("p a d -> p (a d)"), start=True, stop=True)
                    last.then_inc(qv_mm, 1)
                    pe.wait_ge(on_ok, c + 1)
                    for b in range(NB):
                        last = nc.tensor.transpose(T[:, b, :], o1n[:, b, :], idf[:])
                    last.then_inc(o_mm, 1)
                    pe.wait_ge(ots_ok, c + 1)
                    pe.wait_ge(yb_ok, CREDIT + c)
                    for b in range(NB):
                        last = nc.tensor.matmul(Y[:, b, :], ots1[:, b * P:(b + 1) * P], ow1[:], start=True, stop=True)
                    last.then_inc(y_mm, 1)
                    pe.wait_ge(norm.done, n3(c) + 1)
                    for b in range(NB):
                        last = nc.tensor.transpose(T[:, b, :], xn[:, b, :], idf[:])
                    last.then_inc(x3_mm, 1)
                    pe.wait_ge(x3s_ok, c + 1)
                    pe.wait_ge(lg_ok, CREDIT + c)
                    for b in range(NB):
                        last = nc.tensor.matmul(R[:, b, :], xts[:, b * P:(b + 1) * P], rw1[:], start=True, stop=True)
                    last.then_inc(r_mm, 1)
                    pe.wait_ge(w3_ok, 3 * c + 3)
                    pe.wait_ge(c_ok, CREDIT + c)
                    hold(pe)
                    for b in range(NB):
                        last = nc.tensor.transpose(C[:, b * P:(b + 1) * P],
                                                   w3[:, b, :, :].rearrange("p a e -> p (a e)"), idb[:])
                    last.then_inc(c_mm, 1)

            @block.scalar
            def _(act):
                credit(act, c_ok, ex_ok, qv_ok, x3_ok)
                with act.Fori(0, TT) as c:
                    act.wait_ge(x2_mm, CREDIT + c + 1)
                    act.wait_ge(r_mm, CREDIT + c)
                    nc.scalar.copy(xts[:].rearrange(TOK, b=NB), T[:]).then_inc(x2_ok, 1)
                    act.wait_ge(qv_mm, c + 1)
                    act.wait_ge(pr_ok, CREDIT + 4 * c)
                    act.wait_ge(dif_ok, CREDIT + c)
                    nc.scalar.copy(qv[:].rearrange("p a b d -> p b a d"),
                                   QV[:].rearrange("p b (a d) -> p b a d", a=2)).then_inc(qv_ok, 1)
                    act.wait_ge(dif_ok, CREDIT + c + 1)
                    act.wait_ge(dist_ok, CREDIT + c)
                    nc.scalar.activation(sqd[:], dif[:], ACT.Square).then_inc(sqd_ok, 1)
                    act.wait_ge(dist_ok, CREDIT + c + 1)
                    act.wait_ge(wf_ok, CREDIT + c)
                    nc.scalar.activation(wp[:], dist[:], ACT.Exp, scale=-(DH1 ** -0.5)).then_inc(wp_ok, 1)
                    act.wait_ge(o_mm, c + 1)
                    act.wait_ge(y_mm, CREDIT + c)
                    nc.scalar.copy(ots1[:].rearrange(TOK, b=NB), T[:]).then_inc(ots_ok, 1)
                    act.wait_ge(x3_mm, c + 1)
                    act.wait_ge(qv_mm, c + 1)
                    nc.scalar.copy(xts[:].rearrange(TOK, b=NB), T[:]).then_inc(x3s_ok, 1)
                    nc.scalar.copy(xt(c).rearrange(TOK, b=NB), T[:]).then_inc(x3_ok, 1)
                    act.wait_ge(lg_ok, CREDIT + c + 1)
                    act.wait_ge(ex1_ok, CREDIT + c)
                    nc.scalar.activation(sc1[:, 1], sc1[:, 0], ACT.Exp, scale=-1.0).then_inc(ex_ok, 1)
                    act.wait_ge(c_mm, CREDIT + c + 1)
                    nc.scalar.copy(comb1[:, bass.ds(c, 1), :].rearrange("p a n -> p (a n)"), C[:]).then_inc(c_ok, 1)

            @block.vector
            def _(dve):
                credit(dve, dif_ok, dist_ok, ex1_ok, lg_ok, pr_ok, wf_ok, xk2, yb_ok)
                nc.vector.memset(wf[:], 1.0)
                nc.vector.memset(wt[:], 0.0).then_inc(init, 1)
                dve.wait_ge(init, 1)
                nc.vector.memset(wt[:, 0, :, E1:NE1], 1.0).then_inc(init, 1)
                dve.wait_ge(init, 2)
                with dve.Fori(0, TT) as c:
                    dve.wait_ge(x2_mm, CREDIT + c)
                    norm.vector(dve, chunk(X, c), x2, n2(c))
                    dve.wait_ge(qv_ok, CREDIT + c + 1)
                    at = 0
                    for t in range(NB - 1):
                        n = NB - 1 - t
                        last = nc.vector.tensor_tensor(dif[:, at:at + n, :], qv[:, 0, t + 1:NB, :],
                                                       qv[:, 0, t:t + 1, :].broadcast_to([P, n, D]), ALU.subtract)
                        at += n
                    last.then_inc(dif_ok, 1)
                    dve.wait_ge(sqd_ok, c + 1)
                    nc.vector.tensor_reduce(dist[:], sqd[:].rearrange("p a (h d) -> p (a h) d", d=DH1), AX.X,
                                            ALU.add).then_inc(dist_ok, 1)
                    dve.wait_ge(wp_ok, c + 1)
                    for k, (t, s) in enumerate(PAIRS):
                        nc.vector.tensor_copy(wf[:, t, s, :], wp[:, k, :])
                        last = nc.vector.tensor_copy(wf[:, s, t, :], wp[:, k, :])
                    last.then_inc(wf_ok, 1)
                    dve.wait_ge(wf_ok, CREDIT + c + 1)
                    nc.vector.tensor_reduce(den[:, 0, :], wf[:].rearrange("p t s h -> p t h s"), AX.X,
                                            ALU.add).then_inc(den_ok, 1)
                    dve.wait_ge(den_ok, c + 1)
                    nc.vector.reciprocal(den[:, 1, :], den[:, 0, :]).then_inc(rden_ok, 1)
                    for t in range(NB):
                        nc.vector.tensor_tensor(
                            prod[:, t % 2].rearrange("p s (h d) -> p (s h) d", d=DH1),
                            qv[:, 1].rearrange("p s (h d) -> p (s h) d", d=DH1),
                            wf[:, t].rearrange("p s h -> p (s h)").unsqueeze(2).broadcast_to([P, NB * H1, DH1]),
                            ALU.mult).then_inc(pr_ok, 1)
                        dve.wait_ge(pr_ok, CREDIT + 4 * c + t + 1)
                        nc.vector.tensor_reduce(o1[:, t, :], prod[:, t % 2].rearrange("p s n -> p n s"), AX.X,
                                                ALU.add).then_inc(o1_ok, 1)
                    dve.wait_ge(o1_ok, 4 * c + 4)
                    dve.wait_ge(rden_ok, c + 1)
                    nc.vector.tensor_tensor(o1n[:].rearrange("p b (h d) -> p (b h) d", d=DH1),
                                            o1[:].rearrange("p b (h d) -> p (b h) d", d=DH1),
                                            den[:, 1, :].unsqueeze(2).broadcast_to([P, NB * H1, DH1]),
                                            ALU.mult).then_inc(on_ok, 1)
                    dve.wait_ge(norm.done, n2(c) + 1)
                    nc.vector.tensor_tensor(y1[:], x2[:], ob1[:].unsqueeze(1).broadcast_to([P, NB, D]),
                                            ALU.add).then_inc(yb_pre, 1)
                    dve.wait_ge(yb_pre, c + 1)
                    dve.wait_ge(y_mm, CREDIT + c + 1)
                    nc.vector.tensor_tensor(y2[:], Y[:], y1[:], ALU.add).then_inc(yb_ok, 1)
                    dve.wait_ge(yb_ok, CREDIT + c + 1)
                    dve.wait_ge(xk2, CREDIT + c)
                    norm.vector(dve, y2, xn, n3(c))
                    dve.wait_ge(norm.done, n3(c) + 1)
                    hold(dve)
                    nc.vector.tensor_copy(chunk(X, c), xn[:]).then_inc(xk2, 1)
                    dve.wait_ge(r_mm, CREDIT + c + 1)
                    dve.wait_ge(ex_ok, CREDIT + c)
                    nc.vector.tensor_tensor(sc1[:, 0], R[:], gb1[:].unsqueeze(1).broadcast_to([P, NB, E1]),
                                            ALU.add).then_inc(lg_ok, 1)
                    dve.wait_ge(ex_ok, CREDIT + c + 1)
                    nc.vector.tensor_scalar(sc1[:, 2], sc1[:, 1], 1.0, None, ALU.add).then_inc(ex1_ok, 1)
                    dve.wait_ge(ex1_ok, CREDIT + c + 1)
                    nc.vector.reciprocal(sc1[:, 3], sc1[:, 2]).then_inc(sig_ok, 1)
                    dve.wait_ge(sig_ok, c + 1)
                    rk = rank[:, NB * E0:].rearrange("p (b e) -> p b e", b=NB)
                    first_of(dve, sc1[:, 3], top[:, 0, :], eq[:], key[:], top[:, 1, :], hot[:, 0], pick1, c, rk, E1)
                    dve.wait_ge(pick1[4], c + 1)
                    nc.vector.scalar_tensor_tensor(rest[:], hot[:, 0], -4.0, sc1[:, 3], ALU.mult, ALU.add).then_inc(rest_ok, 1)
                    dve.wait_ge(rest_ok, c + 1)
                    first_of(dve, rest[:], top[:, 2, :], eq[:], key[:], top[:, 3, :], hot[:, 1], pick2, c, rk, E1)
                    dve.wait_ge(pick2[4], c + 1)
                    nc.vector.tensor_tensor(top[:, 4, :], top[:, 0, :], top[:, 2, :], ALU.add)
                    nc.vector.tensor_tensor(hot[:, 0], hot[:, 0], hot[:, 1], ALU.add).then_inc(num_ok, 1)
                    dve.wait_ge(num_ok, c + 1)
                    nc.vector.reciprocal(top[:, 5, :], top[:, 4, :])
                    nc.vector.tensor_tensor(rest[:], hot[:, 0], sc1[:, 3], ALU.mult).then_inc(rd_ok, 1)
                    dve.wait_ge(rd_ok, c + 1)
                    nc.vector.tensor_tensor(wt[:, 0, :, 0:E1], rest[:],
                                            top[:, 5, :].unsqueeze(2).broadcast_to([P, NB, E1]), ALU.mult).then_inc(w_ok, 1)
                    dve.wait_ge(w_ok, c + 1)
                    dve.wait_ge(c_mm, CREDIT + c)
                    for k in range(3):
                        nc.vector.tensor_copy(w3[:, :, k, :], wt[:, k]).then_inc(w3_ok, 1)
                        if k < 2:
                            dve.wait_ge(w3_ok, 3 * c + k + 1)
                            nc.vector.tensor_tensor(wt[:, k + 1], wt[:, k], w3[:, :, k, :], ALU.subtract).then_inc(part_ok, 1)
                            dve.wait_ge(part_ok, 2 * c + k + 1)

            @block.gpsimd
            def _(pool):
                with pool.Fori(0, TT) as c:
                    norm.pool(pool, n2(c))
                    norm.pool(pool, n3(c))

        with ExitStack() as sc:
            def s5(name):
                return ctx.enter_context(nc.semaphore(name))

            G = [ps(f"G5{i}", [P, CH], F32, sc) for i in range(2)]
            U = [ps(f"U5{i}", [P, CH], F32, sc) for i in range(2)]
            M = [ps(f"M5{i}", [P, CH], F32, sc) for i in range(2)]
            Y = ps("Y5", [P, CH], F32, sc)
            T = ps("T5", [P, NB, P], F32, sc)
            m_mm, gu, silu, prod_ok, hid_ok, dn, ys_ok, y_t, x_ok, st_out = (
                s5("m_mm5"), s5("gu5"), s5("silu5"), s5("prod_ok5"), s5("hid_ok5"), s5("dn5"), s5("ys_ok5"),
                s5("y_t5"), s5("x_ok5"), s5("st_out"))
            raw = sb("raw", [P, 2, CH], F32, sc)
            xs = sb("xs", [P, NB, D], F32, sc)
            ROWS = [min(P, NE1 * I1 - P * j) for j in range(NJ1)]
            block = sc.enter_context(nc.Block())

            def before(c, j):
                return NJ1 * c + max(j - 1, 0)

            @block.sync
            def _(sp):
                with sp.Fori(0, TT) as c:
                    sp.wait_ge(norm.done, n4(c) + 1)
                    sp.dma_start(out[:, bass.ds(c, 1)].rearrange("p a b d -> p (a b) d"), chunk(X, c)).then_inc(st_out, 16)
                sp.wait_ge(st_out, 16 * TT)

            @block.tensor
            def _(pe):
                credit(pe, dn, y_t)
                def down(c, j):
                    if j == 0:
                        pe.wait_ge(ys_ok, CREDIT + c)
                    pe.wait_ge(hid_ok, CREDIT + NJ1 * c + j + 1)
                    nc.tensor.matmul(Y[:], dw1[0:ROWS[j], j, :], hid[0:ROWS[j], j % 2, :], start=j == 0,
                                     stop=j == NJ1 - 1).then_inc(dn, 1)

                with pe.Fori(0, TT) as c:
                    for j in range(NJ1):
                        n = ROWS[j]
                        pe.wait_ge(hid_ok, CREDIT + before(c, j))
                        hold(pe)
                        nc.tensor.matmul(M[j % 2][:], sel1[:, j, :],
                                         comb1[:, bass.ds(c, 1), :].rearrange("p a n -> p (a n)"),
                                         start=True, stop=True)
                        for w, o in ((gw1, G), (uw1, U)):
                            last = nc.tensor.matmul(o[j % 2][0:n, :], w[:, j * P:j * P + n], xt(c), start=True, stop=True)
                        last.then_inc(gu, 1)
                        if j:
                            down(c, j - 1)
                    down(c, NJ1 - 1)
                    pe.wait_ge(ys_ok, CREDIT + c + 1)
                    pe.wait_ge(x_ok, CREDIT + c)
                    for b in range(NB):
                        last = nc.tensor.transpose(T[:, b, :], ys[:, b * P:(b + 1) * P], idf[:])
                    last.then_inc(y_t, 1)

            @block.scalar
            def _(act):
                credit(act, ys_ok)
                with act.Fori(0, TT) as c:
                    for j in range(NJ1):
                        n = ROWS[j]
                        act.wait_ge(gu, NJ1 * c + j + 1)
                        act.wait_ge(prod_ok, CREDIT + before(c, j))
                        nc.scalar.activation(sg[0:n, j % 2, :], G[j % 2][0:n, :], ACT.Silu).then_inc(silu, 1)
                    act.wait_ge(dn, CREDIT + NJ1 * c + NJ1)
                    act.wait_ge(y_t, CREDIT + c)
                    nc.scalar.copy(ys[:], Y[:]).then_inc(ys_ok, 1)

            @block.vector
            def _(dve):
                credit(dve, hid_ok, prod_ok, x_ok)
                with dve.Fori(0, TT) as c:
                    for j in range(NJ1):
                        n = ROWS[j]
                        dve.wait_ge(silu, NJ1 * c + j + 1)
                        nc.vector.tensor_tensor(raw[0:n, j % 2, :], sg[0:n, j % 2, :], U[j % 2][0:n, :],
                                                ALU.mult).then_inc(prod_ok, 1)
                        dve.wait_ge(prod_ok, CREDIT + NJ1 * c + j + 1)
                        dve.wait_ge(dn, CREDIT + before(c, j))
                        nc.vector.tensor_tensor(hid[0:n, j % 2, :], raw[0:n, j % 2, :], M[j % 2][0:n, :],
                                                ALU.mult).then_inc(hid_ok, 1)
                    dve.wait_ge(y_t, CREDIT + c + 1)
                    nc.vector.scalar_tensor_tensor(xs[:], chunk(X, c), 2.0, T[:], ALU.mult, ALU.add).then_inc(x_ok, 1)
                    dve.wait_ge(x_ok, CREDIT + c + 1)
                    norm.vector(dve, xs, chunk(X, c), n4(c))

            @block.gpsimd
            def _(pool):
                with pool.Fori(0, TT) as c:
                    norm.pool(pool, n4(c))


def credit(engine, *signals):
    for signal in signals:
        engine.sem_inc(signal, CREDIT)


def hold(engine):
    engine.nop(nofuse=True)


def layout(x):
    f = lambda v: np.ascontiguousarray(v)
    nkv = x["L0_attn_null_kv"].reshape(H, NNULL, 2, DH)
    wq = x["L0_attn_w_q"].reshape(D, NG, KW)
    wkv = x["L0_attn_w_kv"].reshape(D, 2, NG, KW)
    down = x["L0_ffn_down_w"].transpose(0, 2, 1)
    dw0 = np.zeros((P, E0 * NK0, D), np.float32)
    for e in range(E0):
        for k, (at, rows) in enumerate(KB0):
            dw0[:rows, e * NK0 + k] = down[e, at:at + rows]
    both = lambda ew, sw: np.concatenate([ew, sw[None]], axis=0)
    gate = both(x["L1_ffn_experts_wg"], x["L1_ffn_shared_wg"]).transpose(1, 0, 2).reshape(D, NE1 * I1)
    up = both(x["L1_ffn_experts_wu"], x["L1_ffn_shared_wu"]).transpose(1, 0, 2).reshape(D, NE1 * I1)
    d1 = both(x["L1_ffn_experts_wd"], x["L1_ffn_shared_wd"]).reshape(NE1 * I1, D)
    dw1 = np.zeros((P, NJ1, D), np.float32)
    for j in range(NJ1):
        part = d1[j * P:(j + 1) * P]
        dw1[:part.shape[0], j] = part
    q1 = x["L1_attn_q_weight"].reshape(D, H1 * DH1)
    return {
        "x": f(x["L0_attn_x"].reshape(NB, TT, P, D).transpose(2, 1, 0, 3)),
        "gamma": f(x["L0_attn_gamma"].reshape(P, 1)),
        "q_scale": f(x["L0_attn_q_scale"]), "k_scale": f(x["L0_attn_k_scale"]),
        "null_k": f(nkv[:, :, 0].reshape(H * NNULL, DH)),
        "null_v": f(nkv[:, :, 1].reshape(NG, HG, NNULL, DH).transpose(1, 2, 0, 3)),
        "w_q_t": f(x["L0_attn_w_q"].reshape(D, H, DH).transpose(2, 1, 0).reshape(DH, 2, SEQ)),
        "w_qkv": f(np.concatenate([wq, wkv[:, 0], wkv[:, 1]], axis=2)),
        "w_out": f(x["L0_attn_w_out"].reshape(H * DH // P, P, D).transpose(1, 0, 2)),
        "rw0": f(x["L0_ffn_router_w"].T),
        "gw0": f(x["L0_ffn_gate_w"].transpose(2, 0, 1).reshape(D, E0 * I0)),
        "uw0": f(x["L0_ffn_up_w"].transpose(2, 0, 1).reshape(D, E0 * I0)),
        "dw0": dw0,
        "w1_q": f(q1), "w1_q_t": f(q1.T), "w1_v": f(x["L1_attn_v_weight"].reshape(D, H1 * DH1)),
        "w1_o": f(x["L1_attn_out_w"].T), "ob1": f(x["L1_attn_out_b"]),
        "rw1": f(x["L1_ffn_gate_w"]), "gb1": f(x["L1_ffn_gate_b"]),
        "gw1": f(gate), "uw1": f(up), "dw1": dw1,
    }


def kernel(**inputs):
    import concourse.bacc as _bacc
    from concourse import mybir as _mybir
    from concourse.bass_utils import run_bass_kernel_spmd as _run

    data = layout({k: np.asarray(v) for k, v in inputs.items()})
    data.update(constants())
    nc = _bacc.Bacc("TRN2", target_bir_lowering=False, num_devices=1)
    arrays, aps = {}, {}
    for name, arr in data.items():
        arrays[f"in_{name}"] = arr
        aps[name] = nc.dram_tensor(f"in_{name}", arr.shape, _mybir.dt.from_np(arr.dtype), kind="ExternalInput").ap()
    out = nc.dram_tensor("out", (P, TT, NB, D), F32, kind="ExternalOutput").ap()
    build(nc, aps, out)
    r = _run(nc, [arrays], core_ids=[0])
    return r.results[0]["out"].transpose(2, 1, 0, 3).reshape(NB, SEQ, D)
```

```python
from contextlib import ExitStack

import numpy as np

import concourse.bass as bass
from concourse import mybir

F32 = mybir.dt.float32
BF16 = mybir.dt.bfloat16
ALU = mybir.AluOpType
ACT = mybir.ActivationFunctionType
AX = mybir.AxisListType

P = 128
NB, SEQ, D = 4, 1024, 128
TT = SEQ // P
H, DH = 16, 64
NNULL = 2
HG = 4
NG = H // HG
TURNS = NB * NG
VW = DH + 1
SWQ, SWK = 3 * DH, 4 * DH
KW = HG * DH
CEN = SEQ // 2
LIFT = 40.0
EPS = 1e-5
CREDIT = 1
E0, I0 = 8, 352
E1, I1 = 16, 64
H1, DH1 = 16, 8
CH = NB * P
KB0 = [(k, min(P, I0 - k)) for k in range(0, I0, P)]
NK0 = len(KB0)
NJ1 = E1 // 2 + 1
NE1 = E1 + 1
PAIRS = [(t, s) for t in range(NB) for s in range(t + 1, NB)]
OFF = [sum(SEQ - P * i for i in range(j)) for j in range(TT + 1)]
TAB = HG * TT + TT * HG + HG * NNULL


def slopes():
    start = 2.0 ** (-2.0 ** (-(np.log2(H) - 3.0)))
    return np.array([start * start ** i for i in range(H)], dtype=np.float32).astype(np.float64)


def constants():
    sl = slopes()
    p = np.arange(P)[:, None, None]
    jt = np.arange(TT)
    key = sl[None, :, None] * (P * jt[None, None, :] + p - CEN)
    qry = LIFT - sl[None, None, :] * (P * jt[None, :, None] + p - CEN)
    nul = np.broadcast_to(sl[:, None] * (np.arange(NNULL)[None] - NNULL - CEN), (P, H, NNULL))
    tab = np.zeros((P, NG, TAB), np.float32)
    for g in range(NG):
        h = slice(g * HG, g * HG + HG)
        tab[:, g] = np.concatenate([key[:, h].reshape(P, -1), qry[:, :, h].reshape(P, -1),
                                    nul[:, h].reshape(P, -1)], axis=1)
    bits = lambda v: (np.asarray(v, np.float32).view(np.uint32) >> 16).astype(np.uint16)
    sel0 = np.zeros((E0, E0, P), np.float32)
    for e in range(E0):
        sel0[e, e] = 1
    sel1 = np.zeros((3, NE1, NJ1, P), np.float32)
    for e in range(NE1):
        sel1[:, e, e // 2, (e % 2) * I1:(e % 2) * I1 + I1] = 1
    blk = np.zeros((P, P), np.float32)
    for h in range(H1):
        blk[h * DH1:(h + 1) * DH1, h * DH1:(h + 1) * DH1] = DH1 ** -0.5
    rank = np.concatenate([np.tile(E0 - np.arange(E0), NB), np.tile(E1 - np.arange(E1), NB)])
    return {
        "c_tab": tab, "c_sel0": bits(sel0), "c_sel1": bits(sel1.reshape(3 * NE1, NJ1, P)),
        "c_blk": blk,
        "c_idf": np.eye(P, dtype=np.float32), "c_idb": bits(np.eye(P)),
        "c_future": bits(np.where(np.arange(P)[:, None] > np.arange(P)[None], -1e30, 0.0)),
        "c_rank": np.broadcast_to(rank.astype(np.float32), (P, rank.size)).copy(),
    }


def build(nc, a, out):
    ctx = ExitStack()
    with ctx:
        def sb(name, shape, dt=F32, scope=ctx):
            return scope.enter_context(nc.sbuf_tensor(name, shape, dt))

        def ps(name, shape, dt=F32, scope=ctx):
            return scope.enter_context(nc.psum_tensor(name, shape, dt))

        X = sb("X", [P, TT, NB, D])
        idf = sb("idf", [P, P])
        idb = sb("idb", [P, P], BF16)
        future = sb("future", [P, P], BF16)
        rank = sb("rank", [P, NB * (E0 + E1)])
        half = sb("half", [P, 2, 64])
        rw0 = sb("rw0", [P, E0])
        w1q = sb("w1q", [P, 2, D])
        ow1 = sb("ow1", [P, D])
        stat = sb("stat", [P, NB, 6])
        mv = sb("mv", [P, NB, 2])
        vareps = sb("vareps", [P, NB])
        rstd = sb("rstd", [P, NB])
        xn = sb("xn", [P, NB, D])

        def chunk(t, c):
            return t[:, bass.ds(c, 1), :, :].rearrange("p a b d -> p (a b) d")

        class Norm:

            def __init__(self, name):
                s = lambda n: ctx.enter_context(nc.semaphore(f"{name}_{n}"))
                self.stats, self.mean, self.var, self.root, self.done = (
                    s("stats"), s("mean"), s("var"), s("root"), s("done"))

            def vector_stats(self, dve, src, n):
                for b in range(NB):
                    last = nc.vector.bn_stats(stat[:, b, :], src[:, b, :])
                last.then_inc(self.stats, 1)
                dve.wait_ge(self.stats, n + 1)
                hold(dve)
                for b in range(NB):
                    last = nc.vector.bn_aggr(mv[:, b, :], stat[:, b, :])
                last.then_inc(self.mean, 1)
                dve.wait_ge(self.mean, n + 1)
                nc.vector.tensor_scalar(vareps[:], mv[:, :, 1], EPS, None, ALU.add).then_inc(self.var, 1)

            def vector_apply(self, dve, src, dst, n):
                dve.wait_ge(self.root, n + 1)
                for b in range(NB):
                    last = nc.vector.tensor_scalar(dst[:, b, :], src[:, b, :], mv[:, b, 0:1],
                                                   rstd[:, b:b + 1], ALU.subtract, ALU.mult)
                last.then_inc(self.done, 1)

            def vector(self, dve, src, dst, n):
                self.vector_stats(dve, src, n)
                self.vector_apply(dve, src, dst, n)

            def pool(self, pool, n):
                pool.wait_ge(self.var, n + 1)
                nc.gpsimd.tensor_tensor(rstd[:], vareps[:], half[:, 0, 0:NB], ALU.pow).then_inc(self.root, 1)

        norm = Norm("norm")
        n0, n1, n2, n3, n4 = (lambda c: c), (lambda c: TT + c), (lambda c: 2 * TT + 2 * c), (
            lambda c: 2 * TT + 2 * c + 1), (lambda c: 4 * TT + c)

        with ExitStack() as sc:
            def s1(name):
                return ctx.enter_context(nc.semaphore(name))

            wqkv = sb("wqkv", [P, NG, 3 * KW + HG * NNULL], F32, sc)
            wout = sb("wout", [P, H * DH // P, D], F32, sc)
            tabs = sb("tabs", [P, NG, TAB], F32, sc)
            nvb = sb("nvb", [P, NG, NNULL, HG, VW], F32, sc)
            scl = sb("scl", [P, DH], F32, sc)
            ksc = sb("ksc", [P, DH], F32, sc)
            w1qt = sb("w1qt", [P, D], F32, sc)
            w1v = sb("w1v", [P, D], F32, sc)
            w1m = sb("w1m", [P, D], F32, sc)
            blk = sb("blk", [P, D], F32, sc)
            nks = sb("nks", [H * NNULL, 3, DH], F32, sc)
            nkt = sb("nkt", [DH, H * NNULL], F32, sc)
            nkss = sb("nkss", [H * NNULL, 2], F32, sc)
            gam = sb("gam", [P, 1], F32, sc)
            xnt = nc.dram_tensor("xnt", (P, NB, TT, P), F32).ap()
            xnst = sb("xnst", [P, 2, NB, P], F32, sc)
            xns = sb("xns", [P, SEQ], F32, sc)
            keyb = sb("keyb", [P, HG * TT], F32, sc)
            qterm = sb("qterm", [P, TT * HG + HG * NNULL], F32, sc)
            nvc = sb("nvc", [P, TT, HG, VW], F32, sc)
            nvt = sb("nvt", [P, 2, HG, VW], F32, sc)
            Pw = sb("Pw", [P, 2, OFF[TT]], F32, sc)
            QT = sb("QT", [P, 2, HG, SEQ], BF16, sc)
            KT = sb("KT", [P, 2, HG, SEQ], BF16, sc)
            V = sb("V", [P, 2, TT, HG, VW], F32, sc)
            QS = sb("QS", [P, TT, HG, SWQ], BF16, sc)
            KS = sb("KS", [P, TT, HG, SWK], BF16, sc)
            kn = sb("kn", [P, HG, DH], F32, sc)
            qp = sb("qp", [P, HG, DH], F32, sc)
            ee = sb("ee", [P, 3, HG], F32, sc)
            qkraw = sb("qkraw", [P, 2 * KW], F32, sc)
            rawn = sb("rawn", [P, HG * NNULL], F32, sc)
            sq = sb("sq", [P, 2 * KW], F32, sc)
            sqq = sb("sqq", [P, KW], F32, sc)
            qn = sb("qn", [P, HG, DH], F32, sc)
            ss = sb("ss", [P, 2, 2 * HG], F32, sc)
            rn = sb("rn", [P, 2 * HG], F32, sc)
            bs = sb("bs", [P, HG], F32, sc)
            bn = sb("bn", [P, HG], F32, sc)
            nl = sb("nl", [P, TT, HG * NNULL], F32, sc)
            pn = sb("pn", [P, TT, HG * NNULL], F32, sc)
            oraw = sb("oraw", [P, 4, VW], F32, sc)
            rl = sb("rl", [P, 2, 4], F32, sc)
            OS = sb("OS", [P, TT, KW], F32, sc)
            ots = sb("ots", [P, 2, KW], F32, sc)

            S = [ps(f"S{i}", [P, SEQ], F32, sc) for i in range(2)]
            O = [ps(f"O{i}", [P, 4, P], F32, sc) for i in range(2)]
            A = [ps(f"A{i}", [P, 512], F32, sc) for i in range(2)]

            ld_xn, ld_x, ld_w, ld_c, ld_nv = s1("ld_xn"), s1("ld_x"), s1("ld_w"), s1("ld_c"), s1("ld_nv")
            consts = s1("consts")
            scale2, scale_ok, null_sq, null_ss, null_cl, null_rn, null_n, null_k = (
                s1("scale2"), s1("scale_ok"), s1("null_sq"), s1("null_ss"), s1("null_cl"), s1("null_rn"),
                s1("null_n"), s1("null_k"))
            st_xn, null_t, null_te, wnull_mm, wnull_ok = s1("st_xn"), s1("null_t"), s1("null_te"), s1("wnull_mm"), s1("wnull_ok")
            g_mm, g_ok, m_mm, m_ok = s1("g_mm"), s1("g_ok"), s1("m_mm"), s1("m_ok")
            xnt_mm, xnt_ok = s1("xnt_mm"), s1("xnt_ok")
            xns_ok = s1("xns_ok")
            proj = s1("proj")
            raw_ok, sq_ok, v_ok, ss_red, ss_ok, rn_ok = s1("raw_ok"), s1("sq_ok"), s1("v_ok"), s1("ss_red"), s1("ss_ok"), s1("rn_ok")
            kq_ok, qp_ok, sq2_ok, bs_ok, bn_ok = s1("kq_ok"), s1("qp_ok"), s1("sq2_ok"), s1("bs_ok"), s1("bn_ok")
            khi_ok, klo_ok, qhi_ok, qlo_ok = s1("khi_ok"), s1("klo_ok"), s1("qhi_ok"), s1("qlo_ok")
            e_ok, ep_ok, er_ok, nl_add, nl_ok = s1("e_ok"), s1("ep_ok"), s1("er_ok"), s1("nl_add"), s1("nl_ok")
            pn_ok = s1("pn_ok")
            tr, tq_ok, tk_ok = s1("tr"), s1("tq_ok"), s1("tk_ok")
            nvt_ok, nvu_ok = s1("nvt_ok"), s1("nvu_ok")
            tab_ok = s1("tab_ok")
            qk, exp_ok, pv = s1("qk"), s1("exp_ok"), s1("pv")
            or_ok, rl_ok, on = s1("or_ok"), s1("rl_ok"), s1("on")
            ctr, cot, cmm, cy = s1("ctr"), s1("cot"), s1("cmm"), s1("cy")

            PREP_AT = [0] + [5 + 4 * u for u in range(TT - 1)]
            NULL_AT = (2, 4, 4, 5, 7, 9, 9, 12)

            def prep(slot, lag):
                return [u for u in range(TT) if PREP_AT[u] + lag == slot]

            block = sc.enter_context(nc.Block())

            @block.sync
            def _(sp):
                credit(sp, st_xn)
                for c in range(TT):
                    sp.dma_start(X[:, c], a["x"][:, c]).then_inc(ld_x, 16)
                for dst, src in ((idf, "c_idf"), (idb, "c_idb"), (future, "c_future"), (rank, "c_rank"), (tabs, "c_tab")):
                    sp.dma_start(dst[:], a[src].bitcast(dst.dtype)).then_inc(ld_c, 16)
                sp.dma_start(gam[:], a["gamma"]).then_inc(ld_c, 16)
                sp.dma_start(scl[:], a["q_scale"].partition_broadcast(P)).then_inc(ld_c, 16)
                sp.dma_start(ksc[:], a["k_scale"].partition_broadcast(P)).then_inc(ld_c, 16)
                sp.dma_start(nks[:, 0, :], a["null_k"]).then_inc(ld_c, 16)
                sp.dma_start(Pw[0:DH, 0, 0:H * P], a["w_q_t"]).then_inc(ld_c, 16)
                sp.dma_start(wqkv[:, :, 0:3 * KW], a["w_qkv"]).then_inc(ld_w, 16)
                for g in range(NG):
                    for k in range(NNULL):
                        sp.dma_start(nvb[:, g, k, :, 0:DH], a["null_v"][g, k].partition_broadcast(P)).then_inc(ld_nv, 16)
                sp.dma_start(wout[:], a["w_out"]).then_inc(ld_w, 16)
                for dst, src in ((w1q[:, 0, :], "w1_q"), (ow1[:], "w1_o"), (rw0[:], "rw0"),
                                 (w1qt[:], "w1_q_t"), (w1v[:], "w1_v"), (blk[:], "c_blk")):
                    sp.dma_start(dst, a[src]).then_inc(ld_w, 16)
                with sp.Fori(0, TT // 2) as i:
                    for r in range(2):
                        c = 2 * i + r
                        sp.wait_ge(xnt_ok, CREDIT + c + 1)
                        sp.dma_start(xnt[:, :, bass.ds(c, 1), :].rearrange("p b a n -> p (b a) n"), xnst[:, r]).then_inc(st_xn, 16)
                sp.wait_ge(st_xn, CREDIT + 16 * TT)

                def load_x(n):
                    sp.wait_ge(proj, 8 * n)
                    sp.dma_start(xns[:].rearrange("p (c n) -> p c n", n=P),
                                 xnt[:, bass.ds((n // NG) % NB, 1)].rearrange("p a c n -> p (a c) n")).then_inc(ld_xn, 16)

                load_x(0)
                with sp.Fori(0, TURNS) as t:
                    load_x(t + 1)

            LDC, LDW, LDNV = 16 * 10, 16 * 8, 16 * NG * NNULL

            def bcast(ap, shape):
                return ap.broadcast_to(shape)

            @block.tensor
            def _(pe):
                credit(pe, cmm, ctr, pv, xnt_mm)
                def project(n, u):
                    g = n % NG
                    if u == 0:
                        pe.wait_ge(ld_xn, 16 * (n + 1))
                    pe.wait_ge(v_ok, 8 * n + u)
                    pe.wait_ge(raw_ok, 8 * n + u)
                    x = xns[:, u * P:(u + 1) * P]
                    w = wqkv[:, bass.ds(g, 1), :].rearrange("p a n -> p (a n)")
                    nc.tensor.matmul(A[0][:], x, w[:, 0:2 * KW], start=True, stop=True)
                    nc.tensor.matmul(A[1][:, 0:KW + HG * NNULL], x, w[:, 2 * KW:], start=True, stop=True).then_inc(proj, 1)

                def transposes(t, us):
                    for part in (khi_ok, klo_ok, qhi_ok, qlo_ok):
                        pe.wait_ge(part, 8 * t + 8)
                    pe.wait_ge(ep_ok, 24 * t + 24)
                    pe.wait_ge(exp_ok, CREDIT + 32 * t)
                    for u in us:
                        if u >= 2:
                            pe.wait_ge(tq_ok, 8 * t + u - 1)
                            pe.wait_ge(tk_ok, 8 * t + u - 1)
                        Sb = S[u % 2][:].bitcast(BF16).rearrange("p (k h n) -> p k h n", k=4, h=HG)
                        for h in range(HG):
                            nc.tensor.transpose(Sb[:, 0, h, :], QS[:, u, h, 0:P], idb[:])
                            nc.tensor.transpose(Sb[:, 1, h, :], QS[:, u, h, DH:DH + P], idb[:])
                        for h in range(HG):
                            nc.tensor.transpose(Sb[:, 2, h, :], KS[:, u, h, 0:P], idb[:])
                            last = nc.tensor.transpose(Sb[:, 3, h, :], KS[:, u, h, P:2 * P], idb[:])
                        last.then_inc(tr, 1)

                def scores(t, h, jt):
                    k = h * TT + jt
                    if k == 0:
                        pe.wait_ge(tq_ok, 8 * t + 8)
                        pe.wait_ge(tk_ok, 8 * t + 8)
                    if k >= 2:
                        pe.wait_ge(exp_ok, CREDIT + 32 * t + k - 1)
                    n = SEQ - P * jt
                    for c in range(0, n, 512):
                        w = min(512, n - c)
                        for k in range(2):
                            last = nc.tensor.matmul(S[jt % 2][:, c:c + w], KT[:, k, h, jt * P:(jt + 1) * P],
                                                    QT[:, k, h, jt * P + c:jt * P + c + w], start=k == 0,
                                                    stop=k == 1 and c > 0)
                        if c == 0:
                            last = nc.tensor.matmul(S[jt % 2][:, 0:P], idb[:], future[:], start=False, stop=True)
                    last.then_inc(qk, 1)

                def values(t, r, h, it):
                    if h == 0 and it == 0:
                        pe.wait_ge(v_ok, 8 * t + 8)
                    if it % 4 == 0:
                        if h:
                            pe.wait_ge(on, CREDIT + 8 * t + 2 * (h - 1) + it // 4 + 1)
                        else:
                            pe.wait_ge(cy, CREDIT + 2 * t)
                    pe.wait_ge(exp_ok, CREDIT + 32 * t + h * TT + it + 1)
                    o = O[it // 4][:, it % 4, 0:VW]
                    for jt in range(it + 1):
                        at = OFF[jt] + (it - jt) * P
                        last = nc.tensor.matmul(o, Pw[:, h % 2, at:at + P], V[:, r, jt, h, :],
                                                start=jt == 0, stop=jt == it)
                    last.then_inc(pv, 1)

                def project_out(t):
                    g = t % NG
                    pe.wait_ge(v_ok, 8 * t + 16)
                    pe.wait_ge(raw_ok, 8 * t + 16)
                    w = wout[:, bass.ds(g * 2, 2), :]
                    for it in range(TT + 1):
                        if it < TT:
                            transposes(t + 1, [it])
                            pe.wait_ge(on, CREDIT + 8 * t + 7 + it // 4)
                            if it >= 2:
                                pe.wait_ge(cot, CREDIT + 8 * t + it - 1)
                            for k in range(2):
                                last = nc.tensor.transpose(A[it % 2][:, k * P:(k + 1) * P],
                                                           OS[:, it, k * P:(k + 1) * P], idf[:])
                            last.then_inc(ctr, 1)
                        if it:
                            j = it - 1
                            if j % 4 == 0:
                                pe.wait_ge(on, CREDIT + 8 * t + 7 + j // 4)
                            pe.wait_ge(cot, CREDIT + 8 * t + j + 1)
                            for k in range(2):
                                last = nc.tensor.matmul(O[j // 4][:, j % 4, :], ots[:, j % 2, k * P:(k + 1) * P],
                                                        w[:, k, :], start=k == 0, stop=k == 1)
                            last.then_inc(cmm, 1)

                pe.wait_ge(ld_c, LDC)
                pe.wait_ge(ld_w, LDW)
                pe.wait_ge(null_k, 1)
                nc.tensor.transpose(A[0][0:DH, 0:H * NNULL], nks[:, 2, :], idf[0:H * NNULL, 0:H * NNULL]).then_inc(null_t, 1)
                pe.wait_ge(null_te, 1)
                for h in range(H):
                    wt = Pw[0:DH, 0, h * P:(h + 1) * P]
                    last = nc.tensor.matmul(A[1][:, h * NNULL:(h + 1) * NNULL], wt,
                                            nkt[:, h * NNULL:(h + 1) * NNULL], start=True, stop=True)
                last.then_inc(wnull_mm, 1)
                nc.tensor.matmul(O[0][:, 0, :], w1q[:, 0, :], w1v[:], start=True, stop=True).then_inc(g_mm, 1)
                pe.wait_ge(g_ok, 1)
                nc.tensor.matmul(O[1][:, 0, :], w1qt[:], w1m[:], start=True, stop=True).then_inc(m_mm, 1)

                with pe.Fori(0, TT // 2) as i:
                    for r in range(2):
                        c = 2 * i + r
                        pe.wait_ge(norm.done, n0(c) + 1)
                        pe.wait_ge(xnt_ok, CREDIT + 2 * i)
                        for b in range(NB):
                            last = nc.tensor.transpose(S[r][:, b * P:(b + 1) * P], xn[:, b, :], idf[:])
                        last.then_inc(xnt_mm, 1)

                pe.wait_ge(wnull_ok, 1)
                pe.wait_ge(xnt_ok, CREDIT + TT)
                for u in range(TT):
                    project(0, u)
                transposes(0, range(TT))
                with pe.Fori(0, TURNS // 2) as i:
                    for r in range(2):
                        t = 2 * i + r
                        for slot in range((HG + 1) * TT):
                            h, s = slot // TT, slot % TT
                            if h < HG:
                                scores(t, h, s)
                            if h:
                                values(t, r, h - 1, s)
                            for u in prep(slot, 0):
                                if u == 0:
                                    pe.wait_ge(cot, CREDIT + 8 * t)
                                project(t + 1, u)
                        project_out(t)

            @block.scalar
            def _(act):
                credit(act, cot, exp_ok, xnt_ok)
                def products_out(n, u):
                    act.wait_ge(proj, 8 * n + u + 1)
                    act.wait_ge(kq_ok, 8 * n + u)
                    act.wait_ge(ss_red, 8 * n + u)
                    nc.scalar.copy(qkraw[:], A[0][:]).then_inc(raw_ok, 1)

                def high_key(n, u):
                    act.wait_ge(kq_ok, 8 * n + u + 1)
                    act.wait_ge(tr, 8 * n)
                    nc.scalar.copy(KS[:, u, :, 0:2 * DH].rearrange("p h (k d) -> p h k d", k=2),
                                   kn[:].unsqueeze(2).broadcast_to([P, HG, 2, DH])).then_inc(khi_ok, 1)

                def squares2(n, u):
                    act.wait_ge(qp_ok, 8 * n + u + 1)
                    act.wait_ge(bs_ok, 8 * n + u)
                    nc.scalar.copy(QS[:, u, :, DH:2 * DH], qp[:]).then_inc(qhi_ok, 1)
                    nc.scalar.activation(sqq[:].rearrange("p (h d) -> p h d", h=HG), qp[:],
                                         ACT.Square).then_inc(sq2_ok, 1)

                def queries_out(t, u):
                    act.wait_ge(tr, 8 * t + u + 1)
                    nc.scalar.copy(QT[:].rearrange("p k h n -> p (k h) n")[:, :, u * P:(u + 1) * P],
                                   S[u % 2][:, 0:512].bitcast(BF16).rearrange("p (k n) -> p k n", n=P)).then_inc(tq_ok, 1)

                def null_exp(n):
                    act.wait_ge(nl_ok, 8 * n + 8)
                    act.wait_ge(nvu_ok, 8 * n)
                    nc.scalar.activation(pn[:], nl[:], ACT.Exp).then_inc(pn_ok, 1)

                act.wait_ge(ld_c, LDC)
                act.wait_ge(null_t, 1)
                nc.scalar.copy(nkt[:], A[0][0:DH, 0:H * NNULL]).then_inc(null_te, 1)
                act.wait_ge(wnull_mm, 1)
                nc.scalar.copy(wqkv[:, :, 3 * KW:], A[1][:, 0:H * NNULL].rearrange("p (g n) -> p g n", g=NG)).then_inc(wnull_ok, 1)
                with act.Fori(0, TT // 2) as i:
                    for r in range(2):
                        c = 2 * i + r
                        act.wait_ge(xnt_mm, CREDIT + c + 1)
                        act.wait_ge(st_xn, CREDIT + 32 * i)
                        nc.scalar.activation(xnst[:, r], S[r][:, 0:CH].rearrange("p (b n) -> p b n", b=NB), ACT.Copy,
                                             scale=gam[:, 0:1]).then_inc(xnt_ok, 1)
                for u in range(TT):
                    products_out(0, u)
                    high_key(0, u)
                    squares2(0, u)
                null_exp(0)
                for u in range(TT):
                    queries_out(0, u)
                with act.Fori(0, TURNS // 2) as i:
                    for r in range(2):
                        t = 2 * i + r
                        for slot in range((HG + 1) * TT):
                            h, jt = slot // TT, slot % TT
                            if h < HG:
                                if h == 0 and jt == 0:
                                    act.wait_ge(tab_ok, t + 1)
                                    act.wait_ge(pv, CREDIT + 32 * t)
                                if h >= 2 and jt == 0:
                                    act.wait_ge(pv, CREDIT + 32 * t + (h - 1) * TT)
                                act.wait_ge(qk, 32 * t + h * TT + jt + 1)
                                n = SEQ - P * jt
                                nc.scalar.activation(Pw[:, h % 2, OFF[jt]:OFF[jt] + n], S[jt % 2][:, 0:n], ACT.Exp,
                                                     bias=keyb[:, h * TT + jt:h * TT + jt + 1]).then_inc(exp_ok, 1)
                            for u in prep(slot, 1):
                                products_out(t + 1, u)
                            for u in prep(slot, 4):
                                high_key(t + 1, u)
                            for u in prep(slot, 5):
                                squares2(t + 1, u)
                        null_exp(t + 1)
                        for it in range(TT):
                            queries_out(t + 1, it)
                            act.wait_ge(ctr, CREDIT + 8 * t + it + 1)
                            act.wait_ge(cmm, CREDIT + 8 * t + max(it - 1, 0))
                            nc.scalar.copy(ots[:, it % 2, :], A[it % 2][:, 0:KW]).then_inc(cot, 1)

            @block.vector
            def _(dve):
                credit(dve, cy, on)
                def values_out(n, r, u):
                    dve.wait_ge(proj, 8 * n + u + 1)
                    if u == 0 and not isinstance(n, int):
                        dve.wait_ge(pv, CREDIT + 32 * (n - 1))
                    nc.vector.tensor_copy(rawn[:], A[1][:, KW:KW + HG * NNULL])
                    nc.vector.tensor_copy(V[:, r, u, :, 0:DH],
                                          A[1][:, 0:KW].rearrange("p (h d) -> p h d", h=HG)).then_inc(v_ok, 1)

                def sums(n, u):
                    dve.wait_ge(raw_ok, 8 * n + u + 1)
                    nc.vector.tensor_tensor(sq[:], qkraw[:], qkraw[:], ALU.mult).then_inc(sq_ok, 1)
                    dve.wait_ge(sq_ok, 8 * n + u + 1)
                    nc.vector.tensor_reduce(ss[:, 0, :], sq[:].rearrange("p (h d) -> p h d", d=DH), AX.X,
                                            ALU.add).then_inc(ss_red, 1)
                    dve.wait_ge(ss_red, 8 * n + u + 1)
                    nc.vector.tensor_scalar(ss[:, 1, :], ss[:, 0, :], 1e-24, None, ALU.max).then_inc(ss_ok, 1)

                def directions(n, u):
                    dve.wait_ge(rn_ok, 8 * n + u + 1)
                    dve.wait_ge(qp_ok, 8 * n + u)
                    dve.wait_ge(klo_ok, 8 * n + u)
                    if u == 0:
                        dve.wait_ge(pn_ok, n)
                    dve.wait_ge(v_ok, 8 * n + u + 1)
                    nc.vector.tensor_tensor(kn[:], qkraw[:, KW:2 * KW].rearrange("p (h d) -> p h d", h=HG),
                                            bcast(rn[:, HG:2 * HG].unsqueeze(2), [P, HG, DH]), ALU.mult)
                    nc.vector.tensor_tensor(nl[:, u, :].rearrange("p (h k) -> p h k", k=NNULL),
                                            rawn[:].rearrange("p (h k) -> p h k", k=NNULL),
                                            bcast(rn[:, 0:HG].unsqueeze(2), [P, HG, NNULL]), ALU.mult)
                    nc.vector.tensor_tensor(qn[:], qkraw[:, 0:KW].rearrange("p (h d) -> p h d", h=HG),
                                            bcast(rn[:, 0:HG].unsqueeze(2), [P, HG, DH]), ALU.mult).then_inc(kq_ok, 1)

                def bound(n, u):
                    dve.wait_ge(sq2_ok, 8 * n + u + 1)
                    dve.wait_ge(bn_ok, 8 * n + u)
                    nc.vector.tensor_reduce(bs[:], sqq[:].rearrange("p (h d) -> p h d", d=DH), AX.X,
                                            ALU.add).then_inc(bs_ok, 1)

                def low_query(n, u):
                    dve.wait_ge(qhi_ok, 8 * n + u + 1)
                    dve.wait_ge(tr, 8 * n)
                    nc.vector.tensor_tensor(QS[:, u, :, 0:DH], qp[:], QS[:, u, :, DH:2 * DH], ALU.subtract).then_inc(qlo_ok, 1)

                def guard(n, u):
                    dve.wait_ge(bn_ok, 8 * n + u + 1)
                    dve.wait_ge(kq_ok, 8 * n + u + 1)
                    nc.vector.tensor_tensor(ee[:, 0], qterm[:, u * HG:(u + 1) * HG], bn[:], ALU.subtract).then_inc(e_ok, 1)
                    dve.wait_ge(e_ok, 8 * n + u + 1)
                    x = nl[:, u, :].rearrange("p (h k) -> p h k", k=NNULL)
                    nc.vector.tensor_tensor(x, x, bcast(ee[:, 0].unsqueeze(2), [P, HG, NNULL]), ALU.add).then_inc(nl_add, 1)
                    for k in range(3):
                        part = QS[:, u, :, 2 * DH + k]
                        nc.vector.tensor_copy(part, ee[:, k]).then_inc(ep_ok, 1)
                        if k < 2:
                            dve.wait_ge(ep_ok, 24 * n + 3 * u + k + 1)
                            nc.vector.tensor_tensor(ee[:, k + 1], ee[:, k], part, ALU.subtract).then_inc(er_ok, 1)
                            dve.wait_ge(er_ok, 16 * n + 2 * u + k + 1)
                    dve.wait_ge(nl_add, 8 * n + u + 1)
                    nc.vector.tensor_tensor(nl[:, u, :], nl[:, u, :], qterm[:, TT * HG:], ALU.add).then_inc(nl_ok, 1)

                def head_out(t, h, half_):
                    dve.wait_ge(pv, CREDIT + 32 * t + h * TT + half_ * 4 + 4)
                    if h == 0:
                        dve.wait_ge(ctr, CREDIT + 8 * t)
                        dve.wait_ge(nvu_ok, 8 * t + half_ * 4 + 4)
                    k = 8 * t + h * 2 + half_
                    dve.wait_ge(on, CREDIT + k)
                    nc.vector.tensor_tensor(oraw[:], O[half_][:, :, 0:VW], nvc[:, half_ * 4:half_ * 4 + 4, h, :],
                                            ALU.add).then_inc(or_ok, 1)
                    dve.wait_ge(or_ok, k + 1)
                    nc.vector.reciprocal(rl[:, half_, :], oraw[:, :, DH]).then_inc(rl_ok, 1)
                    dve.wait_ge(rl_ok, k + 1)
                    nc.vector.tensor_tensor(OS[:, half_ * 4:half_ * 4 + 4, h * DH:(h + 1) * DH], oraw[:, :, 0:DH],
                                            bcast(rl[:, half_, :].unsqueeze(2), [P, 4, DH]), ALU.mult).then_inc(on, 1)

                def keys_out(t, u):
                    dve.wait_ge(tr, 8 * t + u + 1)
                    nc.vector.tensor_copy(KT[:].rearrange("p k h n -> p (k h) n")[:, :, u * P:(u + 1) * P],
                                          S[u % 2][:, 512:].bitcast(BF16).rearrange("p (k n) -> p k n", n=P)).then_inc(tk_ok, 1)

                def null_values(n, u):
                    if u == 0:
                        dve.wait_ge(pn_ok, n + 1)
                        dve.wait_ge(on, CREDIT + 8 * n)
                    w = pn[:, u, :].rearrange("p (h k) -> p h k", k=NNULL)
                    vals = nvb[:, bass.ds(n % NG, 1)].rearrange("p a k h d -> p (a k) h d")
                    nc.vector.tensor_tensor(nvc[:, u], bcast(w[:, :, 0:1], [P, HG, VW]), vals[:, 0], ALU.mult)
                    nc.vector.tensor_tensor(nvt[:, u % 2], bcast(w[:, :, 1:2], [P, HG, VW]), vals[:, 1],
                                            ALU.mult).then_inc(nvt_ok, 1)
                    dve.wait_ge(nvt_ok, 8 * n + u + 1)
                    nc.vector.tensor_tensor(nvc[:, u], nvc[:, u], nvt[:, u % 2], ALU.add).then_inc(nvu_ok, 1)

                nc.vector.memset(half[:, 0, :], -0.5)
                nc.vector.memset(half[:, 1, :], 0.5).then_inc(consts, 1)
                for r in range(2):
                    last = nc.vector.memset(V[:, r, :, :, DH:VW], 1.0)
                last.then_inc(consts, 1)
                nc.vector.memset(nvb[:, :, :, :, DH:VW], 1.0)
                nc.vector.memset(QS[:, :, :, 2 * DH:SWQ], 0.0)
                nc.vector.memset(KS[:, :, :, 3 * DH:SWK], 0.0)
                dve.wait_ge(ld_c, LDC)
                dve.wait_ge(ld_w, LDW)
                nc.vector.scalar_tensor_tensor(scl[:], scl[:], 8.0, ksc[:], ALU.mult, ALU.mult).then_inc(scale_ok, 1)
                nc.vector.tensor_tensor(nks[:, 1, :], nks[:, 0, :], nks[:, 0, :], ALU.mult).then_inc(null_sq, 1)
                dve.wait_ge(null_sq, 1)
                nc.vector.tensor_reduce(nkss[:, 0:1], nks[:, 1, :], AX.X, ALU.add).then_inc(null_ss, 1)
                dve.wait_ge(null_ss, 1)
                nc.vector.tensor_scalar(nkss[:, 0:1], nkss[:, 0:1], 1e-24, None, ALU.max).then_inc(null_cl, 1)
                dve.wait_ge(null_rn, 1)
                dve.wait_ge(scale_ok, 1)
                nc.vector.scalar_tensor_tensor(nks[:, 2, :], nks[:, 0, :], nkss[:, 1:2], scl[0:H * NNULL, :],
                                               ALU.mult, ALU.mult).then_inc(null_k, 1)
                dve.wait_ge(g_mm, 1)
                nc.vector.tensor_tensor(w1m[:], O[0][:, 0, :], blk[:], ALU.mult).then_inc(g_ok, 1)
                dve.wait_ge(m_mm, 1)
                nc.vector.tensor_copy(w1q[:, 1, :], O[1][:, 0, :]).then_inc(m_ok, 1)
                nc.vector.memset(KS[:, :, :, 3 * DH:3 * DH + 3], 1.0).then_inc(consts, 1)

                dve.wait_ge(ld_x, 16 * TT)
                dve.wait_ge(consts, 3)
                dve.wait_ge(ld_nv, LDNV)
                with dve.Fori(0, TT) as c:
                    dve.wait_ge(xnt_mm, CREDIT + c)
                    norm.vector(dve, chunk(X, c), xn, n0(c))
                for u in range(TT):
                    values_out(0, 0, u)
                    sums(0, u)
                    directions(0, u)
                    low_query(0, u)
                    bound(0, u)
                    guard(0, u)
                for u in range(TT):
                    keys_out(0, u)
                with dve.Fori(0, TURNS // 2) as i:
                    for r in range(2):
                        t = 2 * i + r
                        for slot in range((HG + 1) * TT):
                            h, s = slot // TT, slot % TT
                            if h and s % 4 == 3:
                                head_out(t, h - 1, s // 4)
                            for u in prep(slot, 1):
                                values_out(t + 1, 1 - r, u)
                                sums(t + 1, u)
                            for u in prep(slot, 6):
                                low_query(t + 1, u)
                                bound(t + 1, u)
                            for u in prep(slot, 3):
                                directions(t + 1, u)
                            for u in prep(slot, 8):
                                guard(t + 1, u)
                            for u in range(TT):
                                if NULL_AT[u] == slot:
                                    null_values(t, u)
                        for u in range(TT):
                            keys_out(t + 1, u)
                        b = t // NG
                        for k in range(2):
                            dve.wait_ge(cmm, CREDIT + 8 * t + 4 * k + 4)
                            dve.wait_ge(cy, CREDIT + 2 * t)
                            x = X[:, 4 * k:4 * k + 4, bass.ds(b, 1), :].rearrange("p c a d -> p (c a) d")
                            nc.vector.tensor_tensor(x, x, O[k][:], ALU.add).then_inc(cy, 1)

            @block.gpsimd
            def _(pool):
                def load_turn(n):
                    pool.wait_ge(nl_ok, 8 * n)
                    g = n % NG
                    nc.gpsimd.tensor_copy(qterm[:], tabs[:, bass.ds(g, 1), HG * TT:].rearrange("p a n -> p (a n)")).then_inc(xns_ok, 1)

                def roots(n, u):
                    pool.wait_ge(ss_ok, 8 * n + u + 1)
                    pool.wait_ge(kq_ok, 8 * n + u)
                    nc.gpsimd.tensor_tensor(rn[:], ss[:, 1, :], half[:, 0, 0:2 * HG], ALU.pow).then_inc(rn_ok, 1)

                def low_key(n, u):
                    pool.wait_ge(khi_ok, 8 * n + u + 1)
                    nc.gpsimd.tensor_tensor(KS[:, u, :, 2 * DH:3 * DH], kn[:], KS[:, u, :, 0:DH], ALU.subtract).then_inc(klo_ok, 1)

                def scale_q(n, u):
                    pool.wait_ge(kq_ok, 8 * n + u + 1)
                    pool.wait_ge(qlo_ok, 8 * n + u)
                    nc.gpsimd.tensor_tensor(qp[:], qn[:], bcast(scl[:].unsqueeze(1), [P, HG, DH]),
                                            ALU.mult).then_inc(qp_ok, 1)

                def bound_root(n, u):
                    pool.wait_ge(bs_ok, 8 * n + u + 1)
                    pool.wait_ge(e_ok, 8 * n + u)
                    nc.gpsimd.tensor_tensor(bn[:], bs[:], half[:, 1, 0:HG], ALU.pow).then_inc(bn_ok, 1)

                pool.wait_ge(consts, 1)
                pool.wait_ge(ld_c, LDC)
                pool.wait_ge(null_cl, 1)
                nc.gpsimd.tensor_tensor(nkss[:, 1:2], nkss[:, 0:1], half[0:H * NNULL, 0, 0:1], ALU.pow).then_inc(null_rn, 1)
                with pool.Fori(0, TT) as c:
                    norm.pool(pool, n0(c))
                pool.wait_ge(xnt_ok, CREDIT + TT)
                pool.wait_ge(wnull_mm, 1)
                pool.wait_ge(scale_ok, 1)
                load_turn(0)
                for u in range(TT):
                    roots(0, u)
                    low_key(0, u)
                    scale_q(0, u)
                    bound_root(0, u)
                with pool.Fori(0, TURNS // 2) as i:
                    for r in range(2):
                        t = 2 * i + r
                        g = t % NG
                        pool.wait_ge(exp_ok, CREDIT + 32 * t)
                        nc.gpsimd.tensor_copy(keyb[:], tabs[:, bass.ds(g, 1), 0:HG * TT].rearrange("p a n -> p (a n)")).then_inc(tab_ok, 1)
                        load_turn(t + 1)
                        for slot in range((HG + 1) * TT):
                            for u in prep(slot, 1):
                                roots(t + 1, u)
                            for u in prep(slot, 6):
                                bound_root(t + 1, u)
                            for u in prep(slot, 3):
                                scale_q(t + 1, u)
                            for u in prep(slot, 4):
                                low_key(t + 1, u)

        XT = sb("XT", [P, NB * SEQ])
        gw0 = sb("gw0", [P, E0 * I0])
        uw0 = sb("uw0", [P, E0 * I0])
        dw0 = sb("dw0", [P, E0 * NK0, D])
        gw1 = sb("gw1", [P, NE1 * I1])
        uw1 = sb("uw1", [P, NE1 * I1])
        dw1 = sb("dw1", [P, NJ1, D])
        rw1 = sb("rw1", [P, E1])
        gb1 = sb("gb1", [P, E1])
        ob1 = sb("ob1", [P, D])
        sel0 = sb("sel0", [E0, E0, P], BF16)
        sel1 = sb("sel1", [3 * NE1, NJ1, P], BF16)
        mask0 = sb("mask0", [E0, TT, CH], BF16)
        comb1 = sb("comb1", [3 * NE1, TT, CH], BF16)
        xts = sb("xts", [P, CH])
        xm = sb("xm", [P, 2, CH])
        sg = sb("sg", [P, 2, CH])
        hid = sb("hid", [P, 2, CH])
        ys = sb("ys", [P, CH])
        ld2, ld3 = (ctx.enter_context(nc.semaphore(n)) for n in ("ld2", "ld3"))
        TOK = "p (b n) -> p b n"
        chunks = XT[:].rearrange("p (c n) -> p c n", c=TT)

        def xt(c):
            return chunks[:, bass.ds(c, 1), :].rearrange("p a n -> p (a n)")

        def first_of(dve, vals, top, eq, key, mkey, hot, s, n, rk, w):
            shape = [P, NB, w]
            nc.vector.tensor_reduce(top, vals, AX.X, ALU.max).then_inc(s[0], 1)
            dve.wait_ge(s[0], n + 1)
            nc.vector.tensor_tensor(eq, vals, top.unsqueeze(2).broadcast_to(shape), ALU.is_equal).then_inc(s[1], 1)
            dve.wait_ge(s[1], n + 1)
            nc.vector.tensor_tensor(key, eq, rk, ALU.mult).then_inc(s[2], 1)
            dve.wait_ge(s[2], n + 1)
            nc.vector.tensor_reduce(mkey, key, AX.X, ALU.max).then_inc(s[3], 1)
            dve.wait_ge(s[3], n + 1)
            nc.vector.tensor_tensor(hot, key, mkey.unsqueeze(2).broadcast_to(shape), ALU.is_equal).then_inc(s[4], 1)

        with ExitStack() as sc:
            def s2(name):
                return ctx.enter_context(nc.semaphore(name))

            lg = sb("lg", [P, NB, E0], F32, sc)
            eq = sb("eq0", [P, NB, E0], F32, sc)
            key = sb("key0", [P, NB, E0], F32, sc)
            top = sb("top0", [P, 2, NB], F32, sc)
            hot = sb("hot0", [P, NB, E0], BF16, sc)
            T = ps("T2", [P, NB, P], F32, sc)
            R = ps("R2", [P, NB, E0], F32, sc)
            MT = ps("MT2", [E0, CH], BF16, sc)
            pick = [s2(f"pick{i}") for i in range(5)]
            xt_mm, xt_ok, xts_ok, r_mm, r_ok, h_mm, h_ok, xk = (
                s2("xt_mm"), s2("xt_ok"), s2("xts_ok"), s2("r_mm"), s2("r_ok"), s2("h_mm"), s2("h_ok"), s2("xk"))
            block = sc.enter_context(nc.Block())

            @block.sync
            def _(sp):
                for dst, src in ((gw0, "gw0"), (uw0, "uw0"), (dw0, "dw0"), (sel0, "c_sel0")):
                    sp.dma_start(dst[:], a[src].bitcast(dst.dtype)).then_inc(ld2, 16)
                for dst, src in ((gw1, "gw1"), (uw1, "uw1"), (dw1, "dw1"), (rw1, "rw1"), (sel1, "c_sel1")):
                    sp.dma_start(dst[:], a[src].bitcast(dst.dtype)).then_inc(ld3, 16)
                sp.dma_start(gb1[:], a["gb1"].partition_broadcast(P)).then_inc(ld3, 16)
                sp.dma_start(ob1[:], a["ob1"].partition_broadcast(P)).then_inc(ld3, 16)
                sp.wait_ge(ld2, 64)
                sp.wait_ge(ld3, 112)

            @block.tensor
            def _(pe):
                credit(pe, h_mm, r_mm, xt_mm)
                with pe.Fori(0, TT) as c:
                    pe.wait_ge(norm.done, n1(c) + 1)
                    pe.wait_ge(xts_ok, CREDIT + c)
                    pe.wait_ge(xt_ok, CREDIT + c)
                    for b in range(NB):
                        last = nc.tensor.transpose(T[:, b, :], xn[:, b, :], idf[:])
                    last.then_inc(xt_mm, 1)
                    pe.wait_ge(xts_ok, CREDIT + c + 1)
                    pe.wait_ge(r_ok, CREDIT + c)
                    for b in range(NB):
                        last = nc.tensor.matmul(R[:, b, :], xts[:, b * P:(b + 1) * P], rw0[:], start=True, stop=True)
                    last.then_inc(r_mm, 1)
                    pe.wait_ge(pick[4], c + 1)
                    pe.wait_ge(h_ok, CREDIT + c)
                    for b in range(NB):
                        last = nc.tensor.transpose(MT[:, b * P:(b + 1) * P], hot[:, b, :], idb[:])
                    last.then_inc(h_mm, 1)

            @block.scalar
            def _(act):
                credit(act, h_ok, xt_ok, xts_ok)
                with act.Fori(0, TT) as c:
                    act.wait_ge(xt_mm, CREDIT + c + 1)
                    act.wait_ge(r_mm, CREDIT + c)
                    nc.scalar.copy(xts[:].rearrange(TOK, b=NB), T[:]).then_inc(xts_ok, 1)
                    nc.scalar.copy(xt(c).rearrange(TOK, b=NB), T[:]).then_inc(xt_ok, 1)
                    act.wait_ge(h_mm, CREDIT + c + 1)
                    nc.scalar.copy(mask0[:, bass.ds(c, 1), :].rearrange("p a n -> p (a n)"), MT[:]).then_inc(h_ok, 1)

            @block.vector
            def _(dve):
                credit(dve, r_ok, xk)
                with dve.Fori(0, TT) as c:
                    dve.wait_ge(xt_mm, CREDIT + c)
                    dve.wait_ge(xk, CREDIT + c)
                    norm.vector(dve, chunk(X, c), xn, n1(c))
                    dve.wait_ge(norm.done, n1(c) + 1)
                    hold(dve)
                    nc.vector.tensor_copy(chunk(X, c), xn[:]).then_inc(xk, 1)
                    dve.wait_ge(r_mm, CREDIT + c + 1)
                    nc.vector.tensor_copy(lg[:], R[:]).then_inc(r_ok, 1)
                    dve.wait_ge(r_ok, CREDIT + c + 1)
                    dve.wait_ge(h_mm, CREDIT + c)
                    first_of(dve, lg[:], top[:, 0, :], eq[:], key[:], top[:, 1, :], hot[:], pick, c,
                             rank[:, 0:NB * E0].rearrange("p (b e) -> p b e", b=NB), E0)

            @block.gpsimd
            def _(pool):
                with pool.Fori(0, TT) as c:
                    norm.pool(pool, n1(c))

        with ExitStack() as sc:
            def s3(name):
                return ctx.enter_context(nc.semaphore(name))

            NP = len(PAIRS)
            dif = sb("dif", [P, NP, D], F32, sc)
            sqd = sb("sqd", [P, NP, D], F32, sc)
            qv = sb("qv", [P, 2, NB, D], F32, sc)
            dist = sb("dist", [P, NP, H1], F32, sc)
            wp = sb("wp", [P, NP, H1], F32, sc)
            wf = sb("wf", [P, NB, NB, H1], F32, sc)
            prod = sb("prod", [P, 2, NB, D], F32, sc)
            den = sb("den", [P, 2, NB * H1], F32, sc)
            o1 = sb("o1", [P, NB, D], F32, sc)
            o1n = sb("o1n", [P, NB, D], F32, sc)
            ots1 = sb("ots1", [P, CH], F32, sc)
            x2 = sb("x2", [P, NB, D], F32, sc)
            y1 = sb("y1", [P, NB, D], F32, sc)
            y2 = sb("y2", [P, NB, D], F32, sc)
            sc1 = sb("sc1", [P, 4, NB, E1], F32, sc)
            eq = sb("eq1", [P, NB, E1], F32, sc)
            key = sb("key1", [P, NB, E1], F32, sc)
            top = sb("top1", [P, 6, NB], F32, sc)
            hot = sb("hot1", [P, 2, NB, E1], F32, sc)
            rest = sb("rest", [P, NB, E1], F32, sc)
            wt = sb("wt", [P, 3, NB, NE1], F32, sc)
            w3 = sb("w3", [P, NB, 3, NE1], BF16, sc)
            G = [ps(f"G3{i}", [P, CH], F32, sc) for i in range(2)]
            U = [ps(f"U3{i}", [P, CH], F32, sc) for i in range(2)]
            M = ps("M3", [P, CH], F32, sc)
            Y = ps("Y3", [P, CH], F32, sc)
            W = ps("W3", [P, 2, CH], F32, sc)
            T = W[:, 0, :].rearrange("p (b n) -> p b n", b=NB)
            Y1 = W[:, 1, :].rearrange("p (b n) -> p b n", b=NB)
            QV = W[:].rearrange("p k n -> p (k n)").rearrange("p (b n) -> p b n", b=NB)
            R = W[:, 1, 0:NB * E1].rearrange("p (b e) -> p b e", b=NB)
            C = W[0:3 * NE1, 0, 0:CH // 2].bitcast(BF16)
            m_mm, xm_ok, gu, silu, hid_ok, dn, ys_ok, y_t, x_ok = (
                s3("m_mm3"), s3("xm_ok3"), s3("gu3"), s3("silu3"), s3("hid_ok3"), s3("dn3"), s3("ys_ok3"),
                s3("y_t3"), s3("x_ok3"))
            pick1 = [s3(f"pick1{i}") for i in range(5)]
            pick2 = [s3(f"pick2{i}") for i in range(5)]
            init = s3("init4")
            (x2_mm, x2_ok, qv_mm, qv_ok, dif_ok, sqd_ok, dist_ok, wp_ok, wf_ok, pr_ok, o1_ok, den_ok, rden_ok,
             on_ok, o_mm, ots_ok, y_mm, yb_ok, x3_mm, x3s_ok, x3_ok, r_mm, lg_ok, ex_ok, ex1_ok, sig_ok,
             rest_ok, num_ok, rd_ok, w_ok, part_ok, w3_ok, c_mm, c_ok, xk2, yb_pre) = (
                s3(n + "4") for n in ("x2_mm x2_ok qv_mm qv_ok dif_ok sqd_ok dist_ok wp_ok wf_ok pr_ok o1_ok "
                "den_ok rden_ok on_ok o_mm ots_ok y_mm yb_ok x3_mm x3s_ok x3_ok r_mm lg_ok ex_ok ex1_ok "
                "sig_ok rest_ok num_ok rd_ok w_ok part_ok w3_ok c_mm c_ok xk2 yb_pre").split())
            NQ = E0 * NK0

            def back(c, n):
                return max(n, 0) if isinstance(c, int) and c == 0 else n

            block = sc.enter_context(nc.Block())

            @block.tensor
            def _(pe):
                credit(pe, c_mm, dn, gu, r_mm, x2_mm, y_mm, y_t)

                def spread(c, e):
                    pe.wait_ge(xm_ok, CREDIT + E0 * c + e)
                    hold(pe)
                    nc.tensor.matmul(M[:], sel0[:, e, :],
                                     mask0[:, bass.ds(c % TT, 1), :].rearrange("p a n -> p (a n)"),
                                     start=True, stop=True).then_inc(m_mm, 1)

                def gate_up(c, q):
                    e, (at, rows) = q // NK0, KB0[q % NK0]
                    if q % NK0 == 0:
                        pe.wait_ge(xm_ok, CREDIT + E0 * c + e + 1)
                    pe.wait_ge(hid_ok, CREDIT + NQ * c + back(c, q - 1))
                    for w, o in ((gw0, G), (uw0, U)):
                        last = nc.tensor.matmul(o[q % 2][0:rows, :], w[:, e * I0 + at:e * I0 + at + rows],
                                                xm[:, e % 2, :], start=True, stop=True)
                    last.then_inc(gu, 1)

                def down(c, q):
                    if q == 0:
                        pe.wait_ge(ys_ok, CREDIT + c)
                    pe.wait_ge(hid_ok, CREDIT + NQ * c + q + 1)
                    rows = KB0[q % NK0][1]
                    nc.tensor.matmul(Y[:], dw0[0:rows, q, :], hid[0:rows, q % 2, :], start=q == 0,
                                     stop=q == NQ - 1).then_inc(dn, 1)

                def experts(c, q):
                    gate_up(c, q)
                    if q % NK0 == 0:
                        if q // NK0 + 1 < E0:
                            spread(c, q // NK0 + 1)
                        else:
                            spread(c + 1, 0)
                    if q:
                        down(c, q - 1)

                def after(c, q):
                    if q == 0:
                        down(c, NQ - 1)
                    if q == 1:
                        pe.wait_ge(ys_ok, CREDIT + c + 1)
                        pe.wait_ge(c_ok, CREDIT + c)
                        for b in range(NB):
                            last = nc.tensor.transpose(T[:, b, :], ys[:, b * P:(b + 1) * P], idf[:])
                        last.then_inc(y_t, 1)
                    if q == 5:
                        pe.wait_ge(x_ok, CREDIT + c + 1)
                        pe.wait_ge(norm.done, n2(c) + 1)
                        hold(pe)
                        for b in range(NB):
                            last = nc.tensor.transpose(T[:, b, :], x2[:, b, :], idf[:])
                        last.then_inc(x2_mm, 1)
                    if q == 6:
                        pe.wait_ge(x2_ok, c + 1)
                        pe.wait_ge(lg_ok, CREDIT + c)
                        hold(pe)
                        for b in range(NB):
                            last = nc.tensor.matmul(QV[:, b, :], xts[:, b * P:(b + 1) * P],
                                                    w1q[:].rearrange("p a d -> p (a d)"), start=True, stop=True)
                        last.then_inc(qv_mm, 1)
                    if q == 14:
                        pe.wait_ge(on_ok, c + 1)
                        for b in range(NB):
                            last = nc.tensor.transpose(T[:, b, :], o1n[:, b, :], idf[:])
                        last.then_inc(o_mm, 1)
                    if q == 15:
                        pe.wait_ge(ots_ok, c + 1)
                        for b in range(NB):
                            last = nc.tensor.matmul(Y1[:, b, :], ots1[:, b * P:(b + 1) * P], ow1[:], start=True, stop=True)
                        last.then_inc(y_mm, 1)
                    if q == 18:
                        pe.wait_ge(norm.done, n3(c) + 1)
                        for b in range(NB):
                            last = nc.tensor.transpose(T[:, b, :], xn[:, b, :], idf[:])
                        last.then_inc(x3_mm, 1)
                    if q == 19:
                        pe.wait_ge(x3s_ok, c + 1)
                        pe.wait_ge(yb_ok, CREDIT + c + 1)
                        hold(pe)
                        for b in range(NB):
                            last = nc.tensor.matmul(R[:, b, :], xts[:, b * P:(b + 1) * P], rw1[:], start=True, stop=True)
                        last.then_inc(r_mm, 1)
                    if q == 23:
                        pe.wait_ge(w3_ok, 3 * c + 3)
                        pe.wait_ge(x3_ok, CREDIT + c + 1)
                        hold(pe)
                        for b in range(NB):
                            last = nc.tensor.transpose(C[:, b * P:(b + 1) * P],
                                                       w3[:, b, :, :].rearrange("p a e -> p (a e)"), idb[:])
                        last.then_inc(c_mm, 1)

                spread(0, 0)
                for q in range(NQ):
                    experts(0, q)
                with pe.Fori(0, TT - 1) as c:
                    for q in range(NQ):
                        if q:
                            experts(c + 1, q)
                        else:
                            gate_up(c + 1, 0)
                            spread(c + 1, 1)
                        after(c, q)
                for q in range(NQ):
                    after(TT - 1, q)

            @block.scalar
            def _(act):
                credit(act, c_ok, ex_ok, qv_ok, x3_ok, ys_ok)

                def experts(c, q):
                    rows = KB0[q % NK0][1]
                    act.wait_ge(gu, CREDIT + NQ * c + q + 1)
                    nc.scalar.activation(sg[0:rows, q % 2, :], G[q % 2][0:rows, :], ACT.Silu).then_inc(silu, 1)

                def after(c, q):
                    if q == 0:
                        act.wait_ge(dn, CREDIT + NQ * c + NQ)
                        act.wait_ge(y_t, CREDIT + c)
                        nc.scalar.copy(ys[:], Y[:]).then_inc(ys_ok, 1)
                    if q == 5:
                        act.wait_ge(x2_mm, CREDIT + c + 1)
                        act.wait_ge(r_mm, CREDIT + c)
                        nc.scalar.copy(xts[:].rearrange(TOK, b=NB), T).then_inc(x2_ok, 1)
                    if q == 7:
                        act.wait_ge(qv_mm, c + 1)
                        act.wait_ge(pr_ok, CREDIT + 4 * c)
                        act.wait_ge(dif_ok, CREDIT + c)
                        nc.scalar.copy(qv[:].rearrange("p a b d -> p b a d"),
                                       QV.rearrange("p b (a d) -> p b a d", a=2)).then_inc(qv_ok, 1)
                    if q == 8:
                        act.wait_ge(dif_ok, CREDIT + c + 1)
                        act.wait_ge(dist_ok, CREDIT + c)
                        nc.scalar.activation(sqd[:], dif[:], ACT.Square).then_inc(sqd_ok, 1)
                    if q == 9:
                        act.wait_ge(dist_ok, CREDIT + c + 1)
                        act.wait_ge(wf_ok, CREDIT + c)
                        nc.scalar.activation(wp[:], dist[:], ACT.Exp, scale=-(DH1 ** -0.5)).then_inc(wp_ok, 1)
                    if q == 14:
                        act.wait_ge(o_mm, c + 1)
                        act.wait_ge(y_mm, CREDIT + c)
                        nc.scalar.copy(ots1[:].rearrange(TOK, b=NB), T).then_inc(ots_ok, 1)
                    if q == 18:
                        act.wait_ge(x3_mm, c + 1)
                        act.wait_ge(qv_mm, c + 1)
                        nc.scalar.copy(xts[:].rearrange(TOK, b=NB), T).then_inc(x3s_ok, 1)
                        nc.scalar.copy(xt(c).rearrange(TOK, b=NB), T).then_inc(x3_ok, 1)
                    if q == 20:
                        act.wait_ge(lg_ok, CREDIT + c + 1)
                        act.wait_ge(ex1_ok, CREDIT + c)
                        nc.scalar.activation(sc1[:, 1], sc1[:, 0], ACT.Exp, scale=-1.0).then_inc(ex_ok, 1)
                    if q == 23:
                        act.wait_ge(c_mm, CREDIT + c + 1)
                        nc.scalar.copy(comb1[:, bass.ds(c, 1), :].rearrange("p a n -> p (a n)"), C).then_inc(c_ok, 1)

                for q in range(NQ):
                    experts(0, q)
                with act.Fori(0, TT - 1) as c:
                    for q in range(NQ):
                        experts(c + 1, q)
                        after(c, q)
                for q in range(NQ):
                    after(TT - 1, q)

            @block.vector
            def _(dve):
                credit(dve, hid_ok, x_ok, xm_ok, dif_ok, dist_ok, ex1_ok, lg_ok, pr_ok, wf_ok, xk2, yb_ok, yb_pre)

                def masked(c, e):
                    dve.wait_ge(m_mm, E0 * c + e + 1)
                    dve.wait_ge(gu, CREDIT + NQ * c + back(c, NK0 * (e - 1)))
                    nc.vector.tensor_tensor(xm[:, e % 2, :], xt(c % TT), M[:], ALU.mult).then_inc(xm_ok, 1)

                def experts(c, q):
                    if q % NK0 == 0:
                        if q // NK0 + 1 < E0:
                            masked(c, q // NK0 + 1)
                        else:
                            masked(c + 1, 0)
                    rows = KB0[q % NK0][1]
                    dve.wait_ge(silu, NQ * c + q + 1)
                    dve.wait_ge(dn, CREDIT + NQ * c + back(c, q - 1))
                    nc.vector.tensor_tensor(hid[0:rows, q % 2, :], sg[0:rows, q % 2, :], U[q % 2][0:rows, :],
                                            ALU.mult).then_inc(hid_ok, 1)

                def weigh(c, t):
                    nc.vector.tensor_tensor(
                        prod[:, t % 2].rearrange("p s (h d) -> p (s h) d", d=DH1),
                        qv[:, 1].rearrange("p s (h d) -> p (s h) d", d=DH1),
                        wf[:, t].rearrange("p s h -> p (s h)").unsqueeze(2).broadcast_to([P, NB * H1, DH1]),
                        ALU.mult).then_inc(pr_ok, 1)
                    dve.wait_ge(pr_ok, CREDIT + 4 * c + t + 1)
                    nc.vector.tensor_reduce(o1[:, t, :], prod[:, t % 2].rearrange("p s n -> p n s"), AX.X,
                                            ALU.add).then_inc(o1_ok, 1)

                def after(c, q):
                    rk = rank[:, NB * E0:].rearrange("p (b e) -> p b e", b=NB)
                    if q == 2:
                        dve.wait_ge(y_t, CREDIT + c + 1)
                        nc.vector.tensor_tensor(chunk(X, c), chunk(X, c), T, ALU.add).then_inc(x_ok, 1)
                        dve.wait_ge(x_ok, CREDIT + c + 1)
                        hold(dve)
                        norm.vector_stats(dve, chunk(X, c), n2(c))
                    if q == 3:
                        dve.wait_ge(yb_pre, CREDIT + c)
                        hold(dve)
                        norm.vector_apply(dve, chunk(X, c), x2, n2(c))
                    if q == 7:
                        dve.wait_ge(qv_ok, CREDIT + c + 1)
                        at = 0
                        for t in range(NB - 1):
                            n = NB - 1 - t
                            last = nc.vector.tensor_tensor(dif[:, at:at + n, :], qv[:, 0, t + 1:NB, :],
                                                           qv[:, 0, t:t + 1, :].broadcast_to([P, n, D]), ALU.subtract)
                            at += n
                        last.then_inc(dif_ok, 1)
                    if q == 8:
                        dve.wait_ge(sqd_ok, c + 1)
                        nc.vector.tensor_reduce(dist[:], sqd[:].rearrange("p a (h d) -> p (a h) d", d=DH1), AX.X,
                                                ALU.add).then_inc(dist_ok, 1)
                    if q == 10:
                        dve.wait_ge(wp_ok, c + 1)
                        for k, (t, s) in enumerate(PAIRS):
                            nc.vector.tensor_copy(wf[:, t, s, :], wp[:, k, :])
                            last = nc.vector.tensor_copy(wf[:, s, t, :], wp[:, k, :])
                        last.then_inc(wf_ok, 1)
                        dve.wait_ge(wf_ok, CREDIT + c + 1)
                        nc.vector.tensor_reduce(den[:, 0, :], wf[:].rearrange("p t s h -> p t h s"), AX.X,
                                                ALU.add).then_inc(den_ok, 1)
                        dve.wait_ge(den_ok, c + 1)
                        nc.vector.reciprocal(den[:, 1, :], den[:, 0, :]).then_inc(rden_ok, 1)
                    if q == 11:
                        weigh(c, 0)
                        weigh(c, 1)
                    if q == 12:
                        weigh(c, 2)
                        weigh(c, 3)
                        dve.wait_ge(o1_ok, 4 * c + 4)
                        dve.wait_ge(rden_ok, c + 1)
                        nc.vector.tensor_tensor(o1n[:].rearrange("p b (h d) -> p (b h) d", d=DH1),
                                                o1[:].rearrange("p b (h d) -> p (b h) d", d=DH1),
                                                den[:, 1, :].unsqueeze(2).broadcast_to([P, NB * H1, DH1]),
                                                ALU.mult).then_inc(on_ok, 1)
                    if q == 13:
                        dve.wait_ge(norm.done, n2(c) + 1)
                        nc.vector.tensor_tensor(y1[:], x2[:], ob1[:].unsqueeze(1).broadcast_to([P, NB, D]),
                                                ALU.add).then_inc(yb_pre, 1)
                    if q == 15:
                        dve.wait_ge(yb_pre, CREDIT + c + 1)
                        dve.wait_ge(y_mm, CREDIT + c + 1)
                        nc.vector.tensor_tensor(y2[:], Y1, y1[:], ALU.add).then_inc(yb_ok, 1)
                        dve.wait_ge(yb_ok, CREDIT + c + 1)
                        hold(dve)
                        norm.vector_stats(dve, y2, n3(c))
                    if q == 16:
                        dve.wait_ge(xk2, CREDIT + c)
                        hold(dve)
                        norm.vector_apply(dve, y2, xn, n3(c))
                        dve.wait_ge(norm.done, n3(c) + 1)
                        hold(dve)
                        nc.vector.tensor_copy(chunk(X, c), xn[:]).then_inc(xk2, 1)
                    if q == 19:
                        dve.wait_ge(r_mm, CREDIT + c + 1)
                        dve.wait_ge(ex_ok, CREDIT + c)
                        nc.vector.tensor_tensor(sc1[:, 0], R, gb1[:].unsqueeze(1).broadcast_to([P, NB, E1]),
                                                ALU.add).then_inc(lg_ok, 1)
                    if q == 21:
                        dve.wait_ge(ex_ok, CREDIT + c + 1)
                        nc.vector.tensor_scalar(sc1[:, 2], sc1[:, 1], 1.0, None, ALU.add).then_inc(ex1_ok, 1)
                        dve.wait_ge(ex1_ok, CREDIT + c + 1)
                        nc.vector.reciprocal(sc1[:, 3], sc1[:, 2]).then_inc(sig_ok, 1)
                        dve.wait_ge(sig_ok, c + 1)
                        first_of(dve, sc1[:, 3], top[:, 0, :], eq[:], key[:], top[:, 1, :], hot[:, 0], pick1, c, rk, E1)
                    if q == 22:
                        dve.wait_ge(pick1[4], c + 1)
                        nc.vector.scalar_tensor_tensor(rest[:], hot[:, 0], -4.0, sc1[:, 3], ALU.mult, ALU.add).then_inc(rest_ok, 1)
                        dve.wait_ge(rest_ok, c + 1)
                        first_of(dve, rest[:], top[:, 2, :], eq[:], key[:], top[:, 3, :], hot[:, 1], pick2, c, rk, E1)
                        dve.wait_ge(pick2[4], c + 1)
                        nc.vector.tensor_tensor(top[:, 4, :], top[:, 0, :], top[:, 2, :], ALU.add)
                        nc.vector.tensor_tensor(hot[:, 0], hot[:, 0], hot[:, 1], ALU.add).then_inc(num_ok, 1)
                        dve.wait_ge(num_ok, c + 1)
                        nc.vector.reciprocal(top[:, 5, :], top[:, 4, :])
                        nc.vector.tensor_tensor(rest[:], hot[:, 0], sc1[:, 3], ALU.mult).then_inc(rd_ok, 1)
                        dve.wait_ge(rd_ok, c + 1)
                        nc.vector.tensor_tensor(wt[:, 0, :, 0:E1], rest[:],
                                                top[:, 5, :].unsqueeze(2).broadcast_to([P, NB, E1]), ALU.mult).then_inc(w_ok, 1)
                        dve.wait_ge(w_ok, c + 1)
                        dve.wait_ge(c_mm, CREDIT + c)
                        for k in range(3):
                            nc.vector.tensor_copy(w3[:, :, k, :], wt[:, k]).then_inc(w3_ok, 1)
                            if k < 2:
                                dve.wait_ge(w3_ok, 3 * c + k + 1)
                                nc.vector.tensor_tensor(wt[:, k + 1], wt[:, k], w3[:, :, k, :], ALU.subtract).then_inc(part_ok, 1)
                                dve.wait_ge(part_ok, 2 * c + k + 1)

                nc.vector.memset(wf[:], 1.0)
                nc.vector.memset(wt[:], 0.0).then_inc(init, 1)
                dve.wait_ge(init, 1)
                nc.vector.memset(wt[:, 0, :, E1:NE1], 1.0).then_inc(init, 1)
                dve.wait_ge(init, 2)
                masked(0, 0)
                for q in range(NQ):
                    experts(0, q)
                with dve.Fori(0, TT - 1) as c:
                    for q in range(NQ):
                        experts(c + 1, q)
                        after(c, q)
                for q in range(NQ):
                    after(TT - 1, q)

            @block.gpsimd
            def _(pool):
                with pool.Fori(0, TT) as c:
                    norm.pool(pool, n2(c))
                    norm.pool(pool, n3(c))

        with ExitStack() as sc:
            def s5(name):
                return ctx.enter_context(nc.semaphore(name))

            G = [ps(f"G5{i}", [P, CH], F32, sc) for i in range(2)]
            U = [ps(f"U5{i}", [P, CH], F32, sc) for i in range(2)]
            M = [ps(f"M5{i}", [P, CH], F32, sc) for i in range(2)]
            Y = ps("Y5", [P, CH], F32, sc)
            T = ps("T5", [P, NB, P], F32, sc)
            m_mm, gu, silu, prod_ok, hid_ok, dn, ys_ok, y_t, x_ok, st_out = (
                s5("m_mm5"), s5("gu5"), s5("silu5"), s5("prod_ok5"), s5("hid_ok5"), s5("dn5"), s5("ys_ok5"),
                s5("y_t5"), s5("x_ok5"), s5("st_out"))
            raw = sb("raw", [P, 2, CH], F32, sc)
            xs = sb("xs", [P, NB, D], F32, sc)
            ROWS = [min(P, NE1 * I1 - P * j) for j in range(NJ1)]
            block = sc.enter_context(nc.Block())

            def before(c, j):
                return NJ1 * c + max(j - 1, 0)

            @block.sync
            def _(sp):
                with sp.Fori(0, TT) as c:
                    sp.wait_ge(norm.done, n4(c) + 1)
                    sp.dma_start(out[:, bass.ds(c, 1)].rearrange("p a b d -> p (a b) d"), chunk(X, c)).then_inc(st_out, 16)
                sp.wait_ge(st_out, 16 * TT)

            @block.tensor
            def _(pe):
                credit(pe, dn, y_t)
                def down(c, j):
                    if j == 0:
                        pe.wait_ge(ys_ok, CREDIT + c)
                    pe.wait_ge(hid_ok, CREDIT + NJ1 * c + j + 1)
                    nc.tensor.matmul(Y[:], dw1[0:ROWS[j], j, :], hid[0:ROWS[j], j % 2, :], start=j == 0,
                                     stop=j == NJ1 - 1).then_inc(dn, 1)

                with pe.Fori(0, TT) as c:
                    for j in range(NJ1):
                        n = ROWS[j]
                        pe.wait_ge(hid_ok, CREDIT + before(c, j))
                        hold(pe)
                        nc.tensor.matmul(M[j % 2][:], sel1[:, j, :],
                                         comb1[:, bass.ds(c, 1), :].rearrange("p a n -> p (a n)"),
                                         start=True, stop=True)
                        for w, o in ((gw1, G), (uw1, U)):
                            last = nc.tensor.matmul(o[j % 2][0:n, :], w[:, j * P:j * P + n], xt(c), start=True, stop=True)
                        last.then_inc(gu, 1)
                        if j:
                            down(c, j - 1)
                    down(c, NJ1 - 1)
                    pe.wait_ge(ys_ok, CREDIT + c + 1)
                    pe.wait_ge(x_ok, CREDIT + c)
                    for b in range(NB):
                        last = nc.tensor.transpose(T[:, b, :], ys[:, b * P:(b + 1) * P], idf[:])
                    last.then_inc(y_t, 1)

            @block.scalar
            def _(act):
                credit(act, ys_ok)
                with act.Fori(0, TT) as c:
                    for j in range(NJ1):
                        n = ROWS[j]
                        act.wait_ge(gu, NJ1 * c + j + 1)
                        act.wait_ge(prod_ok, CREDIT + before(c, j))
                        nc.scalar.activation(sg[0:n, j % 2, :], G[j % 2][0:n, :], ACT.Silu).then_inc(silu, 1)
                    act.wait_ge(dn, CREDIT + NJ1 * c + NJ1)
                    act.wait_ge(y_t, CREDIT + c)
                    nc.scalar.copy(ys[:], Y[:]).then_inc(ys_ok, 1)

            @block.vector
            def _(dve):
                credit(dve, hid_ok, prod_ok, x_ok)
                with dve.Fori(0, TT) as c:
                    for j in range(NJ1):
                        n = ROWS[j]
                        dve.wait_ge(silu, NJ1 * c + j + 1)
                        nc.vector.tensor_tensor(raw[0:n, j % 2, :], sg[0:n, j % 2, :], U[j % 2][0:n, :],
                                                ALU.mult).then_inc(prod_ok, 1)
                        dve.wait_ge(prod_ok, CREDIT + NJ1 * c + j + 1)
                        dve.wait_ge(dn, CREDIT + before(c, j))
                        nc.vector.tensor_tensor(hid[0:n, j % 2, :], raw[0:n, j % 2, :], M[j % 2][0:n, :],
                                                ALU.mult).then_inc(hid_ok, 1)
                    dve.wait_ge(y_t, CREDIT + c + 1)
                    nc.vector.scalar_tensor_tensor(xs[:], chunk(X, c), 2.0, T[:], ALU.mult, ALU.add).then_inc(x_ok, 1)
                    dve.wait_ge(x_ok, CREDIT + c + 1)
                    norm.vector(dve, xs, chunk(X, c), n4(c))

            @block.gpsimd
            def _(pool):
                with pool.Fori(0, TT) as c:
                    norm.pool(pool, n4(c))


def credit(engine, *signals):
    for signal in signals:
        engine.sem_inc(signal, CREDIT)


def hold(engine):
    engine.nop(nofuse=True)


def layout(x):
    f = lambda v: np.ascontiguousarray(v)
    nkv = x["L0_attn_null_kv"].reshape(H, NNULL, 2, DH)
    wq = x["L0_attn_w_q"].reshape(D, NG, KW)
    wkv = x["L0_attn_w_kv"].reshape(D, 2, NG, KW)
    down = x["L0_ffn_down_w"].transpose(0, 2, 1)
    dw0 = np.zeros((P, E0 * NK0, D), np.float32)
    for e in range(E0):
        for k, (at, rows) in enumerate(KB0):
            dw0[:rows, e * NK0 + k] = down[e, at:at + rows]
    both = lambda ew, sw: np.concatenate([ew, sw[None]], axis=0)
    gate = both(x["L1_ffn_experts_wg"], x["L1_ffn_shared_wg"]).transpose(1, 0, 2).reshape(D, NE1 * I1)
    up = both(x["L1_ffn_experts_wu"], x["L1_ffn_shared_wu"]).transpose(1, 0, 2).reshape(D, NE1 * I1)
    d1 = both(x["L1_ffn_experts_wd"], x["L1_ffn_shared_wd"]).reshape(NE1 * I1, D)
    dw1 = np.zeros((P, NJ1, D), np.float32)
    for j in range(NJ1):
        part = d1[j * P:(j + 1) * P]
        dw1[:part.shape[0], j] = part
    q1 = x["L1_attn_q_weight"].reshape(D, H1 * DH1)
    return {
        "x": f(x["L0_attn_x"].reshape(NB, TT, P, D).transpose(2, 1, 0, 3)),
        "gamma": f(x["L0_attn_gamma"].reshape(P, 1)),
        "q_scale": f(x["L0_attn_q_scale"]), "k_scale": f(x["L0_attn_k_scale"]),
        "null_k": f(nkv[:, :, 0].reshape(H * NNULL, DH)),
        "null_v": f(nkv[:, :, 1].reshape(NG, HG, NNULL, DH).transpose(0, 2, 1, 3)),
        "w_q_t": f(x["L0_attn_w_q"].reshape(D, H, DH).transpose(2, 1, 0).reshape(DH, H * P)),
        "w_qkv": f(np.concatenate([wq, wkv[:, 0], wkv[:, 1]], axis=2)),
        "w_out": f(x["L0_attn_w_out"].reshape(H * DH // P, P, D).transpose(1, 0, 2)),
        "rw0": f(x["L0_ffn_router_w"].T),
        "gw0": f(x["L0_ffn_gate_w"].transpose(2, 0, 1).reshape(D, E0 * I0)),
        "uw0": f(x["L0_ffn_up_w"].transpose(2, 0, 1).reshape(D, E0 * I0)),
        "dw0": dw0,
        "w1_q": f(q1), "w1_q_t": f(q1.T), "w1_v": f(x["L1_attn_v_weight"].reshape(D, H1 * DH1)),
        "w1_o": f(x["L1_attn_out_w"].T), "ob1": f(x["L1_attn_out_b"]),
        "rw1": f(x["L1_ffn_gate_w"]), "gb1": f(x["L1_ffn_gate_b"]),
        "gw1": f(gate), "uw1": f(up), "dw1": dw1,
    }


def kernel(**inputs):
    import concourse.bacc as _bacc
    from concourse import mybir as _mybir
    from concourse.bass_utils import run_bass_kernel_spmd as _run

    data = layout({k: np.asarray(v) for k, v in inputs.items()})
    data.update(constants())
    nc = _bacc.Bacc("TRN2", target_bir_lowering=False, num_devices=1)
    arrays, aps = {}, {}
    for name, arr in data.items():
        arrays[f"in_{name}"] = arr
        aps[name] = nc.dram_tensor(f"in_{name}", arr.shape, _mybir.dt.from_np(arr.dtype), kind="ExternalInput").ap()
    out = nc.dram_tensor("out", (P, TT, NB, D), F32, kind="ExternalOutput").ap()
    build(nc, aps, out)
    r = _run(nc, [arrays], core_ids=[0])
    return r.results[0]["out"].transpose(2, 1, 0, 3).reshape(NB, SEQ, D)
```

```python
from contextlib import ExitStack

import numpy as np

import concourse.bass as bass
from concourse import mybir

F32 = mybir.dt.float32
BF16 = mybir.dt.bfloat16
ALU = mybir.AluOpType
ACT = mybir.ActivationFunctionType
AX = mybir.AxisListType

P = 128
NB, SEQ, D = 4, 1024, 128
TT = SEQ // P
H, DH = 16, 64
NNULL = 2
HG = 4
NG = H // HG
TURNS = NB * NG
VW = DH + 1
SWQ, SWK = 3 * DH, 4 * DH
KW = HG * DH
CEN = SEQ // 2
LIFT = 40.0
EPS = 1e-5
CREDIT = 1
E0, I0 = 8, 352
E1, I1 = 16, 64
H1, DH1 = 16, 8
CH = NB * P
KB0 = [(k, min(P, I0 - k)) for k in range(0, I0, P)]
NK0 = len(KB0)
NJ1 = E1 // 2 + 1
NE1 = E1 + 1
PAIRS = [(t, s) for t in range(NB) for s in range(t + 1, NB)]
OFF = [sum(SEQ - P * i for i in range(j)) for j in range(TT + 1)]
TAB = HG * TT + TT * HG + HG * NNULL


def slopes():
    start = 2.0 ** (-2.0 ** (-(np.log2(H) - 3.0)))
    return np.array([start * start ** i for i in range(H)], dtype=np.float32).astype(np.float64)


def constants():
    sl = slopes()
    p = np.arange(P)[:, None, None]
    jt = np.arange(TT)
    key = sl[None, :, None] * (P * jt[None, None, :] + p - CEN)
    qry = LIFT - sl[None, None, :] * (P * jt[None, :, None] + p - CEN)
    nul = np.broadcast_to(sl[:, None] * (np.arange(NNULL)[None] - NNULL - CEN), (P, H, NNULL))
    tab = np.zeros((P, NG, TAB), np.float32)
    for g in range(NG):
        h = slice(g * HG, g * HG + HG)
        tab[:, g] = np.concatenate([key[:, h].reshape(P, -1), qry[:, :, h].reshape(P, -1),
                                    nul[:, h].reshape(P, -1)], axis=1)
    bits = lambda v: (np.asarray(v, np.float32).view(np.uint32) >> 16).astype(np.uint16)
    sel0 = np.zeros((E0, E0, P), np.float32)
    for e in range(E0):
        sel0[e, e] = 1
    sel1 = np.zeros((3, NE1, NJ1, P), np.float32)
    for e in range(NE1):
        sel1[:, e, e // 2, (e % 2) * I1:(e % 2) * I1 + I1] = 1
    blk = np.zeros((P, P), np.float32)
    for h in range(H1):
        blk[h * DH1:(h + 1) * DH1, h * DH1:(h + 1) * DH1] = DH1 ** -0.5
    rank = np.concatenate([np.tile(E0 - np.arange(E0), NB), np.tile(E1 - np.arange(E1), NB)])
    return {
        "c_tab": tab, "c_sel0": bits(sel0), "c_sel1": bits(sel1.reshape(3 * NE1, NJ1, P)),
        "c_blk": blk,
        "c_idf": np.eye(P, dtype=np.float32), "c_idb": bits(np.eye(P)),
        "c_future": bits(np.where(np.arange(P)[:, None] > np.arange(P)[None], -1e30, 0.0)),
        "c_rank": np.broadcast_to(rank.astype(np.float32), (P, rank.size)).copy(),
    }


def build(nc, a, out):
    ctx = ExitStack()
    with ctx:
        def sb(name, shape, dt=F32, scope=ctx):
            return scope.enter_context(nc.sbuf_tensor(name, shape, dt))

        def ps(name, shape, dt=F32, scope=ctx):
            return scope.enter_context(nc.psum_tensor(name, shape, dt))

        X = sb("X", [P, TT, NB, D])
        idf = sb("idf", [P, P])
        idb = sb("idb", [P, P], BF16)
        future = sb("future", [P, P], BF16)
        rank = sb("rank", [P, NB * (E0 + E1)])
        half = sb("half", [P, 2, 64])
        rw0 = sb("rw0", [P, E0])
        w1q = sb("w1q", [P, 2, D])
        ow1 = sb("ow1", [P, D])
        xn = sb("xn", [P, NB, D])

        def chunk(t, c):
            return t[:, bass.ds(c, 1), :, :].rearrange("p a b d -> p (a b) d")

        class Norm:

            def __init__(self, name):
                s = lambda n: ctx.enter_context(nc.semaphore(f"{name}_{n}"))
                self.stats, self.mean, self.var, self.root, self.done = (
                    s("stats"), s("mean"), s("var"), s("root"), s("done"))
                self.stat, self.mv = sb(f"{name}_stat", [P, NB, 6]), sb(f"{name}_mv", [P, NB, 2])
                self.vareps, self.rstd = sb(f"{name}_vareps", [P, NB]), sb(f"{name}_rstd", [P, NB])

            def vector_stats(self, dve, src, n):
                for b in range(NB):
                    last = nc.vector.bn_stats(self.stat[:, b, :], src[:, b, :])
                last.then_inc(self.stats, 1)
                dve.wait_ge(self.stats, n + 1)
                hold(dve)
                for b in range(NB):
                    last = nc.vector.bn_aggr(self.mv[:, b, :], self.stat[:, b, :])
                last.then_inc(self.mean, 1)
                dve.wait_ge(self.mean, n + 1)
                nc.vector.tensor_scalar(self.vareps[:], self.mv[:, :, 1], EPS, None, ALU.add).then_inc(self.var, 1)

            def vector_apply(self, dve, src, dst, n):
                dve.wait_ge(self.root, n + 1)
                for b in range(NB):
                    last = nc.vector.tensor_scalar(dst[:, b, :], src[:, b, :], self.mv[:, b, 0:1],
                                                   self.rstd[:, b:b + 1], ALU.subtract, ALU.mult)
                last.then_inc(self.done, 1)

            def vector(self, dve, src, dst, n):
                self.vector_stats(dve, src, n)
                self.vector_apply(dve, src, dst, n)

            def pool(self, pool, n):
                pool.wait_ge(self.var, n + 1)
                nc.gpsimd.tensor_tensor(self.rstd[:], self.vareps[:], half[:, 0, 0:NB], ALU.pow).then_inc(self.root, 1)

        norm = Norm("norm")
        norm1 = Norm("norm1")
        n1, n2, n3 = (lambda c: TT // 2 + c), (lambda c: TT // 2 + 2 * c), (lambda c: TT // 2 + 2 * c + 1)
        n4 = lambda c: TT // 2 + TT + c

        with ExitStack() as sc:
            def s1(name):
                return ctx.enter_context(nc.semaphore(name))

            wqkv = sb("wqkv", [P, NG, 3 * KW + HG * NNULL], F32, sc)
            wout = sb("wout", [P, H * DH // P, D], F32, sc)
            tabs = sb("tabs", [P, NG, TAB], F32, sc)
            nvb = sb("nvb", [P, NG, NNULL, HG, VW], F32, sc)
            scl = sb("scl", [P, DH], F32, sc)
            ksc = sb("ksc", [P, DH], F32, sc)
            w1qt = sb("w1qt", [P, D], F32, sc)
            w1v = sb("w1v", [P, D], F32, sc)
            w1m = sb("w1m", [P, D], F32, sc)
            blk = sb("blk", [P, D], F32, sc)
            nks = sb("nks", [H * NNULL, 3, DH], F32, sc)
            nkt = sb("nkt", [DH, H * NNULL], F32, sc)
            nkss = sb("nkss", [H * NNULL, 2], F32, sc)
            gam = sb("gam", [P, 1], F32, sc)
            xnt = nc.dram_tensor("xnt", (P, NB, TT, P), F32).ap()
            xnst = sb("xnst", [P, 2, NB, P], F32, sc)
            xns = sb("xns", [P, SEQ], F32, sc)
            keyb = sb("keyb", [P, HG * TT], F32, sc)
            qterm = sb("qterm", [P, TT * HG + HG * NNULL], F32, sc)
            nvc = sb("nvc", [P, TT, HG, VW], F32, sc)
            nvt = sb("nvt", [P, 2, HG, VW], F32, sc)
            Pw = sb("Pw", [P, 2, OFF[TT]], F32, sc)
            QT = sb("QT", [P, 2, HG, SEQ], BF16, sc)
            KT = sb("KT", [P, 2, HG, SEQ], BF16, sc)
            V = sb("V", [P, 2, TT, HG, VW], F32, sc)
            QS = sb("QS", [P, TT, HG, SWQ], BF16, sc)
            KS = sb("KS", [P, TT, HG, SWK], BF16, sc)
            kn = sb("kn", [P, HG, DH], F32, sc)
            qp = sb("qp", [P, HG, DH], F32, sc)
            ee = sb("ee", [P, 3, HG], F32, sc)
            qkraw = sb("qkraw", [P, 2 * KW], F32, sc)
            rawn = sb("rawn", [P, HG * NNULL], F32, sc)
            sq = sb("sq", [P, 2 * KW], F32, sc)
            sqq = sb("sqq", [P, KW], F32, sc)
            qn = sb("qn", [P, HG, DH], F32, sc)
            ss = sb("ss", [P, 2, 2 * HG], F32, sc)
            rn = sb("rn", [P, 2 * HG], F32, sc)
            bs = sb("bs", [P, HG], F32, sc)
            bn = sb("bn", [P, HG], F32, sc)
            nl = sb("nl", [P, TT, HG * NNULL], F32, sc)
            pn = sb("pn", [P, TT, HG * NNULL], F32, sc)
            oraw = sb("oraw", [P, 4, VW], F32, sc)
            rl = sb("rl", [P, 2, 4], F32, sc)
            OS = sb("OS", [P, TT, KW], F32, sc)
            ots = sb("ots", [P, 2, KW], F32, sc)

            S = [ps(f"S{i}", [P, SEQ], F32, sc) for i in range(2)]
            O = [ps(f"O{i}", [P, 4, P], F32, sc) for i in range(2)]
            A = [ps(f"A{i}", [P, 512], F32, sc) for i in range(2)]

            ld_xn, ld_x, ld_w, ld_c, ld_nv, ld_f = (
                s1("ld_xn"), s1("ld_x"), s1("ld_w"), s1("ld_c"), s1("ld_nv"), s1("ld_f"))
            consts = s1("consts")
            scale_ok, null_sq, null_ss, null_cl, null_rn, null_k = (
                s1("scale_ok"), s1("null_sq"), s1("null_ss"), s1("null_cl"), s1("null_rn"),
                s1("null_k"))
            st_xn, null_t, null_te, wnull_mm, wnull_ok = s1("st_xn"), s1("null_t"), s1("null_te"), s1("wnull_mm"), s1("wnull_ok")
            g_mm, g_ok, m_mm, m_ok = s1("g_mm"), s1("g_ok"), s1("m_mm"), s1("m_ok")
            xnt_mm, xnt_ok = s1("xnt_mm"), s1("xnt_ok")
            xns_ok = s1("xns_ok")
            proj = s1("proj")
            raw_ok, sq_ok, v_ok, ss_red, ss_ok, rn_ok = s1("raw_ok"), s1("sq_ok"), s1("v_ok"), s1("ss_red"), s1("ss_ok"), s1("rn_ok")
            kq_ok, qp_ok, sq2_ok, bs_ok, bn_ok = s1("kq_ok"), s1("qp_ok"), s1("sq2_ok"), s1("bs_ok"), s1("bn_ok")
            khi_ok, klo_ok, qhi_ok, qlo_ok = s1("khi_ok"), s1("klo_ok"), s1("qhi_ok"), s1("qlo_ok")
            e_ok, ep_ok, er_ok, nl_add, nl_ok = s1("e_ok"), s1("ep_ok"), s1("er_ok"), s1("nl_add"), s1("nl_ok")
            pn_ok = s1("pn_ok")
            tr, tq_ok, tk_ok = s1("tr"), s1("tq_ok"), s1("tk_ok")
            nvt_ok, nvu_ok = s1("nvt_ok"), s1("nvu_ok")
            tab_ok = s1("tab_ok")
            qk, exp_ok, pv = s1("qk"), s1("exp_ok"), s1("pv")
            or_ok, rl_ok, on = s1("or_ok"), s1("rl_ok"), s1("on")
            ctr, cot, cmm, cy = s1("ctr"), s1("cot"), s1("cmm"), s1("cy")

            PREP_AT = [0] + [5 + 4 * u for u in range(TT - 1)]
            NULL_AT = (2, 4, 4, 5, 7, 9, 9, 12)

            def prep(slot, lag):
                return [u for u in range(TT) if PREP_AT[u] + lag == slot]

            block = sc.enter_context(nc.Block())

            @block.sync
            def _(sp):
                credit(sp, st_xn)
                sp.dma_start(idf[:], a["c_idf"]).then_inc(ld_f, 16)
                sp.dma_start(gam[:], a["gamma"]).then_inc(ld_f, 16)
                for c in range(TT):
                    sp.dma_start(X[:, c], a["x"][:, c]).then_inc(ld_x, 16)
                for dst, src in ((idb, "c_idb"), (future, "c_future"), (rank, "c_rank"), (tabs, "c_tab")):
                    sp.dma_start(dst[:], a[src].bitcast(dst.dtype)).then_inc(ld_c, 16)
                sp.dma_start(scl[:], a["q_scale"].partition_broadcast(P)).then_inc(ld_c, 16)
                sp.dma_start(ksc[:], a["k_scale"].partition_broadcast(P)).then_inc(ld_c, 16)
                sp.dma_start(nks[:, 0, :], a["null_k"]).then_inc(ld_c, 16)
                sp.dma_start(Pw[0:DH, 0, 0:H * P], a["w_q_t"]).then_inc(ld_c, 16)
                sp.dma_start(wqkv[:, :, 0:3 * KW], a["w_qkv"]).then_inc(ld_w, 16)
                for g in range(NG):
                    for k in range(NNULL):
                        sp.dma_start(nvb[:, g, k, :, 0:DH], a["null_v"][g, k].partition_broadcast(P)).then_inc(ld_nv, 16)
                sp.dma_start(wout[:], a["w_out"]).then_inc(ld_w, 16)
                for dst, src in ((w1q[:, 0, :], "w1_q"), (ow1[:], "w1_o"), (rw0[:], "rw0"),
                                 (w1qt[:], "w1_q_t"), (w1v[:], "w1_v"), (blk[:], "c_blk")):
                    sp.dma_start(dst, a[src]).then_inc(ld_w, 16)
                with sp.Fori(0, TT // 2) as i:
                    for r in range(2):
                        c = 2 * i + r
                        sp.wait_ge(xnt_ok, CREDIT + c + 1)
                        sp.dma_start(xnt[:, :, bass.ds(c, 1), :].rearrange("p b a n -> p (b a) n"), xnst[:, r]).then_inc(st_xn, 16)
                sp.wait_ge(st_xn, CREDIT + 16 * TT)

                def load_x(n):
                    sp.wait_ge(proj, 8 * n)
                    sp.dma_start(xns[:].rearrange("p (c n) -> p c n", n=P),
                                 xnt[:, bass.ds((n // NG) % NB, 1)].rearrange("p a c n -> p (a c) n")).then_inc(ld_xn, 16)

                load_x(0)
                with sp.Fori(0, TURNS) as t:
                    load_x(t + 1)

            LDC, LDW, LDNV = 16 * 8, 16 * 8, 16 * NG * NNULL

            first = [norm, norm1]
            xns0 = [xn[:], Pw[:, 1, 0:CH].rearrange("p (b d) -> p b d", b=NB)]

            def bcast(ap, shape):
                return ap.broadcast_to(shape)

            @block.tensor
            def _(pe):
                credit(pe, cmm, ctr, pv, xnt_mm)
                def project(n, u):
                    g = n % NG
                    if u == 0:
                        pe.wait_ge(ld_xn, 16 * (n + 1))
                    pe.wait_ge(v_ok, 8 * n + u)
                    pe.wait_ge(raw_ok, 8 * n + u)
                    x = xns[:, u * P:(u + 1) * P]
                    w = wqkv[:, bass.ds(g, 1), :].rearrange("p a n -> p (a n)")
                    nc.tensor.matmul(A[0][:], x, w[:, 0:2 * KW], start=True, stop=True)
                    nc.tensor.matmul(A[1][:, 0:KW + HG * NNULL], x, w[:, 2 * KW:], start=True, stop=True).then_inc(proj, 1)

                def transposes(t, us):
                    for part in (khi_ok, klo_ok, qhi_ok, qlo_ok):
                        pe.wait_ge(part, 8 * t + 8)
                    pe.wait_ge(ep_ok, 24 * t + 24)
                    pe.wait_ge(exp_ok, CREDIT + 32 * t)
                    for u in us:
                        if u >= 2:
                            pe.wait_ge(tq_ok, 8 * t + u - 1)
                            pe.wait_ge(tk_ok, 8 * t + u - 1)
                        Sb = S[u % 2][:].bitcast(BF16).rearrange("p (k h n) -> p k h n", k=4, h=HG)
                        for h in range(HG):
                            nc.tensor.transpose(Sb[:, 0, h, :], QS[:, u, h, 0:P], idb[:])
                            nc.tensor.transpose(Sb[:, 1, h, :], QS[:, u, h, DH:DH + P], idb[:])
                        for h in range(HG):
                            nc.tensor.transpose(Sb[:, 2, h, :], KS[:, u, h, 0:P], idb[:])
                            last = nc.tensor.transpose(Sb[:, 3, h, :], KS[:, u, h, P:2 * P], idb[:])
                        last.then_inc(tr, 1)

                def scores(t, h, jt):
                    k = h * TT + jt
                    if k == 0:
                        pe.wait_ge(tq_ok, 8 * t + 8)
                        pe.wait_ge(tk_ok, 8 * t + 8)
                    if k >= 2:
                        pe.wait_ge(exp_ok, CREDIT + 32 * t + k - 1)
                    n = SEQ - P * jt
                    for c in range(0, n, 512):
                        w = min(512, n - c)
                        for k in range(2):
                            last = nc.tensor.matmul(S[jt % 2][:, c:c + w], KT[:, k, h, jt * P:(jt + 1) * P],
                                                    QT[:, k, h, jt * P + c:jt * P + c + w], start=k == 0,
                                                    stop=k == 1 and c > 0)
                        if c == 0:
                            last = nc.tensor.matmul(S[jt % 2][:, 0:P], idb[:], future[:], start=False, stop=True)
                    last.then_inc(qk, 1)

                def values(t, r, h, it):
                    if h == 0 and it == 0:
                        pe.wait_ge(v_ok, 8 * t + 8)
                    if it % 4 == 0:
                        if h:
                            pe.wait_ge(on, CREDIT + 8 * t + 2 * (h - 1) + it // 4 + 1)
                        else:
                            pe.wait_ge(cy, CREDIT + 2 * t)
                    pe.wait_ge(exp_ok, CREDIT + 32 * t + h * TT + it + 1)
                    o = O[it // 4][:, it % 4, 0:VW]
                    for jt in range(it + 1):
                        at = OFF[jt] + (it - jt) * P
                        last = nc.tensor.matmul(o, Pw[:, h % 2, at:at + P], V[:, r, jt, h, :],
                                                start=jt == 0, stop=jt == it)
                    last.then_inc(pv, 1)

                def project_out(t):
                    g = t % NG
                    pe.wait_ge(v_ok, 8 * t + 16)
                    pe.wait_ge(raw_ok, 8 * t + 16)
                    w = wout[:, bass.ds(g * 2, 2), :]
                    for it in range(TT + 1):
                        if it < TT:
                            transposes(t + 1, [it])
                            pe.wait_ge(on, CREDIT + 8 * t + 7 + it // 4)
                            if it >= 2:
                                pe.wait_ge(cot, CREDIT + 8 * t + it - 1)
                            for k in range(2):
                                last = nc.tensor.transpose(A[it % 2][:, k * P:(k + 1) * P],
                                                           OS[:, it, k * P:(k + 1) * P], idf[:])
                            last.then_inc(ctr, 1)
                        if it:
                            j = it - 1
                            if j % 4 == 0:
                                pe.wait_ge(on, CREDIT + 8 * t + 7 + j // 4)
                            pe.wait_ge(cot, CREDIT + 8 * t + j + 1)
                            for k in range(2):
                                last = nc.tensor.matmul(O[j // 4][:, j % 4, :], ots[:, j % 2, k * P:(k + 1) * P],
                                                        w[:, k, :], start=k == 0, stop=k == 1)
                            last.then_inc(cmm, 1)

                pe.wait_ge(ld_f, 32)
                with pe.Fori(0, TT // 2) as i:
                    for r in range(2):
                        c = 2 * i + r
                        pe.wait_ge(first[r].done, i + 1)
                        pe.wait_ge(xnt_ok, CREDIT + 2 * i)
                        for b in range(NB):
                            last = nc.tensor.transpose(S[r][:, b * P:(b + 1) * P], xns0[r][:, b, :], idf[:])
                        last.then_inc(xnt_mm, 1)

                pe.wait_ge(ld_c, LDC)
                pe.wait_ge(ld_w, LDW)
                pe.wait_ge(null_k, 1)
                nc.tensor.transpose(A[0][0:DH, 0:H * NNULL], nks[:, 2, :], idf[0:H * NNULL, 0:H * NNULL]).then_inc(null_t, 1)
                pe.wait_ge(null_te, 1)
                for h in range(H):
                    wt = Pw[0:DH, 0, h * P:(h + 1) * P]
                    last = nc.tensor.matmul(A[1][:, h * NNULL:(h + 1) * NNULL], wt,
                                            nkt[:, h * NNULL:(h + 1) * NNULL], start=True, stop=True)
                last.then_inc(wnull_mm, 1)
                nc.tensor.matmul(O[0][:, 0, :], w1q[:, 0, :], w1v[:], start=True, stop=True).then_inc(g_mm, 1)
                pe.wait_ge(g_ok, 1)
                nc.tensor.matmul(O[1][:, 0, :], w1qt[:], w1m[:], start=True, stop=True).then_inc(m_mm, 1)

                pe.wait_ge(wnull_ok, 1)
                pe.wait_ge(xnt_ok, CREDIT + TT)
                for u in range(TT):
                    project(0, u)
                transposes(0, range(TT))
                with pe.Fori(0, TURNS // 2) as i:
                    for r in range(2):
                        t = 2 * i + r
                        for slot in range((HG + 1) * TT):
                            h, s = slot // TT, slot % TT
                            if h < HG:
                                scores(t, h, s)
                            if h:
                                values(t, r, h - 1, s)
                            for u in prep(slot, 0):
                                if u == 0:
                                    pe.wait_ge(cot, CREDIT + 8 * t)
                                project(t + 1, u)
                        project_out(t)

            @block.scalar
            def _(act):
                credit(act, cot, exp_ok, xnt_ok)
                def products_out(n, u):
                    act.wait_ge(proj, 8 * n + u + 1)
                    act.wait_ge(kq_ok, 8 * n + u)
                    act.wait_ge(ss_red, 8 * n + u)
                    nc.scalar.copy(qkraw[:], A[0][:]).then_inc(raw_ok, 1)

                def high_key(n, u):
                    act.wait_ge(kq_ok, 8 * n + u + 1)
                    act.wait_ge(tr, 8 * n)
                    nc.scalar.copy(KS[:, u, :, 0:2 * DH].rearrange("p h (k d) -> p h k d", k=2),
                                   kn[:].unsqueeze(2).broadcast_to([P, HG, 2, DH])).then_inc(khi_ok, 1)

                def squares2(n, u):
                    act.wait_ge(qp_ok, 8 * n + u + 1)
                    act.wait_ge(bs_ok, 8 * n + u)
                    nc.scalar.copy(QS[:, u, :, DH:2 * DH], qp[:]).then_inc(qhi_ok, 1)
                    nc.scalar.activation(sqq[:].rearrange("p (h d) -> p h d", h=HG), qp[:],
                                         ACT.Square).then_inc(sq2_ok, 1)

                def queries_out(t, u):
                    act.wait_ge(tr, 8 * t + u + 1)
                    nc.scalar.copy(QT[:].rearrange("p k h n -> p (k h) n")[:, :, u * P:(u + 1) * P],
                                   S[u % 2][:, 0:512].bitcast(BF16).rearrange("p (k n) -> p k n", n=P)).then_inc(tq_ok, 1)

                def prepare(n, slot):
                    for u in prep(slot, 1):
                        products_out(n, u)
                    for u in prep(slot, 4):
                        high_key(n, u)
                    for u in prep(slot, 5):
                        squares2(n, u)

                def null_exp(n):
                    act.wait_ge(nl_ok, 8 * n + 8)
                    act.wait_ge(nvu_ok, 8 * n)
                    nc.scalar.activation(pn[:], nl[:], ACT.Exp).then_inc(pn_ok, 1)

                act.wait_ge(ld_f, 32)
                with act.Fori(0, TT // 2) as i:
                    for r in range(2):
                        c = 2 * i + r
                        act.wait_ge(xnt_mm, CREDIT + c + 1)
                        act.wait_ge(st_xn, CREDIT + 32 * i)
                        nc.scalar.activation(xnst[:, r], S[r][:, 0:CH].rearrange("p (b n) -> p b n", b=NB), ACT.Copy,
                                             scale=gam[:, 0:1]).then_inc(xnt_ok, 1)
                act.wait_ge(ld_c, LDC)
                act.wait_ge(null_t, 1)
                nc.scalar.copy(nkt[:], A[0][0:DH, 0:H * NNULL]).then_inc(null_te, 1)
                act.wait_ge(wnull_mm, 1)
                nc.scalar.copy(wqkv[:, :, 3 * KW:], A[1][:, 0:H * NNULL].rearrange("p (g n) -> p g n", g=NG)).then_inc(wnull_ok, 1)
                for slot in range((HG + 1) * TT):
                    prepare(0, slot)
                null_exp(0)
                for u in range(TT):
                    queries_out(0, u)
                with act.Fori(0, TURNS // 2) as i:
                    for r in range(2):
                        t = 2 * i + r
                        for slot in range((HG + 1) * TT):
                            h, jt = slot // TT, slot % TT
                            if h < HG:
                                if h == 0 and jt == 0:
                                    act.wait_ge(tab_ok, t + 1)
                                    act.wait_ge(pv, CREDIT + 32 * t)
                                if h >= 2 and jt == 0:
                                    act.wait_ge(pv, CREDIT + 32 * t + (h - 1) * TT)
                                act.wait_ge(qk, 32 * t + h * TT + jt + 1)
                                n = SEQ - P * jt
                                nc.scalar.activation(Pw[:, h % 2, OFF[jt]:OFF[jt] + n], S[jt % 2][:, 0:n], ACT.Exp,
                                                     bias=keyb[:, h * TT + jt:h * TT + jt + 1]).then_inc(exp_ok, 1)
                            prepare(t + 1, slot)
                        null_exp(t + 1)
                        for it in range(TT):
                            queries_out(t + 1, it)
                            act.wait_ge(ctr, CREDIT + 8 * t + it + 1)
                            act.wait_ge(cmm, CREDIT + 8 * t + max(it - 1, 0))
                            nc.scalar.copy(ots[:, it % 2, :], A[it % 2][:, 0:KW]).then_inc(cot, 1)

            @block.vector
            def _(dve):
                credit(dve, cy, on)
                def values_out(n, r, u):
                    dve.wait_ge(proj, 8 * n + u + 1)
                    dve.wait_ge(kq_ok, 8 * n + u)
                    if u == 0 and not isinstance(n, int):
                        dve.wait_ge(pv, CREDIT + 32 * (n - 1))
                    nc.vector.tensor_copy(rawn[:], A[1][:, KW:KW + HG * NNULL])
                    nc.vector.tensor_copy(V[:, r, u, :, 0:DH],
                                          A[1][:, 0:KW].rearrange("p (h d) -> p h d", h=HG)).then_inc(v_ok, 1)

                def sums(n, u):
                    dve.wait_ge(raw_ok, 8 * n + u + 1)
                    nc.vector.tensor_tensor(sq[:], qkraw[:], qkraw[:], ALU.mult).then_inc(sq_ok, 1)
                    dve.wait_ge(sq_ok, 8 * n + u + 1)
                    nc.vector.tensor_reduce(ss[:, 0, :], sq[:].rearrange("p (h d) -> p h d", d=DH), AX.X,
                                            ALU.add).then_inc(ss_red, 1)
                    dve.wait_ge(ss_red, 8 * n + u + 1)
                    nc.vector.tensor_scalar(ss[:, 1, :], ss[:, 0, :], 1e-24, None, ALU.max).then_inc(ss_ok, 1)

                def directions(n, u):
                    dve.wait_ge(rn_ok, 8 * n + u + 1)
                    dve.wait_ge(qp_ok, 8 * n + u)
                    dve.wait_ge(klo_ok, 8 * n + u)
                    if u == 0:
                        dve.wait_ge(pn_ok, n)
                    dve.wait_ge(v_ok, 8 * n + u + 1)
                    nc.vector.tensor_tensor(kn[:], qkraw[:, KW:2 * KW].rearrange("p (h d) -> p h d", h=HG),
                                            bcast(rn[:, HG:2 * HG].unsqueeze(2), [P, HG, DH]), ALU.mult)
                    nc.vector.tensor_tensor(nl[:, u, :].rearrange("p (h k) -> p h k", k=NNULL),
                                            rawn[:].rearrange("p (h k) -> p h k", k=NNULL),
                                            bcast(rn[:, 0:HG].unsqueeze(2), [P, HG, NNULL]), ALU.mult)
                    nc.vector.tensor_tensor(qn[:], qkraw[:, 0:KW].rearrange("p (h d) -> p h d", h=HG),
                                            bcast(rn[:, 0:HG].unsqueeze(2), [P, HG, DH]), ALU.mult).then_inc(kq_ok, 1)

                def bound(n, u):
                    dve.wait_ge(sq2_ok, 8 * n + u + 1)
                    dve.wait_ge(bn_ok, 8 * n + u)
                    nc.vector.tensor_reduce(bs[:], sqq[:].rearrange("p (h d) -> p h d", d=DH), AX.X,
                                            ALU.add).then_inc(bs_ok, 1)

                def low_query(n, u):
                    dve.wait_ge(qhi_ok, 8 * n + u + 1)
                    dve.wait_ge(tr, 8 * n)
                    nc.vector.tensor_tensor(QS[:, u, :, 0:DH], qp[:], QS[:, u, :, DH:2 * DH], ALU.subtract).then_inc(qlo_ok, 1)

                def guard(n, u):
                    dve.wait_ge(bn_ok, 8 * n + u + 1)
                    dve.wait_ge(kq_ok, 8 * n + u + 1)
                    nc.vector.tensor_tensor(ee[:, 0], qterm[:, u * HG:(u + 1) * HG], bn[:], ALU.subtract).then_inc(e_ok, 1)
                    dve.wait_ge(e_ok, 8 * n + u + 1)
                    x = nl[:, u, :].rearrange("p (h k) -> p h k", k=NNULL)
                    nc.vector.tensor_tensor(x, x, bcast(ee[:, 0].unsqueeze(2), [P, HG, NNULL]), ALU.add).then_inc(nl_add, 1)
                    for k in range(3):
                        part = QS[:, u, :, 2 * DH + k]
                        nc.vector.tensor_copy(part, ee[:, k]).then_inc(ep_ok, 1)
                        if k < 2:
                            dve.wait_ge(ep_ok, 24 * n + 3 * u + k + 1)
                            nc.vector.tensor_tensor(ee[:, k + 1], ee[:, k], part, ALU.subtract).then_inc(er_ok, 1)
                            dve.wait_ge(er_ok, 16 * n + 2 * u + k + 1)
                    dve.wait_ge(nl_add, 8 * n + u + 1)
                    nc.vector.tensor_tensor(nl[:, u, :], nl[:, u, :], qterm[:, TT * HG:], ALU.add).then_inc(nl_ok, 1)

                def prepare(n, r, slot):
                    for u in prep(slot, 1):
                        values_out(n, r, u)
                        sums(n, u)
                    for u in prep(slot, 6):
                        low_query(n, u)
                        bound(n, u)
                    for u in prep(slot, 3):
                        directions(n, u)
                    for u in prep(slot, 8):
                        guard(n, u)

                def head_out(t, h, half_):
                    dve.wait_ge(pv, CREDIT + 32 * t + h * TT + half_ * 4 + 4)
                    if h == 0:
                        dve.wait_ge(ctr, CREDIT + 8 * t)
                        dve.wait_ge(nvu_ok, 8 * t + half_ * 4 + 4)
                    k = 8 * t + h * 2 + half_
                    dve.wait_ge(on, CREDIT + k)
                    nc.vector.tensor_tensor(oraw[:], O[half_][:, :, 0:VW], nvc[:, half_ * 4:half_ * 4 + 4, h, :],
                                            ALU.add).then_inc(or_ok, 1)
                    dve.wait_ge(or_ok, k + 1)
                    nc.vector.reciprocal(rl[:, half_, :], oraw[:, :, DH]).then_inc(rl_ok, 1)
                    dve.wait_ge(rl_ok, k + 1)
                    nc.vector.tensor_tensor(OS[:, half_ * 4:half_ * 4 + 4, h * DH:(h + 1) * DH], oraw[:, :, 0:DH],
                                            bcast(rl[:, half_, :].unsqueeze(2), [P, 4, DH]), ALU.mult).then_inc(on, 1)

                def keys_out(t, u):
                    dve.wait_ge(tr, 8 * t + u + 1)
                    nc.vector.tensor_copy(KT[:].rearrange("p k h n -> p (k h) n")[:, :, u * P:(u + 1) * P],
                                          S[u % 2][:, 512:].bitcast(BF16).rearrange("p (k n) -> p k n", n=P)).then_inc(tk_ok, 1)

                def null_values(n, u):
                    if u == 0:
                        dve.wait_ge(pn_ok, n + 1)
                        dve.wait_ge(on, CREDIT + 8 * n)
                    w = pn[:, u, :].rearrange("p (h k) -> p h k", k=NNULL)
                    vals = nvb[:, bass.ds(n % NG, 1)].rearrange("p a k h d -> p (a k) h d")
                    nc.vector.tensor_tensor(nvc[:, u], bcast(w[:, :, 0:1], [P, HG, VW]), vals[:, 0], ALU.mult)
                    nc.vector.tensor_tensor(nvt[:, u % 2], bcast(w[:, :, 1:2], [P, HG, VW]), vals[:, 1],
                                            ALU.mult).then_inc(nvt_ok, 1)
                    dve.wait_ge(nvt_ok, 8 * n + u + 1)
                    nc.vector.tensor_tensor(nvc[:, u], nvc[:, u], nvt[:, u % 2], ALU.add).then_inc(nvu_ok, 1)

                nc.vector.memset(half[:, 0, :], -0.5)
                nc.vector.memset(half[:, 1, :], 0.5).then_inc(consts, 1)
                for r in range(2):
                    last = nc.vector.memset(V[:, r, :, :, DH:VW], 1.0)
                last.then_inc(consts, 1)
                nc.vector.memset(nvb[:, :, :, :, DH:VW], 1.0)
                nc.vector.memset(QS[:, :, :, 2 * DH:SWQ], 0.0)
                nc.vector.memset(KS[:, :, :, 3 * DH:SWK], 0.0).then_inc(consts, 1)
                dve.wait_ge(consts, 3)
                nc.vector.memset(KS[:, :, :, 3 * DH:3 * DH + 3], 1.0).then_inc(consts, 1)

                dve.wait_ge(ld_x, 16 * TT)
                with dve.Fori(0, TT // 2) as i:
                    for r in range(2):
                        first[r].vector_stats(dve, chunk(X, 2 * i + r), i)
                    dve.wait_ge(xnt_mm, CREDIT + 2 * i)
                    hold(dve)
                    for r in range(2):
                        first[r].vector_apply(dve, chunk(X, 2 * i + r), xns0[r], i)

                dve.wait_ge(ld_c, LDC)
                dve.wait_ge(ld_w, LDW)
                nc.vector.scalar_tensor_tensor(scl[:], scl[:], 8.0, ksc[:], ALU.mult, ALU.mult).then_inc(scale_ok, 1)
                nc.vector.tensor_tensor(nks[:, 1, :], nks[:, 0, :], nks[:, 0, :], ALU.mult).then_inc(null_sq, 1)
                dve.wait_ge(null_sq, 1)
                nc.vector.tensor_reduce(nkss[:, 0:1], nks[:, 1, :], AX.X, ALU.add).then_inc(null_ss, 1)
                dve.wait_ge(null_ss, 1)
                nc.vector.tensor_scalar(nkss[:, 0:1], nkss[:, 0:1], 1e-24, None, ALU.max).then_inc(null_cl, 1)
                dve.wait_ge(null_rn, 1)
                dve.wait_ge(scale_ok, 1)
                nc.vector.scalar_tensor_tensor(nks[:, 2, :], nks[:, 0, :], nkss[:, 1:2], scl[0:H * NNULL, :],
                                               ALU.mult, ALU.mult).then_inc(null_k, 1)
                dve.wait_ge(g_mm, 1)
                nc.vector.tensor_tensor(w1m[:], O[0][:, 0, :], blk[:], ALU.mult).then_inc(g_ok, 1)
                dve.wait_ge(m_mm, 1)
                nc.vector.tensor_copy(w1q[:, 1, :], O[1][:, 0, :]).then_inc(m_ok, 1)
                dve.wait_ge(consts, 4)
                dve.wait_ge(ld_nv, LDNV)
                for slot in range((HG + 1) * TT):
                    prepare(0, 0, slot)
                for u in range(TT):
                    keys_out(0, u)
                with dve.Fori(0, TURNS // 2) as i:
                    for r in range(2):
                        t = 2 * i + r
                        for slot in range((HG + 1) * TT):
                            h, s = slot // TT, slot % TT
                            if h and s % 4 == 3:
                                head_out(t, h - 1, s // 4)
                            prepare(t + 1, 1 - r, slot)
                            for u in range(TT):
                                if NULL_AT[u] == slot:
                                    null_values(t, u)
                        for u in range(TT):
                            keys_out(t + 1, u)
                        b = t // NG
                        for k in range(2):
                            dve.wait_ge(cmm, CREDIT + 8 * t + 4 * k + 4)
                            dve.wait_ge(cy, CREDIT + 2 * t)
                            x = X[:, 4 * k:4 * k + 4, bass.ds(b, 1), :].rearrange("p c a d -> p (c a) d")
                            nc.vector.tensor_tensor(x, x, O[k][:], ALU.add).then_inc(cy, 1)

            @block.gpsimd
            def _(pool):
                def load_turn(n):
                    pool.wait_ge(nl_ok, 8 * n)
                    g = n % NG
                    nc.gpsimd.tensor_copy(qterm[:], tabs[:, bass.ds(g, 1), HG * TT:].rearrange("p a n -> p (a n)")).then_inc(xns_ok, 1)

                def roots(n, u):
                    pool.wait_ge(ss_ok, 8 * n + u + 1)
                    pool.wait_ge(kq_ok, 8 * n + u)
                    nc.gpsimd.tensor_tensor(rn[:], ss[:, 1, :], half[:, 0, 0:2 * HG], ALU.pow).then_inc(rn_ok, 1)

                def low_key(n, u):
                    pool.wait_ge(khi_ok, 8 * n + u + 1)
                    nc.gpsimd.tensor_tensor(KS[:, u, :, 2 * DH:3 * DH], kn[:], KS[:, u, :, 0:DH], ALU.subtract).then_inc(klo_ok, 1)

                def scale_q(n, u):
                    pool.wait_ge(kq_ok, 8 * n + u + 1)
                    pool.wait_ge(qlo_ok, 8 * n + u)
                    nc.gpsimd.tensor_tensor(qp[:], qn[:], bcast(scl[:].unsqueeze(1), [P, HG, DH]),
                                            ALU.mult).then_inc(qp_ok, 1)

                def bound_root(n, u):
                    pool.wait_ge(bs_ok, 8 * n + u + 1)
                    pool.wait_ge(e_ok, 8 * n + u)
                    nc.gpsimd.tensor_tensor(bn[:], bs[:], half[:, 1, 0:HG], ALU.pow).then_inc(bn_ok, 1)

                def prepare(n, slot):
                    for u in prep(slot, 1):
                        roots(n, u)
                    for u in prep(slot, 6):
                        bound_root(n, u)
                    for u in prep(slot, 3):
                        scale_q(n, u)
                    for u in prep(slot, 4):
                        low_key(n, u)

                pool.wait_ge(consts, 1)
                with pool.Fori(0, TT // 2) as i:
                    for r in range(2):
                        first[r].pool(pool, i)
                pool.wait_ge(ld_c, LDC)
                pool.wait_ge(null_cl, 1)
                nc.gpsimd.tensor_tensor(nkss[:, 1:2], nkss[:, 0:1], half[0:H * NNULL, 0, 0:1], ALU.pow).then_inc(null_rn, 1)
                pool.wait_ge(xnt_ok, CREDIT + TT)
                pool.wait_ge(wnull_mm, 1)
                pool.wait_ge(scale_ok, 1)
                load_turn(0)
                for slot in range((HG + 1) * TT):
                    prepare(0, slot)
                with pool.Fori(0, TURNS // 2) as i:
                    for r in range(2):
                        t = 2 * i + r
                        g = t % NG
                        pool.wait_ge(exp_ok, CREDIT + 32 * t)
                        nc.gpsimd.tensor_copy(keyb[:], tabs[:, bass.ds(g, 1), 0:HG * TT].rearrange("p a n -> p (a n)")).then_inc(tab_ok, 1)
                        load_turn(t + 1)
                        for slot in range((HG + 1) * TT):
                            prepare(t + 1, slot)

        XT = sb("XT", [P, NB * SEQ])
        gw0 = sb("gw0", [P, E0 * I0])
        uw0 = sb("uw0", [P, E0 * I0])
        dw0 = sb("dw0", [P, E0 * NK0, D])
        gw1 = sb("gw1", [P, NE1 * I1])
        uw1 = sb("uw1", [P, NE1 * I1])
        dw1 = sb("dw1", [P, NJ1, D])
        rw1 = sb("rw1", [P, E1])
        gb1 = sb("gb1", [P, E1])
        ob1 = sb("ob1", [P, D])
        sel0 = sb("sel0", [E0, E0, P], BF16)
        sel1 = sb("sel1", [3 * NE1, NJ1, P], BF16)
        mask0 = sb("mask0", [E0, TT, CH], BF16)
        comb1 = sb("comb1", [3 * NE1, TT, CH], BF16)
        xts = sb("xts", [P, CH])
        xm = sb("xm", [P, 2, CH])
        sg = sb("sg", [P, 2, CH])
        hid = sb("hid", [P, 2, CH])
        ys = sb("ys", [P, CH])
        ld_gu, ld_d, ld3, ld4 = (ctx.enter_context(nc.semaphore(n)) for n in ("ld_gu", "ld_d", "ld3", "ld4"))
        TOK = "p (b n) -> p b n"
        chunks = XT[:].rearrange("p (c n) -> p c n", c=TT)

        def xt(c):
            return chunks[:, bass.ds(c, 1), :].rearrange("p a n -> p (a n)")

        def first_of(dve, vals, top, eq, key, mkey, hot, s, n, rk, w):
            shape = [P, NB, w]
            nc.vector.tensor_reduce(top, vals, AX.X, ALU.max).then_inc(s[0], 1)
            dve.wait_ge(s[0], n + 1)
            nc.vector.tensor_tensor(eq, vals, top.unsqueeze(2).broadcast_to(shape), ALU.is_equal).then_inc(s[1], 1)
            dve.wait_ge(s[1], n + 1)
            nc.vector.tensor_tensor(key, eq, rk, ALU.mult).then_inc(s[2], 1)
            dve.wait_ge(s[2], n + 1)
            nc.vector.tensor_reduce(mkey, key, AX.X, ALU.max).then_inc(s[3], 1)
            dve.wait_ge(s[3], n + 1)
            nc.vector.tensor_tensor(hot, key, mkey.unsqueeze(2).broadcast_to(shape), ALU.is_equal).then_inc(s[4], 1)

        with ExitStack() as sc:
            def s3(name):
                return ctx.enter_context(nc.semaphore(name))

            NP = len(PAIRS)
            dif = sb("dif", [P, NP, D], F32, sc)
            sqd = sb("sqd", [P, NP, D], F32, sc)
            qv = sb("qv", [P, 2, NB, D], F32, sc)
            dist = sb("dist", [P, NP, H1], F32, sc)
            wp = sb("wp", [P, NP, H1], F32, sc)
            wf = sb("wf", [P, NB, NB, H1], F32, sc)
            prod = sb("prod", [P, 2, NB, D], F32, sc)
            den = sb("den", [P, 2, NB * H1], F32, sc)
            o1 = sb("o1", [P, NB, D], F32, sc)
            o1n = sb("o1n", [P, NB, D], F32, sc)
            ots1 = sb("ots1", [P, CH], F32, sc)
            x2 = sb("x2", [P, NB, D], F32, sc)
            y1 = sb("y1", [P, NB, D], F32, sc)
            y2 = sb("y2", [P, NB, D], F32, sc)
            sc1 = sb("sc1", [P, 4, NB, E1], F32, sc)
            eq = sb("eq1", [P, NB, E1], F32, sc)
            key = sb("key1", [P, NB, E1], F32, sc)
            top = sb("top1", [P, 6, NB], F32, sc)
            hot = sb("hot1", [P, 2, NB, E1], F32, sc)
            rest = sb("rest", [P, NB, E1], F32, sc)
            wt = sb("wt", [P, 3, NB, NE1], F32, sc)
            w3 = sb("w3", [P, NB, 3, NE1], BF16, sc)
            lg = sb("lg", [P, NB, E0], F32, sc)
            eq0 = sb("eq0", [P, NB, E0], F32, sc)
            key0 = sb("key0", [P, NB, E0], F32, sc)
            top0 = sb("top0", [P, 2, NB], F32, sc)
            hot0 = sb("hot0", [P, NB, E0], BF16, sc)
            xn0 = sb("xn0", [P, NB, D], F32, sc)
            xts0 = sb("xts0", [P, CH], F32, sc)
            G = [ps(f"G3{i}", [P, CH], F32, sc) for i in range(2)]
            U = [ps(f"U3{i}", [P, CH], F32, sc) for i in range(2)]
            M = ps("M3", [P, CH], F32, sc)
            Y = ps("Y3", [P, CH], F32, sc)
            W = ps("W3", [P, 2, CH], F32, sc)
            T = W[:, 0, :].rearrange("p (b n) -> p b n", b=NB)
            Y1 = W[:, 1, :].rearrange("p (b n) -> p b n", b=NB)
            QV = W[:].rearrange("p k n -> p (k n)").rearrange("p (b n) -> p b n", b=NB)
            R = W[:, 1, 0:NB * E1].rearrange("p (b e) -> p b e", b=NB)
            C = W[0:3 * NE1, 0, 0:CH // 2].bitcast(BF16)
            R0 = W[:, 1, 0:NB * E0].rearrange("p (b e) -> p b e", b=NB)
            T5 = W[:, 1, :].rearrange("p (b n) -> p b n", b=NB)
            MT = W[0:E0, 0, 0:CH // 2].bitcast(BF16)
            pick = [s3(f"pick{i}") for i in range(5)]
            xt_mm, xt_ok, xts_ok, r0_mm, r0_ok, h_mm, h_ok, xk = (
                s3("xt_mm"), s3("xt_ok"), s3("xts_ok"), s3("r0_mm"), s3("r0_ok"), s3("h_mm"), s3("h_ok"), s3("xk"))
            m_mm, xm_ok, gu, silu, hid_ok, dn, ys_ok, y_t, x_ok = (
                s3("m_mm3"), s3("xm_ok3"), s3("gu3"), s3("silu3"), s3("hid_ok3"), s3("dn3"), s3("ys_ok3"),
                s3("y_t3"), s3("x_ok3"))
            pick1 = [s3(f"pick1{i}") for i in range(5)]
            pick2 = [s3(f"pick2{i}") for i in range(5)]
            init = s3("init4")
            (x2_mm, x2_ok, qv_mm, qv_ok, dif_ok, sqd_ok, dist_ok, wp_ok, wf_ok, pr_ok, o1_ok, den_ok, rden_ok,
             on_ok, o_mm, ots_ok, y_mm, yb_ok, x3_mm, x3s_ok, x3_ok, r_mm, lg_ok, ex_ok, ex1_ok, sig_ok,
             rest_ok, num_ok, rd_ok, w_ok, part_ok, w3_ok, c_mm, c_ok, xk2, yb_pre) = (
                s3(n + "4") for n in ("x2_mm x2_ok qv_mm qv_ok dif_ok sqd_ok dist_ok wp_ok wf_ok pr_ok o1_ok "
                "den_ok rden_ok on_ok o_mm ots_ok y_mm yb_ok x3_mm x3s_ok x3_ok r_mm lg_ok ex_ok ex1_ok "
                "sig_ok rest_ok num_ok rd_ok w_ok part_ok w3_ok c_mm c_ok xk2 yb_pre").split())
            NQ = E0 * NK0

            gu5, silu5, prod_ok, hid5_ok, dn5, ys5_ok, y5_t, x5_ok, st_out = (
                s3("gu5"), s3("silu5"), s3("prod_ok5"), s3("hid_ok5"), s3("dn5"), s3("ys_ok5"), s3("y_t5"),
                s3("x_ok5"), s3("st_out"))
            raw = sb("raw", [P, 2, CH], F32, sc)
            xs = sb("xs", [P, NB, D], F32, sc)
            ROWS = [min(P, NE1 * I1 - P * j) for j in range(NJ1)]
            BESIDE = 3
            assert BESIDE * NJ1 >= NQ

            def blocks(c, j):
                return NJ1 * c + max(j - 1, 0)

            def ahead(c):
                return min(c + 1, TT) if isinstance(c, int) else c + 1

            def back(c, n):
                return max(n, 0) if isinstance(c, int) and c == 0 else n

            block = sc.enter_context(nc.Block())

            @block.sync
            def _(sp):
                for dst, src in ((sel0, "c_sel0"), (gw0, "gw0"), (uw0, "uw0")):
                    sp.dma_start(dst[:], a[src].bitcast(dst.dtype)).then_inc(ld_gu, 16)
                sp.dma_start(dw0[:], a["dw0"]).then_inc(ld_d, 16)
                sp.dma_start(rw1[:], a["rw1"]).then_inc(ld3, 16)
                sp.dma_start(gb1[:], a["gb1"].partition_broadcast(P)).then_inc(ld3, 16)
                sp.dma_start(ob1[:], a["ob1"].partition_broadcast(P)).then_inc(ld3, 16)
                for dst, src in ((gw1, "gw1"), (uw1, "uw1"), (dw1, "dw1"), (sel1, "c_sel1")):
                    sp.dma_start(dst[:], a[src].bitcast(dst.dtype)).then_inc(ld4, 16)
                with sp.Fori(0, TT) as c:
                    sp.wait_ge(norm1.done, n4(c) + 1)
                    sp.dma_start(out[:, bass.ds(c, 1)].rearrange("p a b d -> p (a b) d"), chunk(X, c)).then_inc(st_out, 16)
                sp.wait_ge(st_out, 16 * TT)

            @block.tensor
            def _(pe):
                credit(pe, c_mm, dn, dn5, gu, h_mm, r_mm, r0_mm, x2_mm, xt_mm, y_mm, y_t, y5_t)

                def before(c, q):
                    if q == 11:
                        pe.wait_ge(norm1.done, n1(c) + 1)
                        pe.wait_ge(h_ok, CREDIT + c)
                        if not isinstance(c, int):
                            pe.wait_ge(qv_ok, CREDIT + c - 1)
                        for b in range(NB):
                            last = nc.tensor.transpose(T[:, b, :], xn0[:, b, :], idf[:])
                        last.then_inc(xt_mm, 1)
                    if q == 12:
                        pe.wait_ge(xts_ok, CREDIT + c + 1)
                        pe.wait_ge(r0_ok, CREDIT + c)
                        hold(pe)
                        for b in range(NB):
                            last = nc.tensor.matmul(R0[:, b, :], xts0[:, b * P:(b + 1) * P], rw0[:], start=True, stop=True)
                        last.then_inc(r0_mm, 1)
                    if q == 17:
                        pe.wait_ge(pick[4], c + 1)
                        pe.wait_ge(xt_ok, CREDIT + c + 1)
                        if not isinstance(c, int):
                            pe.wait_ge(ots_ok, c - 1)
                        hold(pe)
                        for b in range(NB):
                            last = nc.tensor.transpose(MT[:, b * P:(b + 1) * P], hot0[:, b, :], idb[:])
                        last.then_inc(h_mm, 1)

                def spread(c, e):
                    if e == 0:
                        pe.wait_ge(h_ok, CREDIT + ahead(c))
                    pe.wait_ge(xm_ok, CREDIT + E0 * c + e)
                    hold(pe)
                    nc.tensor.matmul(M[:], sel0[:, e, :],
                                     mask0[:, bass.ds(c % TT, 1), :].rearrange("p a n -> p (a n)"),
                                     start=True, stop=True).then_inc(m_mm, 1)

                def gate_up(c, q):
                    e, (at, rows) = q // NK0, KB0[q % NK0]
                    if q % NK0 == 0:
                        pe.wait_ge(xm_ok, CREDIT + E0 * c + e + 1)
                    pe.wait_ge(hid_ok, CREDIT + NQ * c + back(c, q - 1))
                    for w, o in ((gw0, G), (uw0, U)):
                        last = nc.tensor.matmul(o[q % 2][0:rows, :], w[:, e * I0 + at:e * I0 + at + rows],
                                                xm[:, e % 2, :], start=True, stop=True)
                    last.then_inc(gu, 1)

                def down(c, q):
                    if q == 0:
                        pe.wait_ge(ys_ok, CREDIT + c)
                    pe.wait_ge(hid_ok, CREDIT + NQ * c + q + 1)
                    rows = KB0[q % NK0][1]
                    nc.tensor.matmul(Y[:], dw0[0:rows, q, :], hid[0:rows, q % 2, :], start=q == 0,
                                     stop=q == NQ - 1).then_inc(dn, 1)

                def experts(c, q):
                    gate_up(c, q)
                    if q % NK0 == 0:
                        if q // NK0 + 1 < E0:
                            spread(c, q // NK0 + 1)
                        else:
                            spread(c + 1, 0)
                    if q:
                        down(c, q - 1)

                def after(c, q):
                    if q == 0:
                        down(c, NQ - 1)
                    if q == 1:
                        pe.wait_ge(ys_ok, CREDIT + c + 1)
                        pe.wait_ge(c_ok, CREDIT + c)
                        pe.wait_ge(h_ok, CREDIT + ahead(c + 1))
                        hold(pe)
                        for b in range(NB):
                            last = nc.tensor.transpose(T[:, b, :], ys[:, b * P:(b + 1) * P], idf[:])
                        last.then_inc(y_t, 1)
                    if q == 5:
                        pe.wait_ge(x_ok, CREDIT + c + 1)
                        pe.wait_ge(norm.done, n2(c) + 1)
                        hold(pe)
                        for b in range(NB):
                            last = nc.tensor.transpose(T[:, b, :], x2[:, b, :], idf[:])
                        last.then_inc(x2_mm, 1)
                    if q == 6:
                        pe.wait_ge(x2_ok, c + 1)
                        pe.wait_ge(lg_ok, CREDIT + c)
                        pe.wait_ge(r0_ok, CREDIT + ahead(c + 1))
                        hold(pe)
                        for b in range(NB):
                            last = nc.tensor.matmul(QV[:, b, :], xts[:, b * P:(b + 1) * P],
                                                    w1q[:].rearrange("p a d -> p (a d)"), start=True, stop=True)
                        last.then_inc(qv_mm, 1)
                    if q == 14:
                        pe.wait_ge(on_ok, c + 1)
                        pe.wait_ge(xt_ok, CREDIT + ahead(c + 2))
                        hold(pe)
                        for b in range(NB):
                            last = nc.tensor.transpose(T[:, b, :], o1n[:, b, :], idf[:])
                        last.then_inc(o_mm, 1)
                    if q == 15:
                        pe.wait_ge(ots_ok, c + 1)
                        pe.wait_ge(r0_ok, CREDIT + ahead(c + 2))
                        if isinstance(c, int) and c == TT - 1:
                            pe.wait_ge(x5_ok, CREDIT + 15 // NJ1)
                        hold(pe)
                        for b in range(NB):
                            last = nc.tensor.matmul(Y1[:, b, :], ots1[:, b * P:(b + 1) * P], ow1[:], start=True, stop=True)
                        last.then_inc(y_mm, 1)
                    if q == 18:
                        pe.wait_ge(norm.done, n3(c) + 1)
                        pe.wait_ge(h_ok, CREDIT + ahead(c + 2))
                        hold(pe)
                        for b in range(NB):
                            last = nc.tensor.transpose(T[:, b, :], xn[:, b, :], idf[:])
                        last.then_inc(x3_mm, 1)
                    if q == 19:
                        pe.wait_ge(x3s_ok, c + 1)
                        pe.wait_ge(yb_ok, CREDIT + c + 1)
                        if isinstance(c, int) and c == TT - 1:
                            pe.wait_ge(x5_ok, CREDIT + 19 // NJ1)
                        hold(pe)
                        for b in range(NB):
                            last = nc.tensor.matmul(R[:, b, :], xts[:, b * P:(b + 1) * P], rw1[:], start=True, stop=True)
                        last.then_inc(r_mm, 1)
                    if q == 23:
                        pe.wait_ge(w3_ok, 3 * c + 3)
                        pe.wait_ge(x3_ok, CREDIT + c + 1)
                        hold(pe)
                        for b in range(NB):
                            last = nc.tensor.transpose(C[:, b * P:(b + 1) * P],
                                                       w3[:, b, :, :].rearrange("p a e -> p (a e)"), idb[:])
                        last.then_inc(c_mm, 1)

                def second_down(c, j):
                    if j == 0:
                        pe.wait_ge(ys5_ok, CREDIT + c)
                        pe.wait_ge(ys_ok, CREDIT + TT)
                    pe.wait_ge(hid5_ok, CREDIT + NJ1 * c + j + 1)
                    nc.tensor.matmul(Y[:], dw1[0:ROWS[j], j, :], hid[0:ROWS[j], j % 2, :], start=j == 0,
                                     stop=j == NJ1 - 1).then_inc(dn5, 1)

                def second(c, j):
                    n = ROWS[j]
                    if j == 0:
                        pe.wait_ge(x3_ok, CREDIT + c + 1)
                        pe.wait_ge(hid_ok, CREDIT + NQ * TT)
                        pe.wait_ge(xm_ok, CREDIT + E0 * TT + 1)
                    pe.wait_ge(hid5_ok, CREDIT + blocks(c, j))
                    hold(pe)
                    for w, o in ((gw1, G), (uw1, U)):
                        last = nc.tensor.matmul(o[j % 2][0:n, :], w[:, j * P:j * P + n], xt(c), start=True, stop=True)
                    last.then_inc(gu5, 1)
                    if j:
                        second_down(c, j - 1)
                    if j == 0:
                        pe.wait_ge(c_ok, CREDIT + c + 1)
                        hold(pe)
                    nc.tensor.matmul(M[:], sel1[:, j, :], comb1[:, bass.ds(c, 1), :].rearrange("p a n -> p (a n)"),
                                     start=True, stop=True).then_inc(m_mm, 1)

                def second_end(c):
                    second_down(c, NJ1 - 1)
                    pe.wait_ge(ys5_ok, CREDIT + c + 1)
                    pe.wait_ge(x5_ok, CREDIT + c)
                    if isinstance(c, int):
                        pe.wait_ge((qv_ok, yb_ok, lg_ok)[c], CREDIT + TT)
                    for b in range(NB):
                        last = nc.tensor.transpose(T5[:, b, :], ys[:, b * P:(b + 1) * P], idf[:])
                    last.then_inc(y5_t, 1)

                for q in range(NQ):
                    before(0, q)
                pe.wait_ge(ld_gu, 48)
                spread(0, 0)
                for q in range(NQ):
                    if q == 1:
                        pe.wait_ge(ld_d, 16)
                    experts(0, q)
                    before(1, q)
                pe.wait_ge(ld3, 48)
                with pe.Fori(0, TT - 2) as c:
                    for q in range(NQ):
                        experts(c + 1, q)
                        after(c, q)
                        before(c + 2, q)
                for q in range(NQ):
                    experts(TT - 1, q)
                    after(TT - 2, q)
                pe.wait_ge(ld4, 64)
                for c in range(BESIDE):
                    for j in range(NJ1):
                        second(c, j)
                        after(TT - 1, c * NJ1 + j)
                    second_end(c)
                with pe.Fori(BESIDE, TT) as c:
                    for j in range(NJ1):
                        second(c, j)
                    second_end(c)

            @block.scalar
            def _(act):
                credit(act, c_ok, ex_ok, h_ok, qv_ok, x3_ok, xt_ok, xts_ok, ys_ok, ys5_ok)

                def before(c, q):
                    if q == 11:
                        act.wait_ge(xt_mm, CREDIT + c + 1)
                        act.wait_ge(r0_mm, CREDIT + c)
                        nc.scalar.copy(xts0[:].rearrange(TOK, b=NB), T).then_inc(xts_ok, 1)
                        nc.scalar.copy(xt(c).rearrange(TOK, b=NB), T).then_inc(xt_ok, 1)
                    if q == 17:
                        act.wait_ge(h_mm, CREDIT + c + 1)
                        nc.scalar.copy(mask0[:, bass.ds(c, 1), :].rearrange("p a n -> p (a n)"), MT).then_inc(h_ok, 1)

                def experts(c, q):
                    rows = KB0[q % NK0][1]
                    act.wait_ge(gu, CREDIT + NQ * c + q + 1)
                    nc.scalar.activation(sg[0:rows, q % 2, :], G[q % 2][0:rows, :], ACT.Silu).then_inc(silu, 1)

                def after(c, q):
                    if q == 0:
                        act.wait_ge(dn, CREDIT + NQ * c + NQ)
                        act.wait_ge(y_t, CREDIT + c)
                        nc.scalar.copy(ys[:], Y[:]).then_inc(ys_ok, 1)
                    if q == 5:
                        act.wait_ge(x2_mm, CREDIT + c + 1)
                        act.wait_ge(r_mm, CREDIT + c)
                        nc.scalar.copy(xts[:].rearrange(TOK, b=NB), T).then_inc(x2_ok, 1)
                    if q == 7:
                        act.wait_ge(qv_mm, c + 1)
                        act.wait_ge(pr_ok, CREDIT + 4 * c)
                        act.wait_ge(dif_ok, CREDIT + c)
                        nc.scalar.copy(qv[:].rearrange("p a b d -> p b a d"),
                                       QV.rearrange("p b (a d) -> p b a d", a=2)).then_inc(qv_ok, 1)
                    if q == 8:
                        act.wait_ge(dif_ok, CREDIT + c + 1)
                        act.wait_ge(dist_ok, CREDIT + c)
                        nc.scalar.activation(sqd[:], dif[:], ACT.Square).then_inc(sqd_ok, 1)
                    if q == 9:
                        act.wait_ge(dist_ok, CREDIT + c + 1)
                        act.wait_ge(wf_ok, CREDIT + c)
                        nc.scalar.activation(wp[:], dist[:], ACT.Exp, scale=-(DH1 ** -0.5)).then_inc(wp_ok, 1)
                    if q == 14:
                        act.wait_ge(o_mm, c + 1)
                        act.wait_ge(y_mm, CREDIT + c)
                        nc.scalar.copy(ots1[:].rearrange(TOK, b=NB), T).then_inc(ots_ok, 1)
                    if q == 18:
                        act.wait_ge(x3_mm, c + 1)
                        act.wait_ge(qv_mm, c + 1)
                        nc.scalar.copy(xts[:].rearrange(TOK, b=NB), T).then_inc(x3s_ok, 1)
                        nc.scalar.copy(xt(c).rearrange(TOK, b=NB), T).then_inc(x3_ok, 1)
                    if q == 20:
                        act.wait_ge(lg_ok, CREDIT + c + 1)
                        act.wait_ge(ex1_ok, CREDIT + c)
                        nc.scalar.activation(sc1[:, 1], sc1[:, 0], ACT.Exp, scale=-1.0).then_inc(ex_ok, 1)
                    if q == 23:
                        act.wait_ge(c_mm, CREDIT + c + 1)
                        nc.scalar.copy(comb1[:, bass.ds(c, 1), :].rearrange("p a n -> p (a n)"), C).then_inc(c_ok, 1)

                def second(c, j):
                    n = ROWS[j]
                    act.wait_ge(gu5, NJ1 * c + j + 1)
                    act.wait_ge(prod_ok, CREDIT + blocks(c, j))
                    nc.scalar.activation(sg[0:n, j % 2, :], G[j % 2][0:n, :], ACT.Silu).then_inc(silu5, 1)

                def second_end(c):
                    act.wait_ge(dn5, CREDIT + NJ1 * c + NJ1)
                    act.wait_ge(y5_t, CREDIT + c)
                    act.wait_ge(y_t, CREDIT + TT)
                    nc.scalar.copy(ys[:], Y[:]).then_inc(ys5_ok, 1)

                for q in range(NQ):
                    before(0, q)
                for q in range(NQ):
                    experts(0, q)
                    before(1, q)
                with act.Fori(0, TT - 2) as c:
                    for q in range(NQ):
                        experts(c + 1, q)
                        after(c, q)
                        before(c + 2, q)
                for q in range(NQ):
                    experts(TT - 1, q)
                    after(TT - 2, q)
                for c in range(BESIDE):
                    for j in range(NJ1):
                        second(c, j)
                        after(TT - 1, c * NJ1 + j)
                    second_end(c)
                with act.Fori(BESIDE, TT) as c:
                    for j in range(NJ1):
                        second(c, j)
                    second_end(c)

            @block.vector
            def _(dve):
                credit(dve, hid_ok, x_ok, xm_ok, dif_ok, dist_ok, ex1_ok, lg_ok, pr_ok, r0_ok, wf_ok, xk, xk2, yb_ok,
                       yb_pre, hid5_ok, prod_ok, x5_ok)

                def before(c, q):
                    if q == 8:
                        norm1.vector_stats(dve, chunk(X, c), n1(c))
                    if q == 9:
                        dve.wait_ge(xt_mm, CREDIT + c)
                        dve.wait_ge(xk, CREDIT + c)
                        hold(dve)
                        norm1.vector_apply(dve, chunk(X, c), xn0, n1(c))
                        dve.wait_ge(norm1.done, n1(c) + 1)
                        hold(dve)
                        nc.vector.tensor_copy(chunk(X, c), xn0[:]).then_inc(xk, 1)
                    if q == 13:
                        dve.wait_ge(r0_mm, CREDIT + c + 1)
                        nc.vector.tensor_copy(lg[:], R0).then_inc(r0_ok, 1)
                        dve.wait_ge(r0_ok, CREDIT + c + 1)
                        dve.wait_ge(h_mm, CREDIT + c)
                        first_of(dve, lg[:], top0[:, 0, :], eq0[:], key0[:], top0[:, 1, :], hot0[:], pick, c,
                                 rank[:, 0:NB * E0].rearrange("p (b e) -> p b e", b=NB), E0)

                def masked(c, e):
                    dve.wait_ge(m_mm, E0 * c + e + 1)
                    dve.wait_ge(xt_ok, CREDIT + ahead(c))
                    dve.wait_ge(gu, CREDIT + NQ * c + back(c, NK0 * (e - 1)))
                    nc.vector.tensor_tensor(xm[:, e % 2, :], xt(c % TT), M[:], ALU.mult).then_inc(xm_ok, 1)

                def experts(c, q):
                    if q % NK0 == 0:
                        if q // NK0 + 1 < E0:
                            masked(c, q // NK0 + 1)
                        else:
                            masked(c + 1, 0)
                    rows = KB0[q % NK0][1]
                    dve.wait_ge(silu, NQ * c + q + 1)
                    dve.wait_ge(dn, CREDIT + NQ * c + back(c, q - 1))
                    nc.vector.tensor_tensor(hid[0:rows, q % 2, :], sg[0:rows, q % 2, :], U[q % 2][0:rows, :],
                                            ALU.mult).then_inc(hid_ok, 1)

                def weigh(c, t):
                    nc.vector.tensor_tensor(
                        prod[:, t % 2].rearrange("p s (h d) -> p (s h) d", d=DH1),
                        qv[:, 1].rearrange("p s (h d) -> p (s h) d", d=DH1),
                        wf[:, t].rearrange("p s h -> p (s h)").unsqueeze(2).broadcast_to([P, NB * H1, DH1]),
                        ALU.mult).then_inc(pr_ok, 1)
                    dve.wait_ge(pr_ok, CREDIT + 4 * c + t + 1)
                    nc.vector.tensor_reduce(o1[:, t, :], prod[:, t % 2].rearrange("p s n -> p n s"), AX.X,
                                            ALU.add).then_inc(o1_ok, 1)

                def after(c, q):
                    rk = rank[:, NB * E0:].rearrange("p (b e) -> p b e", b=NB)
                    if q == 2:
                        dve.wait_ge(y_t, CREDIT + c + 1)
                        dve.wait_ge(xk, CREDIT + c + 1)
                        hold(dve)
                        nc.vector.tensor_tensor(chunk(X, c), chunk(X, c), T, ALU.add).then_inc(x_ok, 1)
                        dve.wait_ge(x_ok, CREDIT + c + 1)
                        hold(dve)
                        norm.vector_stats(dve, chunk(X, c), n2(c))
                    if q == 3:
                        dve.wait_ge(yb_pre, CREDIT + c)
                        hold(dve)
                        norm.vector_apply(dve, chunk(X, c), x2, n2(c))
                    if q == 7:
                        dve.wait_ge(qv_ok, CREDIT + c + 1)
                        at = 0
                        for t in range(NB - 1):
                            n = NB - 1 - t
                            last = nc.vector.tensor_tensor(dif[:, at:at + n, :], qv[:, 0, t + 1:NB, :],
                                                           qv[:, 0, t:t + 1, :].broadcast_to([P, n, D]), ALU.subtract)
                            at += n
                        last.then_inc(dif_ok, 1)
                    if q == 8:
                        dve.wait_ge(sqd_ok, c + 1)
                        nc.vector.tensor_reduce(dist[:], sqd[:].rearrange("p a (h d) -> p (a h) d", d=DH1), AX.X,
                                                ALU.add).then_inc(dist_ok, 1)
                    if q == 10:
                        dve.wait_ge(wp_ok, c + 1)
                        for k, (t, s) in enumerate(PAIRS):
                            nc.vector.tensor_copy(wf[:, t, s, :], wp[:, k, :])
                            last = nc.vector.tensor_copy(wf[:, s, t, :], wp[:, k, :])
                        last.then_inc(wf_ok, 1)
                        dve.wait_ge(wf_ok, CREDIT + c + 1)
                        nc.vector.tensor_reduce(den[:, 0, :], wf[:].rearrange("p t s h -> p t h s"), AX.X,
                                                ALU.add).then_inc(den_ok, 1)
                        dve.wait_ge(den_ok, c + 1)
                        nc.vector.reciprocal(den[:, 1, :], den[:, 0, :]).then_inc(rden_ok, 1)
                    if q == 11:
                        weigh(c, 0)
                        weigh(c, 1)
                    if q == 12:
                        weigh(c, 2)
                        weigh(c, 3)
                        dve.wait_ge(o1_ok, 4 * c + 4)
                        dve.wait_ge(rden_ok, c + 1)
                        nc.vector.tensor_tensor(o1n[:].rearrange("p b (h d) -> p (b h) d", d=DH1),
                                                o1[:].rearrange("p b (h d) -> p (b h) d", d=DH1),
                                                den[:, 1, :].unsqueeze(2).broadcast_to([P, NB * H1, DH1]),
                                                ALU.mult).then_inc(on_ok, 1)
                    if q == 13:
                        dve.wait_ge(norm.done, n2(c) + 1)
                        nc.vector.tensor_tensor(y1[:], x2[:], ob1[:].unsqueeze(1).broadcast_to([P, NB, D]),
                                                ALU.add).then_inc(yb_pre, 1)
                    if q == 15:
                        dve.wait_ge(yb_pre, CREDIT + c + 1)
                        dve.wait_ge(y_mm, CREDIT + c + 1)
                        nc.vector.tensor_tensor(y2[:], Y1, y1[:], ALU.add).then_inc(yb_ok, 1)
                        dve.wait_ge(yb_ok, CREDIT + c + 1)
                        hold(dve)
                        norm.vector_stats(dve, y2, n3(c))
                    if q == 16:
                        dve.wait_ge(xk2, CREDIT + c)
                        hold(dve)
                        norm.vector_apply(dve, y2, xn, n3(c))
                        dve.wait_ge(norm.done, n3(c) + 1)
                        hold(dve)
                        nc.vector.tensor_copy(chunk(X, c), xn[:]).then_inc(xk2, 1)
                    if q == 19:
                        dve.wait_ge(r_mm, CREDIT + c + 1)
                        dve.wait_ge(ex_ok, CREDIT + c)
                        nc.vector.tensor_tensor(sc1[:, 0], R, gb1[:].unsqueeze(1).broadcast_to([P, NB, E1]),
                                                ALU.add).then_inc(lg_ok, 1)
                    if q == 21:
                        dve.wait_ge(ex_ok, CREDIT + c + 1)
                        nc.vector.tensor_scalar(sc1[:, 2], sc1[:, 1], 1.0, None, ALU.add).then_inc(ex1_ok, 1)
                        dve.wait_ge(ex1_ok, CREDIT + c + 1)
                        nc.vector.reciprocal(sc1[:, 3], sc1[:, 2]).then_inc(sig_ok, 1)
                        dve.wait_ge(sig_ok, c + 1)
                        first_of(dve, sc1[:, 3], top[:, 0, :], eq[:], key[:], top[:, 1, :], hot[:, 0], pick1, c, rk, E1)
                    if q == 22:
                        dve.wait_ge(pick1[4], c + 1)
                        nc.vector.scalar_tensor_tensor(rest[:], hot[:, 0], -4.0, sc1[:, 3], ALU.mult, ALU.add).then_inc(rest_ok, 1)
                        dve.wait_ge(rest_ok, c + 1)
                        first_of(dve, rest[:], top[:, 2, :], eq[:], key[:], top[:, 3, :], hot[:, 1], pick2, c, rk, E1)
                        dve.wait_ge(pick2[4], c + 1)
                        nc.vector.tensor_tensor(top[:, 4, :], top[:, 0, :], top[:, 2, :], ALU.add)
                        nc.vector.tensor_tensor(hot[:, 0], hot[:, 0], hot[:, 1], ALU.add).then_inc(num_ok, 1)
                        dve.wait_ge(num_ok, c + 1)
                        nc.vector.reciprocal(top[:, 5, :], top[:, 4, :])
                        nc.vector.tensor_tensor(rest[:], hot[:, 0], sc1[:, 3], ALU.mult).then_inc(rd_ok, 1)
                        dve.wait_ge(rd_ok, c + 1)
                        nc.vector.tensor_tensor(wt[:, 0, :, 0:E1], rest[:],
                                                top[:, 5, :].unsqueeze(2).broadcast_to([P, NB, E1]), ALU.mult).then_inc(w_ok, 1)
                        dve.wait_ge(w_ok, c + 1)
                        dve.wait_ge(c_mm, CREDIT + c)
                        for k in range(3):
                            nc.vector.tensor_copy(w3[:, :, k, :], wt[:, k]).then_inc(w3_ok, 1)
                            if k < 2:
                                dve.wait_ge(w3_ok, 3 * c + k + 1)
                                nc.vector.tensor_tensor(wt[:, k + 1], wt[:, k], w3[:, :, k, :], ALU.subtract).then_inc(part_ok, 1)
                                dve.wait_ge(part_ok, 2 * c + k + 1)

                def second(c, j):
                    n = ROWS[j]
                    dve.wait_ge(silu5, NJ1 * c + j + 1)
                    nc.vector.tensor_tensor(raw[0:n, j % 2, :], sg[0:n, j % 2, :], U[j % 2][0:n, :],
                                            ALU.mult).then_inc(prod_ok, 1)
                    dve.wait_ge(prod_ok, CREDIT + NJ1 * c + j + 1)
                    dve.wait_ge(dn5, CREDIT + blocks(c, j))
                    dve.wait_ge(m_mm, E0 * TT + 1 + NJ1 * c + j + 1)
                    if j == 0:
                        dve.wait_ge(dn, CREDIT + NQ * TT)
                        hold(dve)
                    nc.vector.tensor_tensor(hid[0:n, j % 2, :], raw[0:n, j % 2, :], M[0:n, :],
                                            ALU.mult).then_inc(hid5_ok, 1)
                    if j == 1 and not (isinstance(c, int) and c == 0):
                        second_norm(c - 1)

                def second_norm(c):
                    norm1.vector_apply(dve, xs, chunk(X, c), n4(c))

                def second_end(c):
                    dve.wait_ge(y5_t, CREDIT + c + 1)
                    dve.wait_ge(xk2, CREDIT + c + 1)
                    hold(dve)
                    nc.vector.scalar_tensor_tensor(xs[:], chunk(X, c), 2.0, T5, ALU.mult, ALU.add).then_inc(x5_ok, 1)
                    dve.wait_ge(x5_ok, CREDIT + c + 1)
                    norm1.vector_stats(dve, xs, n4(c))

                nc.vector.memset(wf[:], 1.0)
                nc.vector.memset(wt[:], 0.0).then_inc(init, 1)
                dve.wait_ge(init, 1)
                nc.vector.memset(wt[:, 0, :, E1:NE1], 1.0).then_inc(init, 1)
                dve.wait_ge(init, 2)
                for q in range(NQ):
                    before(0, q)
                masked(0, 0)
                for q in range(NQ):
                    experts(0, q)
                    before(1, q)
                with dve.Fori(0, TT - 2) as c:
                    for q in range(NQ):
                        experts(c + 1, q)
                        after(c, q)
                        before(c + 2, q)
                for q in range(NQ):
                    experts(TT - 1, q)
                    after(TT - 2, q)
                for c in range(BESIDE):
                    for j in range(NJ1):
                        second(c, j)
                        after(TT - 1, c * NJ1 + j)
                    second_end(c)
                with dve.Fori(BESIDE, TT) as c:
                    for j in range(NJ1):
                        second(c, j)
                    second_end(c)
                second_norm(TT - 1)

            @block.gpsimd
            def _(pool):
                norm1.pool(pool, n1(0))
                norm1.pool(pool, n1(1))
                with pool.Fori(0, TT - 2) as c:
                    norm.pool(pool, n2(c))
                    norm1.pool(pool, n1(c + 2))
                    norm.pool(pool, n3(c))
                norm.pool(pool, n2(TT - 2))
                norm.pool(pool, n3(TT - 2))
                norm.pool(pool, n2(TT - 1))
                norm1.pool(pool, n4(0))
                norm.pool(pool, n3(TT - 1))
                with pool.Fori(1, TT) as c:
                    norm1.pool(pool, n4(c))


def credit(engine, *signals):
    for signal in signals:
        engine.sem_inc(signal, CREDIT)


def hold(engine):
    engine.nop(nofuse=True)


def layout(x):
    f = lambda v: np.ascontiguousarray(v)
    nkv = x["L0_attn_null_kv"].reshape(H, NNULL, 2, DH)
    wq = x["L0_attn_w_q"].reshape(D, NG, KW)
    wkv = x["L0_attn_w_kv"].reshape(D, 2, NG, KW)
    down = x["L0_ffn_down_w"].transpose(0, 2, 1)
    dw0 = np.zeros((P, E0 * NK0, D), np.float32)
    for e in range(E0):
        for k, (at, rows) in enumerate(KB0):
            dw0[:rows, e * NK0 + k] = down[e, at:at + rows]
    both = lambda ew, sw: np.concatenate([ew, sw[None]], axis=0)
    gate = both(x["L1_ffn_experts_wg"], x["L1_ffn_shared_wg"]).transpose(1, 0, 2).reshape(D, NE1 * I1)
    up = both(x["L1_ffn_experts_wu"], x["L1_ffn_shared_wu"]).transpose(1, 0, 2).reshape(D, NE1 * I1)
    d1 = both(x["L1_ffn_experts_wd"], x["L1_ffn_shared_wd"]).reshape(NE1 * I1, D)
    dw1 = np.zeros((P, NJ1, D), np.float32)
    for j in range(NJ1):
        part = d1[j * P:(j + 1) * P]
        dw1[:part.shape[0], j] = part
    q1 = x["L1_attn_q_weight"].reshape(D, H1 * DH1)
    return {
        "x": f(x["L0_attn_x"].reshape(NB, TT, P, D).transpose(2, 1, 0, 3)),
        "gamma": f(x["L0_attn_gamma"].reshape(P, 1)),
        "q_scale": f(x["L0_attn_q_scale"]), "k_scale": f(x["L0_attn_k_scale"]),
        "null_k": f(nkv[:, :, 0].reshape(H * NNULL, DH)),
        "null_v": f(nkv[:, :, 1].reshape(NG, HG, NNULL, DH).transpose(0, 2, 1, 3)),
        "w_q_t": f(x["L0_attn_w_q"].reshape(D, H, DH).transpose(2, 1, 0).reshape(DH, H * P)),
        "w_qkv": f(np.concatenate([wq, wkv[:, 0], wkv[:, 1]], axis=2)),
        "w_out": f(x["L0_attn_w_out"].reshape(H * DH // P, P, D).transpose(1, 0, 2)),
        "rw0": f(x["L0_ffn_router_w"].T),
        "gw0": f(x["L0_ffn_gate_w"].transpose(2, 0, 1).reshape(D, E0 * I0)),
        "uw0": f(x["L0_ffn_up_w"].transpose(2, 0, 1).reshape(D, E0 * I0)),
        "dw0": dw0,
        "w1_q": f(q1), "w1_q_t": f(q1.T), "w1_v": f(x["L1_attn_v_weight"].reshape(D, H1 * DH1)),
        "w1_o": f(x["L1_attn_out_w"].T), "ob1": f(x["L1_attn_out_b"]),
        "rw1": f(x["L1_ffn_gate_w"]), "gb1": f(x["L1_ffn_gate_b"]),
        "gw1": f(gate), "uw1": f(up), "dw1": dw1,
    }


def kernel(**inputs):
    import concourse.bacc as _bacc
    from concourse import mybir as _mybir
    from concourse.bass_utils import run_bass_kernel_spmd as _run

    data = layout({k: np.asarray(v) for k, v in inputs.items()})
    data.update(constants())
    nc = _bacc.Bacc("TRN2", target_bir_lowering=False, num_devices=1)
    arrays, aps = {}, {}
    for name, arr in data.items():
        arrays[f"in_{name}"] = arr
        aps[name] = nc.dram_tensor(f"in_{name}", arr.shape, _mybir.dt.from_np(arr.dtype), kind="ExternalInput").ap()
    out = nc.dram_tensor("out", (P, TT, NB, D), F32, kind="ExternalOutput").ap()
    build(nc, aps, out)
    r = _run(nc, [arrays], core_ids=[0])
    return r.results[0]["out"].transpose(2, 1, 0, 3).reshape(NB, SEQ, D)
```
